# Optimizing a Trainium2 kernel written in Bass

```python
import numpy as np
import jax
import jax.numpy as jnp

def _softmax(x, axis=-1):
    return jax.nn.softmax(x, axis=axis)

def _gelu(x):
    return jax.nn.gelu(x, approximate=True)

def _silu(x):
    return jax.nn.silu(x)

def _sigmoid(x):
    return jax.nn.sigmoid(x)

def _layernorm(x, axis=-1, eps=1e-05):
    m = jnp.mean(x, axis=axis, keepdims=True)
    v = jnp.var(x, axis=axis, keepdims=True)
    return (x - m) / jnp.sqrt(v + eps)

def _scatter_add(tgt, idx, src, axis=0):
    return tgt.at[idx].add(src)

def _segment_sum(src, seg, n):
    return jax.ops.segment_sum(src, seg, n)
kernel_name = 'mk_vit_tower_d2_tok_img1024_r4_66972a'

def setup_inputs(seed: int=0):
    np.random.seed(seed)
    _w = jnp.asarray

    def _rec_inputs():
        import jax
        import jax.numpy as jnp
        _rk = jax.random.key(seed)
        x = -0.00016672 + 0.999947 * jax.random.normal(jax.random.fold_in(_rk, 1), (64, 3, 96, 96), jnp.float32)
        return x
    x = _rec_inputs()

    def _L0_tok_setup():
        import jax, jax.numpy as jnp
        import numpy as np
        DIM = 256
        IMG = 96
        P = 16
        C = 3
        TEMP = 10000.0
        EPS = 1e-05
        PATCH_DIM = C * P * P
        HP = IMG // P

        def layernorm(x, gamma, beta):
            mu = jnp.mean(x, axis=-1, keepdims=True)
            var = jnp.var(x, axis=-1, keepdims=True)
            return (x - mu) * jax.lax.rsqrt(var + EPS) * gamma + beta

        def posemb_sincos_2d(h, w, dim, dtype):
            y, x = jnp.meshgrid(jnp.arange(h), jnp.arange(w), indexing='ij')
            omega = jnp.arange(dim // 4, dtype=jnp.float32) / (dim // 4 - 1)
            omega = 1.0 / TEMP ** omega
            y = y.reshape(-1)[:, None] * omega[None, :]
            x = x.reshape(-1)[:, None] * omega[None, :]
            pe = jnp.concatenate((jnp.sin(x), jnp.cos(x), jnp.sin(y), jnp.cos(y)), axis=1)
            return pe.astype(dtype)
        key = jax.random.key(seed)
        ks = jax.random.split(key, 8)
        B = 64
        img = jax.random.normal(ks[0], (B, C, IMG, IMG), dtype=jnp.float32)
        cls_token = jax.random.normal(ks[1], (1, 1, DIM), dtype=jnp.float32)
        cls_pos_embedding = jax.random.normal(ks[2], (1, 1, DIM), dtype=jnp.float32)
        ln1_g = jnp.ones((PATCH_DIM,), jnp.float32)
        ln1_b = jnp.zeros((PATCH_DIM,), jnp.float32)
        W = jax.random.normal(ks[3], (PATCH_DIM, DIM), dtype=jnp.float32) / np.sqrt(PATCH_DIM)
        bias = jnp.zeros((DIM,), jnp.float32)
        ln2_g = jnp.ones((DIM,), jnp.float32)
        ln2_b = jnp.zeros((DIM,), jnp.float32)
        return {'img': img, 'cls_token': cls_token, 'cls_pos_embedding': cls_pos_embedding, 'ln1_g': ln1_g, 'ln1_b': ln1_b, 'W': W, 'bias': bias, 'ln2_g': ln2_g, 'ln2_b': ln2_b}
    _L0_tok_all = _L0_tok_setup()
    _L0_tok_in = {k: v for k, v in _L0_tok_all.items() if k in ('cls_token', 'cls_pos_embedding', 'ln1_g', 'ln1_b', 'W', 'bias', 'ln2_g', 'ln2_b')}
    del _L0_tok_all

    def _L0_attn_setup():
        import jax, jax.numpy as jnp
        import numpy as np
        N_HEAD = 16
        NEG_BIG = -10000000000.0

        def _rope_cos_sin(T, head_dim, dtype):
            half = head_dim // 2
            i = jnp.arange(half, dtype=jnp.float32)
            theta = 1.0 / 10000.0 ** (2.0 * i / head_dim)
            t = jnp.arange(T, dtype=jnp.float32)[:, None]
            ang = t * theta[None, :]
            return (jnp.cos(ang).astype(dtype), jnp.sin(ang).astype(dtype))

        def _apply_rope(x, cos, sin):
            B, H, T, D = x.shape
            xr = x.reshape(B, H, T, D // 2, 2)
            x0, x1 = (xr[..., 0], xr[..., 1])
            c = cos[None, None, :, :]
            s = sin[None, None, :, :]
            out = jnp.stack((x0 * c - x1 * s, x0 * s + x1 * c), axis=-1)
            return out.reshape(B, H, T, D)
        key = jax.random.key(seed)
        ks = jax.random.split(key, 9)
        B, T, C = (4, 512, 256)
        sc = 1.0 / np.sqrt(C)
        return {'x': jax.random.normal(ks[0], (B, T, C), jnp.float32), 'wq': jax.random.normal(ks[1], (C, C), jnp.float32) * sc, 'bq': jax.random.normal(ks[2], (C,), jnp.float32) * 0.02, 'wk': jax.random.normal(ks[3], (C, C), jnp.float32) * sc, 'bk': jax.random.normal(ks[4], (C,), jnp.float32) * 0.02, 'wv': jax.random.normal(ks[5], (C, C), jnp.float32) * sc, 'bv': jax.random.normal(ks[6], (C,), jnp.float32) * 0.02, 'wp': jax.random.normal(ks[7], (C, C), jnp.float32) * sc, 'bp': jax.random.normal(ks[8], (C,), jnp.float32) * 0.02}
    _L0_attn_all = _L0_attn_setup()
    _L0_attn_in = {k: v for k, v in _L0_attn_all.items() if k in ('wq', 'bq', 'wk', 'bk', 'wv', 'bv', 'wp', 'bp')}
    del _L0_attn_all

    def _L0_ffn_setup():
        import jax, jax.numpy as jnp
        import numpy as np
        B, S, D_MODEL, D_HIDDEN = (4, 512, 256, 1024)

        def act_quant(x):
            scale = 127.0 / jnp.clip(jnp.max(jnp.abs(x), axis=-1, keepdims=True), 1e-05)
            return jnp.clip(jnp.round(x * scale), -128, 127) / scale

        def weight_quant(w):
            scale = 1.0 / jnp.clip(jnp.mean(jnp.abs(w)), 1e-05)
            return jnp.clip(jnp.round(w * scale), -1, 1) / scale

        def bit_linear(x, w):
            xq = x + jax.lax.stop_gradient(act_quant(x) - x)
            wq = w + jax.lax.stop_gradient(weight_quant(w) - w)
            return jnp.einsum('bsd,hd->bsh', xq, wq)

        def depthwise_conv1d(x_bcl, w, b):
            y = jax.lax.conv_general_dilated(x_bcl, w, window_strides=(1,), padding=[(1, 1)], dimension_numbers=('NCH', 'OIH', 'NCH'), feature_group_count=x_bcl.shape[1])
            return y + b[None, :, None]
        key = jax.random.key(seed)
        ks = jax.random.split(key, 5)
        lim1 = 1.0 / np.sqrt(D_MODEL)
        lim2 = 1.0 / np.sqrt(D_HIDDEN)
        limc = 1.0 / np.sqrt(3.0)
        return {'x': jax.random.normal(ks[0], (B, S, D_MODEL), dtype=jnp.float32), 'w1': jax.random.uniform(ks[1], (D_HIDDEN, D_MODEL), jnp.float32, -lim1, lim1), 'conv_w': jax.random.uniform(ks[2], (D_HIDDEN, 1, 3), jnp.float32, -limc, limc), 'conv_b': jax.random.uniform(ks[3], (D_HIDDEN,), jnp.float32, -limc, limc), 'w2': jax.random.uniform(ks[4], (D_MODEL, D_HIDDEN), jnp.float32, -lim2, lim2)}
    _L0_ffn_all = _L0_ffn_setup()
    _L0_ffn_in = {k: v for k, v in _L0_ffn_all.items() if k in ('w1', 'conv_w', 'conv_b', 'w2')}
    del _L0_ffn_all

    def _L1_attn_setup():
        import jax, jax.numpy as jnp
        import numpy as np
        D = 256
        H = 16
        DK = D // H
        C = 64
        MRP = 2 * C
        B, S = (2, 512)
        key = jax.random.key(seed)
        ks = jax.random.split(key, 7)
        s = 0.02
        x = jax.random.normal(ks[0], (B, S, D), jnp.float32)
        Wq = jax.random.normal(ks[1], (D, D), jnp.float32) * s
        Wk = jax.random.normal(ks[2], (D, D), jnp.float32) * s
        Wv = jax.random.normal(ks[3], (D, D), jnp.float32) * s
        Wo = jax.random.normal(ks[4], (D, D), jnp.float32) * s
        bq = jnp.zeros((D,), jnp.float32)
        bk = jnp.zeros((D,), jnp.float32)
        bv = jnp.zeros((D,), jnp.float32)
        bo = jnp.zeros((D,), jnp.float32)
        rel_bias = jax.random.normal(ks[5], (2 * MRP + 1, H), jnp.float32) * s
        return dict(x=x, Wq=Wq, bq=bq, Wk=Wk, bk=bk, Wv=Wv, bv=bv, Wo=Wo, bo=bo, rel_bias=rel_bias)
    _L1_attn_all = _L1_attn_setup()
    _L1_attn_in = {k: v for k, v in _L1_attn_all.items() if k in ('Wq', 'bq', 'Wk', 'bk', 'Wv', 'bv', 'Wo', 'bo', 'rel_bias')}
    del _L1_attn_all

    def _L1_ffn_setup():
        import jax, jax.numpy as jnp
        import numpy as np
        B, S, D, E, H = (2, 256, 256, 16, 512)
        TOP_K = 2
        TEMP = 1.0
        key = jax.random.key(seed)
        ks = jax.random.split(key, 4)
        sc_d = 1.0 / np.sqrt(D)
        sc_h = 1.0 / np.sqrt(H)
        return {'x': jax.random.normal(ks[0], (B, S, D), dtype=jnp.float32), 'Wr': jax.random.normal(ks[1], (D, E), dtype=jnp.float32) * sc_d, 'br': jnp.zeros((E,), dtype=jnp.float32), 'W1': jax.random.normal(ks[2], (E, D, H), dtype=jnp.float32) * sc_d, 'b1': jnp.zeros((E, H), dtype=jnp.float32), 'W2': jax.random.normal(ks[3], (E, H, D), dtype=jnp.float32) * sc_h, 'b2': jnp.zeros((E, D), dtype=jnp.float32)}
    _L1_ffn_all = _L1_ffn_setup()
    _L1_ffn_in = {k: v for k, v in _L1_ffn_all.items() if k in ('Wr', 'br', 'W1', 'b1', 'W2', 'b2')}
    del _L1_ffn_all
    return {'x': x, 'L0_tok_cls_token': _L0_tok_in['cls_token'], 'L0_tok_cls_pos_embedding': _L0_tok_in['cls_pos_embedding'], 'L0_tok_ln1_g': _L0_tok_in['ln1_g'], 'L0_tok_ln1_b': _L0_tok_in['ln1_b'], 'L0_tok_W': _L0_tok_in['W'], 'L0_tok_bias': _L0_tok_in['bias'], 'L0_tok_ln2_g': _L0_tok_in['ln2_g'], 'L0_tok_ln2_b': _L0_tok_in['ln2_b'], 'L0_attn_wq': _L0_attn_in['wq'], 'L0_attn_bq': _L0_attn_in['bq'], 'L0_attn_wk': _L0_attn_in['wk'], 'L0_attn_bk': _L0_attn_in['bk'], 'L0_attn_wv': _L0_attn_in['wv'], 'L0_attn_bv': _L0_attn_in['bv'], 'L0_attn_wp': _L0_attn_in['wp'], 'L0_attn_bp': _L0_attn_in['bp'], 'L0_ffn_w1': _L0_ffn_in['w1'], 'L0_ffn_conv_w': _L0_ffn_in['conv_w'], 'L0_ffn_conv_b': _L0_ffn_in['conv_b'], 'L0_ffn_w2': _L0_ffn_in['w2'], 'L1_attn_Wq': _L1_attn_in['Wq'], 'L1_attn_bq': _L1_attn_in['bq'], 'L1_attn_Wk': _L1_attn_in['Wk'], 'L1_attn_bk': _L1_attn_in['bk'], 'L1_attn_Wv': _L1_attn_in['Wv'], 'L1_attn_bv': _L1_attn_in['bv'], 'L1_attn_Wo': _L1_attn_in['Wo'], 'L1_attn_bo': _L1_attn_in['bo'], 'L1_attn_rel_bias': _L1_attn_in['rel_bias'], 'L1_ffn_Wr': _L1_ffn_in['Wr'], 'L1_ffn_br': _L1_ffn_in['br'], 'L1_ffn_W1': _L1_ffn_in['W1'], 'L1_ffn_b1': _L1_ffn_in['b1'], 'L1_ffn_W2': _L1_ffn_in['W2'], 'L1_ffn_b2': _L1_ffn_in['b2']}

def reference(x, L0_tok_cls_token, L0_tok_cls_pos_embedding, L0_tok_ln1_g, L0_tok_ln1_b, L0_tok_W, L0_tok_bias, L0_tok_ln2_g, L0_tok_ln2_b, L0_attn_wq, L0_attn_bq, L0_attn_wk, L0_attn_bk, L0_attn_wv, L0_attn_bv, L0_attn_wp, L0_attn_bp, L0_ffn_w1, L0_ffn_conv_w, L0_ffn_conv_b, L0_ffn_w2, L1_attn_Wq, L1_attn_bq, L1_attn_Wk, L1_attn_bk, L1_attn_Wv, L1_attn_bv, L1_attn_Wo, L1_attn_bo, L1_attn_rel_bias, L1_ffn_Wr, L1_ffn_br, L1_ffn_W1, L1_ffn_b1, L1_ffn_W2, L1_ffn_b2):
    import jax
    import jax.numpy as jnp

    def _L0_tok_ref(img, cls_token, cls_pos_embedding, ln1_g, ln1_b, W, bias, ln2_g, ln2_b):
        import jax, jax.numpy as jnp
        import numpy as np
        DIM = 256
        IMG = 96
        P = 16
        C = 3
        TEMP = 10000.0
        EPS = 1e-05
        PATCH_DIM = C * P * P
        HP = IMG // P

        def layernorm(x, gamma, beta):
            mu = jnp.mean(x, axis=-1, keepdims=True)
            var = jnp.var(x, axis=-1, keepdims=True)
            return (x - mu) * jax.lax.rsqrt(var + EPS) * gamma + beta

        def posemb_sincos_2d(h, w, dim, dtype):
            y, x = jnp.meshgrid(jnp.arange(h), jnp.arange(w), indexing='ij')
            omega = jnp.arange(dim // 4, dtype=jnp.float32) / (dim // 4 - 1)
            omega = 1.0 / TEMP ** omega
            y = y.reshape(-1)[:, None] * omega[None, :]
            x = x.reshape(-1)[:, None] * omega[None, :]
            pe = jnp.concatenate((jnp.sin(x), jnp.cos(x), jnp.sin(y), jnp.cos(y)), axis=1)
            return pe.astype(dtype)
        b = img.shape[0]
        x = img.reshape(b, C, HP, P, HP, P)
        x = jnp.transpose(x, (0, 2, 4, 3, 5, 1))
        x = x.reshape(b, HP, HP, PATCH_DIM)
        x = layernorm(x, ln1_g, ln1_b)
        x = jnp.einsum('bhwp,pd->bhwd', x, W) + bias
        x = layernorm(x, ln2_g, ln2_b)
        pe = posemb_sincos_2d(HP, HP, DIM, x.dtype)
        x = x.reshape(b, HP * HP, DIM) + pe[None]
        cls_tokens = jnp.broadcast_to(cls_token + cls_pos_embedding, (b, 1, DIM))
        return jnp.concatenate((cls_tokens, x), axis=1)

    def _L0_attn_ref(x, wq, bq, wk, bk, wv, bv, wp, bp):
        import jax, jax.numpy as jnp
        import numpy as np
        N_HEAD = 16
        NEG_BIG = -10000000000.0

        def _rope_cos_sin(T, head_dim, dtype):
            half = head_dim // 2
            i = jnp.arange(half, dtype=jnp.float32)
            theta = 1.0 / 10000.0 ** (2.0 * i / head_dim)
            t = jnp.arange(T, dtype=jnp.float32)[:, None]
            ang = t * theta[None, :]
            return (jnp.cos(ang).astype(dtype), jnp.sin(ang).astype(dtype))

        def _apply_rope(x, cos, sin):
            B, H, T, D = x.shape
            xr = x.reshape(B, H, T, D // 2, 2)
            x0, x1 = (xr[..., 0], xr[..., 1])
            c = cos[None, None, :, :]
            s = sin[None, None, :, :]
            out = jnp.stack((x0 * c - x1 * s, x0 * s + x1 * c), axis=-1)
            return out.reshape(B, H, T, D)
        B, T, C = x.shape
        H = N_HEAD
        D = C // H

        def proj(w, b):
            return (jnp.einsum('btc,oc->bto', x, w) + b).reshape(B, T, H, D).transpose(0, 2, 1, 3)
        q = proj(wq, bq)
        k = proj(wk, bk)
        v = proj(wv, bv)
        cos, sin = _rope_cos_sin(T, D, x.dtype)
        q = _apply_rope(q, cos, sin)
        k = _apply_rope(k, cos, sin)
        att = jnp.einsum('bhtd,bhsd->bhts', q, k) * (1.0 / np.sqrt(D))
        causal = jnp.tril(jnp.ones((T, T), bool))
        att = jnp.where(causal[None, None], att, jnp.asarray(NEG_BIG, att.dtype))
        att = jax.nn.softmax(att, axis=-1)
        y = jnp.einsum('bhts,bhsd->bhtd', att, v)
        y = y.transpose(0, 2, 1, 3).reshape(B, T, C)
        return jnp.einsum('btc,oc->bto', y, wp) + bp

    def _L0_ffn_ref(x, w1, conv_w, conv_b, w2):
        import jax, jax.numpy as jnp
        import numpy as np
        B, S, D_MODEL, D_HIDDEN = (4, 512, 256, 1024)

        def act_quant(x):
            scale = 127.0 / jnp.clip(jnp.max(jnp.abs(x), axis=-1, keepdims=True), 1e-05)
            return jnp.clip(jnp.round(x * scale), -128, 127) / scale

        def weight_quant(w):
            scale = 1.0 / jnp.clip(jnp.mean(jnp.abs(w)), 1e-05)
            return jnp.clip(jnp.round(w * scale), -1, 1) / scale

        def bit_linear(x, w):
            xq = x + jax.lax.stop_gradient(act_quant(x) - x)
            wq = w + jax.lax.stop_gradient(weight_quant(w) - w)
            return jnp.einsum('bsd,hd->bsh', xq, wq)

        def depthwise_conv1d(x_bcl, w, b):
            y = jax.lax.conv_general_dilated(x_bcl, w, window_strides=(1,), padding=[(1, 1)], dimension_numbers=('NCH', 'OIH', 'NCH'), feature_group_count=x_bcl.shape[1])
            return y + b[None, :, None]
        h = bit_linear(x, w1)
        h = depthwise_conv1d(h.transpose(0, 2, 1), conv_w, conv_b)
        h = h.transpose(0, 2, 1)
        h = jax.nn.silu(h)
        return bit_linear(h, w2)

    def _L1_attn_ref(x, Wq, bq, Wk, bk, Wv, bv, Wo, bo, rel_bias):
        import jax, jax.numpy as jnp
        import numpy as np
        D = 256
        H = 16
        DK = D // H
        C = 64
        MRP = 2 * C
        B, S = (2, 512)
        b, s, _ = x.shape

        def heads(w, bias):
            return (x @ w + bias).reshape(b, s, H, DK).transpose(0, 2, 1, 3)
        Q = heads(Wq, bq)
        K = heads(Wk, bk)
        V = heads(Wv, bv)
        scale = jnp.sqrt(jnp.asarray(DK, x.dtype))
        scores = jnp.einsum('bhqd,bhkd->bhqk', Q, K) / scale
        pos = jnp.arange(s)
        rel = jnp.clip(pos[:, None] - pos[None, :], -MRP, MRP) + MRP
        bias2 = rel_bias[rel].transpose(2, 0, 1)
        scores = scores + bias2[None]
        qc = pos // C
        allowed = qc[None, :] <= qc[:, None]
        scores = jnp.where(allowed[None, None], scores, -jnp.inf)
        attn = jax.nn.softmax(scores, axis=-1)
        out = jnp.einsum('bhqk,bhkd->bhqd', attn, V)
        out = out.transpose(0, 2, 1, 3).reshape(b, s, D)
        return out @ Wo + bo

    def _L1_ffn_ref(x, Wr, br, W1, b1, W2, b2):
        import jax, jax.numpy as jnp
        import numpy as np
        B, S, D, E, H = (2, 256, 256, 16, 512)
        TOP_K = 2
        TEMP = 1.0
        token_shape = x.shape[:-1]
        d = x.shape[-1]
        xt = x.reshape(-1, d)
        T = xt.shape[0]
        logits = (xt @ Wr + br) / TEMP
        probs = jax.nn.softmax(logits, axis=-1)
        w, idx = jax.lax.top_k(probs, TOP_K)
        w = w / jnp.clip(jnp.sum(w, axis=-1, keepdims=True), 1e-09)
        comb = jnp.zeros((T, E), dtype=xt.dtype)
        comb = comb.at[jnp.arange(T)[:, None], idx].add(w)
        h = jax.nn.gelu(jnp.einsum('td,edh->teh', xt, W1) + b1, approximate=False)
        o = jnp.einsum('teh,eho->teo', h, W2) + b2
        y = jnp.einsum('teo,te->to', o, comb)
        y = xt + y
        return y.reshape(*token_shape, d)
    h = _L0_tok_ref(x, L0_tok_cls_token, L0_tok_cls_pos_embedding, L0_tok_ln1_g, L0_tok_ln1_b, L0_tok_W, L0_tok_bias, L0_tok_ln2_g, L0_tok_ln2_b)
    h = h + _L0_attn_ref(_layernorm(h, axis=-1), L0_attn_wq, L0_attn_bq, L0_attn_wk, L0_attn_bk, L0_attn_wv, L0_attn_bv, L0_attn_wp, L0_attn_bp)
    h = h + _L0_ffn_ref(_layernorm(h, axis=-1), L0_ffn_w1, L0_ffn_conv_w, L0_ffn_conv_b, L0_ffn_w2)
    h = h + _L1_attn_ref(_layernorm(h, axis=-1), L1_attn_Wq, L1_attn_bq, L1_attn_Wk, L1_attn_bk, L1_attn_Wv, L1_attn_bv, L1_attn_Wo, L1_attn_bo, L1_attn_rel_bias)
    h = h + _L1_ffn_ref(_layernorm(h, axis=-1), L1_ffn_Wr, L1_ffn_br, L1_ffn_W1, L1_ffn_b1, L1_ffn_W2, L1_ffn_b2)
    return h

_drawn_inputs = setup_inputs


def setup_inputs(seed=0):
    import zlib

    import numpy as np

    out = dict(_drawn_inputs(seed))
    spreads = {'L0_tok_ln1_g': (1.0, 0.2),
     'L0_tok_ln1_b': (0.0, 0.1),
     'L0_tok_bias': (0.0, 0.1),
     'L0_tok_ln2_g': (1.0, 0.2),
     'L0_tok_ln2_b': (0.0, 0.1),
     'L1_attn_bq': (0.0, 0.8),
     'L1_attn_bk': (0.0, 2.0),
     'L1_attn_bv': (0.0, 0.1),
     'L1_attn_bo': (0.0, 0.1),
     'L1_ffn_br': (0.0, 0.1),
     'L1_ffn_b1': (0.0, 0.378),
     'L1_ffn_b2': (0.0, 0.1)}
    factors = {'L0_attn_bq': 5.253,
     'L0_attn_bk': 8.0,
     'L1_attn_Wq': 8.0,
     'L1_attn_Wk': 7.313,
     'L1_attn_rel_bias': 46.359}
    for name, (base, spread) in spreads.items():
        noise = np.random.default_rng([zlib.crc32(name.encode()), seed]).standard_normal(out[name].shape)
        drawn = base * np.exp(spread * noise) if base else spread * noise
        out[name] = jnp.asarray(drawn.astype(out[name].dtype))
    for name, factor in factors.items():
        out[name] = (out[name] * factor).astype(out[name].dtype)
    return out
```

```python
from contextlib import ExitStack

import numpy as np
import concourse.bass as bass
from concourse import mybir

F32 = mybir.dt.float32
BF16 = mybir.dt.bfloat16
U32 = mybir.dt.uint32
I32 = mybir.dt.int32
ALU = mybir.AluOpType
ACT = mybir.ActivationFunctionType
AX = mybir.AxisListType

P = 128
B, C, IMG, PATCH = 64, 3, 96, 16
HP = IMG // PATCH
NP = HP * HP
T = NP + 1
D = 256
FP = C * PATCH * PATCH
KF = FP // P
H, DH = 16, 16
QH = 64 // DH
FH = 1024
MH = FH // P
E, EH = 16, 512
EPS = 1e-5
MAGIC = 1.5 * 2.0 ** 23

NI = 8
NB = B // NI
CTX = 2
ITERS = NB // CTX
NT = NI * T
J = 3
R = (NT + J - 1) // J
NTP = J * R
NPB = NI * NP
RP = NPB // J
NPAIR = NI // 2
HT = H * T
GH = 3
G = 6
GK = GH * T
DV = DH + 1
COLS = NB * J
PAIRS = 2 * B * T
TILES = (PAIRS + E * (P - 1)) // P
SLOTS = TILES * P
NROWS = SLOTS + P


class Bag:
    pass


def phase(nc, fn, *args):
    with ExitStack() as c:
        used = []

        def sem(name):
            used.append(c.enter_context(nc.semaphore(name)))
            return used[-1]
        fn(nc, c, sem, *args)
        numbers = sorted(s.num for s in used)
        with nc.Block() as block:
            @block.gpsimd
            def _(g):
                start = 0
                for i in range(1, len(numbers) + 1):
                    if i == len(numbers) or numbers[i] != numbers[i - 1] + 1:
                        g.sem_clear(range(numbers[start], numbers[i - 1] + 1))
                        start = i


def group_col(g):
    return GK * g if g < G - 1 else HT - GK


def build(nc, d, out):
    h0 = nc.dram_tensor("tokens_d", (B * T + P, D), F32, kind="Internal").ap()
    base_d = nc.dram_tensor("base_d", (COLS, R, D), F32, kind="Internal").ap()
    xs_d = nc.dram_tensor("xs_d", (NROWS, D), F32, kind="Internal").ap()
    os_d = nc.dram_tensor("os_d", (NROWS, D), F32, kind="Internal").ap()
    b1_d = nc.dram_tensor("b1_d", (3, E * EH), BF16, kind="Internal").ap()
    b2_d = nc.dram_tensor("b2_d", (3, E * D), BF16, kind="Internal").ap()
    with ExitStack() as ctx:
        def sb(name, shape, dt=F32):
            return ctx.enter_context(nc.sbuf_tensor(name, shape, dt))
        k = Bag()
        k.ident = sb("ident", [P, P])
        k.ident_bf = sb("ident_bf", [P, P], BF16)
        k.ones = sb("ones", [P, P])
        k.xn = sb("xn", [R, COLS, D])
        k.logits = sb("logits", [R, COLS, E])
        k.ps = ctx.enter_context(nc.psum_tensor("ps", [P, 8, 512], F32))
        with ExitStack() as tower_ctx:
            def sbt(name, shape, dt=F32):
                return tower_ctx.enter_context(nc.sbuf_tensor(name, shape, dt))
            k.half = sbt("half", [P, J])
            k.attn = []
            for l in range(2):
                a = Bag()
                a.w = sbt(f"attn_w{l}", [P, 4, 2, D])
                a.qb, a.kb, a.vb = (sbt(f"attn_{n}b{l}", [P, 2]) for n in "qkv")
                a.ob = sbt(f"attn_ob{l}", [P, D])
                a.bias = sbt(f"score_bias{l}", [P, HT])
                k.attn.append(a)
            k.rot = sbt("rot", [P, P])
            k.cos, k.sin = sbt("cos", [P, T]), sbt("sin", [P, T])
            k.head_mask = sbt("head_mask", [P, QH])
            k.value_mask = sbt("value_mask", [GK, H])
            k.w1 = sbt("w1", [P, 2, FH], BF16)
            k.w2 = sbt("w2", [P, MH, D], BF16)
            k.wunit = sbt("wunit", [P, 2])
            k.conv = sbt("conv", [P, MH, 4])
            k.wr = sbt("wr", [P, 2, E])
            k.br = sbt("br", [P, E])
            phase(nc, setup_embed, d, k, h0, xs_d, os_d, b1_d, b2_d)
            phase(nc, tower, k, h0, base_d)
        phase(nc, experts, d, k, base_d, xs_d, os_d, b1_d, b2_d, out)



def setup_embed(nc, ctx, sem, d, k, h0, xs_d, os_d, b1_d, b2_d):
    def sb(name, shape, dt=F32):
        return ctx.enter_context(nc.sbuf_tensor(name, shape, dt))

    wp = sb("wp", [P, KF, D])
    wc = sb("wc", [P, KF, D + 1])
    g1, b1 = sb("g1", [P, KF]), sb("b1", [P, KF])
    mean_w = sb("mean_w", [P, P])
    bias_row = sb("bias_row", [1, D])
    out_bias = sb("out_bias", [RP, D])
    g2, b2, pos = sb("g2", [RP, D]), sb("b2", [RP, D]), sb("pos", [RP, J, D])
    cls, cls_pos = sb("cls", [B, D]), sb("cls_pos", [B, D])
    zero = sb("zero", [P, D])
    rel_rev = sb("rel_rev", [P, H, T])
    wt = [sb("w1_raw", [P, 2 * FH]), sb("w2_raw", [P, MH * D])]
    wq = [sb("w1_round", [P, 2 * FH]), sb("w2_round", [P, MH * D])]
    wsum, wscale = sb("wsum", [P, 2]), sb("wscale", [P, 2])
    eb = [sb("eb1", [E, EH]), sb("eb2", [E, D])]
    ebr = [sb("eb1_rest", [E, EH]), sb("eb2_rest", [E, D])]
    ebp = [[sb(f"eb{n + 1}_part{i}", [E, (EH, D)[n]], BF16) for i in range(3)] for n in range(2)]

    loads = [
        (k.ident[:, :], d.ident), (wp[:, :, :], d.W.rearrange("(k p) n -> p k n", p=P)),
        (g1[:, :], d.ln1_g), (b1[:, :], d.ln1_b), (bias_row[:, :], d.tok_bias.unsqueeze(0)),
        (g2[:, :], d.ln2_g.unsqueeze(0).broadcast_to([RP, D])), (b2[:, :], d.ln2_b.unsqueeze(0).broadcast_to([RP, D])),
        (pos[:, :, :], d.pos), (cls[:, :], d.cls.unsqueeze(0).broadcast_to([B, D])),
        (cls_pos[:, :], d.cls_pos.unsqueeze(0).broadcast_to([B, D])),
        (wt[0][:, :].rearrange("p (k n) -> p k n", k=2), d.w1T.rearrange("(k p) n -> p k n", p=P)),
        (wt[1][:, :].rearrange("p (k n) -> p k n", k=MH), d.w2T.rearrange("(k p) n -> p k n", p=P)),
        (k.rot[:, :], d.rot), (k.cos[:, :], d.cos), (k.sin[:, :], d.sin), (k.head_mask[:, :], d.head_mask),
        (k.value_mask[:, :], d.value_mask), (k.conv[:, :, :], d.conv),
        (k.wr[:, :, :], d.Wr.rearrange("(k p) n -> p k n", p=P)), (k.br[:, :], d.br.unsqueeze(0).broadcast_to([P, E])),
        (k.attn[0].bias[:, :], d.causal), (eb[0][:, :], d.b1), (eb[1][:, :], d.b2),
    ]
    for l in range(2):
        for n in range(4):
            loads.append((k.attn[l].w[:, n, :, :], d.attn_w[l][n].rearrange("(k p) n -> p k n", p=P)))
        for dst, src in zip((k.attn[l].qb, k.attn[l].kb, k.attn[l].vb), d.attn_b[l]):
            loads.append((dst[:, :], src))
        loads.append((k.attn[l].ob[:, :], d.attn_ob[l].unsqueeze(0).broadcast_to([P, D])))

    loaded, rel_loaded, filled = sem("loaded"), sem("rel_loaded"), sem("filled")
    const_set, rel_clear = sem("const_set"), sem("rel_clear")
    gained, mean_mm, centred, bias_mm = sem("gained"), sem("mean_mm"), sem("centred"), sem("bias_mm")
    pos_done, cls_done, rel_done = sem("pos_done"), sem("cls_done"), sem("rel_done")
    wsum_done, wsum_mm, wq_step = sem("wsum_done"), sem("wsum_mm"), sem("wq_step")
    split, split_out = sem("split"), sem("split_out")
    q_scaled = sem("q_scaled")

    with nc.Block() as block:
        @block.sync
        def _(sp):
            for dst, src in loads:
                sp.dma_start(dst, src).then_inc(loaded, 16)
            sp.wait_ge(rel_clear, 1)
            rel = bass.AP(d.relT.tensor, 128 - (T - 1), [[1, T], [2 * 128 + 1, H], [1, T]])
            for o in (0, 64):
                sp.dma_start(rel_rev[o:o + T, :, :], rel).then_inc(rel_loaded, 16)
            sp.wait_ge(const_set, 5)
            sp.dma_start(h0[B * T:B * T + P, :], zero[:, :]).then_inc(filled, 16)
            sp.dma_start(xs_d.rearrange("(a p) n -> p a n", p=P),
                         zero[:, :].unsqueeze(1).broadcast_to([P, NROWS // P, D])).then_inc(filled, 16)
            sp.dma_start(os_d[SLOTS:NROWS, :], zero[:, :]).then_inc(filled, 16)
            sp.wait_ge(cls_done, 1)
            sp.dma_start(h0[0:B * T, :].rearrange("(b t) n -> b t n", t=T)[:, 0, :], cls[:, :]).then_inc(filled, 16)
            for n, dst in enumerate((b1_d, b2_d)):
                for i in range(3):
                    sp.wait_ge(split, 5 * n + (1, 3, 5)[i])
                    sp.dma_start(dst[i, :].rearrange("(e n) -> e n", e=E), ebp[n][i][:, :]).then_inc(split_out, 16)
            sp.wait_ge(filled, 16 * 4)
            sp.wait_ge(split_out, 16 * 6)

        @block.gpsimd
        def _(g):
            g.memset(rel_rev[:, :, :], 0.0).then_inc(rel_clear, 1)
            g.memset(k.ones[:, :], 1.0).then_inc(const_set, 1)
            g.memset(mean_w[:, :], 1.0 / FP).then_inc(const_set, 1)
            g.memset(zero[:, :], 0.0).then_inc(const_set, 1)
            g.memset(k.half[:, :], -0.5).then_inc(const_set, 1)
            g.wait_ge(rel_loaded, 32)
            rr = rel_rev[:, :, :]
            back = bass.AP(rr.tensor, T - 1, [list(rr.ap[0]), [T, H], [-1, T]])
            g.tensor_copy(k.attn[1].bias[:, :].rearrange("p (h t) -> p h t", h=H), back).then_inc(rel_done, 1)

        @block.vector
        def _(v):
            v.wait_ge(loaded, 16 * len(loads))
            v.tensor_copy(k.ident_bf[:, :], k.ident[:, :]).then_inc(const_set, 1)
            for i in range(KF):
                v.tensor_scalar(wc[:, i, 0:D], wp[:, i, :], g1[:, i:i + 1], None, ALU.mult).then_inc(gained, 1)
            v.memset(wc[:, :, D:D + 1], 1.0).then_inc(gained, 1)
            v.tensor_add(cls[:, :], cls[:, :], cls_pos[:, :]).then_inc(cls_done, 1)
            v.tensor_tensor(pos[:, :, :], pos[:, :, :], b2[:, :].unsqueeze(1).broadcast_to([RP, J, D]), ALU.add)\
                .then_inc(pos_done, 1)
            for n in range(2):
                v.tensor_reduce(wsum[:, n:n + 1], wt[n][:, :], AX.X, ALU.add, apply_absolute_value=True)\
                    .then_inc(wsum_done, 1)
            v.wait_ge(mean_mm, 1)
            v.tensor_tensor(wc[:, :, 0:D], wc[:, :, 0:D], k.ps[:, 0, 0:D].unsqueeze(1).broadcast_to([P, KF, D]),
                            ALU.subtract).then_inc(centred, 1)
            v.wait_ge(bias_mm, 1)
            v.tensor_copy(out_bias[:, :], k.ps[0:RP, 1, 0:D]).then_inc(centred, 1)
            v.wait_ge(wsum_mm, 1)
            v.tensor_scalar(wsum[:, :], k.ps[:, 2, 0:2], 1.0 / (D * FH), 1e-5, ALU.mult, ALU.max).then_inc(wq_step, 1)
            v.wait_ge(wq_step, 1)
            v.reciprocal(wscale[:, :], wsum[:, :]).then_inc(wq_step, 1)
            v.wait_ge(wq_step, 2)
            v.reciprocal(k.wunit[:, :], wscale[:, :]).then_inc(wq_step, 1)
            for n, dst in enumerate((k.w1[:, :, :], k.w2[:, :, :])):
                v.tensor_scalar(wq[n][:, :], wt[n][:, :], wscale[:, n:n + 1], MAGIC, ALU.mult, ALU.add)\
                    .then_inc(wq_step, 1)
                v.wait_ge(wq_step, 4 + 3 * n)
                v.tensor_scalar(wq[n][:, :], wq[n][:, :], MAGIC, -1.0, ALU.subtract, ALU.max).then_inc(wq_step, 1)
                v.wait_ge(wq_step, 5 + 3 * n)
                v.tensor_scalar(dst.rearrange("p k n -> p (k n)"), wq[n][:, :], 1.0, None, ALU.min)\
                    .then_inc(wq_step, 1)
            for n in range(2):
                v.tensor_copy(ebp[n][0][:, :], eb[n][:, :]).then_inc(split, 1)
                v.wait_ge(split, 5 * n + 1)
                v.tensor_tensor(ebr[n][:, :], eb[n][:, :], ebp[n][0][:, :], ALU.subtract).then_inc(split, 1)
                v.wait_ge(split, 5 * n + 2)
                v.tensor_copy(ebp[n][1][:, :], ebr[n][:, :]).then_inc(split, 1)
                v.wait_ge(split, 5 * n + 3)
                v.tensor_tensor(ebr[n][:, :], ebr[n][:, :], ebp[n][1][:, :], ALU.subtract).then_inc(split, 1)
                v.wait_ge(split, 5 * n + 4)
                v.tensor_copy(ebp[n][2][:, :], ebr[n][:, :]).then_inc(split, 1)

        @block.scalar
        def _(a):
            a.wait_ge(loaded, 16 * len(loads))
            for l in range(2):
                a.mul(k.attn[l].qb[:, :], k.attn[l].qb[:, :], DH ** -0.5).then_inc(q_scaled, 1)

        @block.tensor
        def _(t):
            t.wait_ge(const_set, 5)
            t.wait_ge(loaded, 16 * len(loads))
            t.wait_ge(gained, KF)
            for i in range(KF):
                mm = t.matmul(k.ps[:, 0, 0:D], mean_w[:, :], wc[:, i, 0:D], start=(i == 0), stop=(i == KF - 1))
            mm.then_inc(mean_mm, 1)
            for i in range(KF):
                t.matmul(k.ps[0:RP, 1, 0:D], b1[:, i:i + 1].broadcast_to([P, RP]), wp[:, i, :],
                         start=(i == 0), stop=False)
            t.matmul(k.ps[0:RP, 1, 0:D], k.ones[0:1, 0:RP], bias_row[:, :], start=False, stop=True)\
                .then_inc(bias_mm, 1)
            t.wait_ge(wsum_done, 2)
            t.matmul(k.ps[:, 2, 0:2], k.ones[:, :], wsum[:, :], start=True, stop=True).then_inc(wsum_mm, 1)

    cs = []
    for s in range(CTX):
        c = Bag()
        c.s = s
        c.x = sb(f"x{s}", [P, KF, NPB])
        c.xx = sb(f"xx{s}", [P, KF, NPB])
        c.z = sb(f"z{s}", [RP, J, D])
        c.tok = sb(f"tok{s}", [RP, J, D])
        c.mean, c.var, c.rstd = (sb(f"{n}{s}", [RP, J]) for n in ("e_mean", "e_var", "e_rstd"))
        c.st, c.mv = sb(f"e_st{s}", [RP, J, 6]), sb(f"e_mv{s}", [RP, J, 2])
        c.x_loaded, c.squared, c.prod_mm = sem(f"x_loaded{s}"), sem(f"squared{s}"), sem(f"prod_mm{s}")
        c.norm, c.powers, c.stored = sem(f"e_norm{s}"), sem(f"e_powers{s}"), sem(f"stored{s}")
        c.z_done, c.tok_done = sem(f"z_done{s}"), sem(f"tok_done{s}")
        cs.append(c)
    ps = k.ps
    NORM = 9
    PIECES = 10

    def pieces(j):
        r, end = RP * j, RP * (j + 1)
        while r < end:
            n = min(end, (r // NP + 1) * NP) - r
            yield r - RP * j, n, r // NP, r % NP
            r += n

    with nc.Block() as block:
        @block.sync
        def _(sp):
            def load(c, it):
                sp.dma_start(c.x[:, :, :], d.x[:, bass.ds(it * (CTX * NPB) + c.s * NPB, NPB)]
                             .rearrange("(k p) n -> p k n", p=P)).then_inc(c.x_loaded, 16)

            for c in cs:
                load(c, 0)

            def body(it, last):
                for c in cs:
                    if not last:
                        sp.wait_ge(c.prod_mm, it + 1)
                        load(c, it + 1)
                for c in cs:
                    sp.wait_ge(c.tok_done, it + 1)
                    for j in range(J):
                        for row, n, img, s in pieces(j):
                            sp.dma_start(h0[bass.ds(it * (CTX * NI * T) + ((c.s * NI + img) * T + 1 + s), n), :],
                                         c.tok[row:row + n, j, :]).then_inc(c.stored, 16)

            with sp.Fori(0, ITERS - 1) as it:
                body(it, False)
            body(ITERS - 1, True)
            for c in cs:
                sp.wait_ge(c.stored, 16 * PIECES * ITERS)

        @block.scalar
        def _(a):
            with a.Fori(0, ITERS) as it:
                for c in cs:
                    a.wait_ge(c.x_loaded, it * 16 + 16)
                    for i in range(KF):
                        a.activation(c.xx[:, i, :], c.x[:, i, :], ACT.Square).then_inc(c.squared, 1)

        @block.tensor
        def _(t):
            def body(it, first):
                for c in cs:
                    t.wait_ge(c.x_loaded, it * 16 + 16)
                    if not first:
                        t.wait_ge(c.z_done, it)
                    for j in range(J):
                        for i in range(KF):
                            t.matmul(ps[0:RP, 4 * c.s + j, 0:D + 1], c.x[:, i, RP * j:RP * j + RP], wc[:, i, :],
                                     start=(i == 0), stop=(i == KF - 1))
                    t.wait_ge(c.squared, it * KF + KF)
                    for j in range(J):
                        for i in range(KF):
                            mm = t.matmul(ps[0:RP, 4 * c.s + 3, j:j + 1], c.xx[:, i, RP * j:RP * j + RP],
                                          k.ones[:, 0:1], start=(i == 0), stop=(i == KF - 1))
                    mm.then_inc(c.prod_mm, 1)

            body(0, True)
            with t.Fori(1, ITERS) as it:
                body(it, False)

        @block.gpsimd
        def _(g):
            def body(it, first):
                for c in cs:
                    g.wait_ge(c.norm, it * NORM + 4)
                    g.tensor_tensor(c.rstd[:, :], c.var[:, :], k.half[0:RP, :], ALU.pow).then_inc(c.powers, 1)
                for c in cs:
                    g.wait_ge(c.norm, it * NORM + 7)
                    g.tensor_tensor(c.rstd[:, :], c.var[:, :], k.half[0:RP, :], ALU.pow).then_inc(c.powers, 1)
                for c in cs:
                    g.wait_ge(c.norm, it * NORM + 9)
                    if not first:
                        g.wait_ge(c.stored, it * (16 * PIECES))
                    g.tensor_tensor(c.tok[:, :, :], c.z[:, :, :], pos[:, :, :], ALU.add).then_inc(c.tok_done, 1)

            body(0, True)
            with g.Fori(1, ITERS) as it:
                body(it, False)

        @block.vector
        def _(v):
            def body(it, first):
                for c in cs:
                    sums = ps[0:RP, 4 * c.s:4 * c.s + J, D:D + 1].rearrange("p j o -> p (j o)")
                    squares = ps[0:RP, 4 * c.s + 3, 0:J]
                    v.wait_ge(c.prod_mm, it + 1)
                    v.tensor_scalar(c.mean[:, :], sums, 1.0 / FP, None, ALU.mult).then_inc(c.norm, 1)
                    v.wait_ge(c.norm, it * NORM + 1)
                    v.scalar_tensor_tensor(c.mean[:, :], c.mean[:, :], -1.0, c.mean[:, :], ALU.mult, ALU.mult)\
                        .then_inc(c.norm, 1)
                    v.wait_ge(c.norm, it * NORM + 2)
                    v.scalar_tensor_tensor(c.var[:, :], squares, 1.0 / FP, c.mean[:, :], ALU.mult, ALU.add)\
                        .then_inc(c.norm, 1)
                    v.wait_ge(c.norm, it * NORM + 3)
                    v.tensor_scalar(c.var[:, :], c.var[:, :], EPS, None, ALU.add).then_inc(c.norm, 1)
                for c in cs:
                    v.wait_ge(c.powers, it * 2 + 1)
                    if not first:
                        v.wait_ge(c.tok_done, it)
                    for j in range(J):
                        zj = v.scalar_tensor_tensor(c.z[:, j, :], ps[0:RP, 4 * c.s + j, 0:D], c.rstd[:, j:j + 1],
                                                    out_bias[:, :], ALU.mult, ALU.add)
                    zj.then_inc(c.z_done, 1)
                    v.wait_ge(c.z_done, it + 1)
                    for j in range(J):
                        st = v.bn_stats(c.st[:, j, :], c.z[:, j, :])
                    st.then_inc(c.norm, 1)
                    v.wait_ge(c.norm, it * NORM + 5)
                    v.nop(nofuse=True)
                    for j in range(J):
                        mv = v.bn_aggr(c.mv[:, j, :], c.st[:, j, :])
                    mv.then_inc(c.norm, 1)
                    v.wait_ge(c.norm, it * NORM + 6)
                    v.tensor_scalar(c.var[:, :], c.mv[:, :, 1:2].rearrange("p j o -> p (j o)"), EPS, None, ALU.add)\
                        .then_inc(c.norm, 1)
                for c in cs:
                    v.wait_ge(c.powers, it * 2 + 2)
                    for j in range(J):
                        zj = v.tensor_scalar(c.z[:, j, :], c.z[:, j, :], c.mv[:, j, 0:1], c.rstd[:, j:j + 1],
                                             ALU.subtract, ALU.mult)
                    zj.then_inc(c.norm, 1)
                    v.wait_ge(c.norm, it * NORM + 8)
                    v.tensor_tensor(c.z[:, :, :], c.z[:, :, :], g2[:, :].unsqueeze(1).broadcast_to([RP, J, D]), ALU.mult)\
                        .then_inc(c.norm, 1)

            body(0, True)
            with v.Fori(1, ITERS) as it:
                body(it, False)



def tower(nc, ctx, sem, k, h0, base_d):
    def sb(name, shape, dt=F32):
        return ctx.enter_context(nc.sbuf_tensor("t_" + name, shape, dt))

    SIGNALS = dict(
        h_loaded=16, base_stored=16,
        ln=16,
        ln_power=4, xt_mm=3, xt=3,
        qk_mm=8, q0=4, rope_mm=4, rope_cos=4, rope_sin=4, rope_sum=4, q1=4, keys=4,
        v_mm=4, v_ev=4, vt_mm=8, values=8,
        score_mm=8, biased=8, row_max=8, shifted=8, prob=8, probt_mm=8, probt=8, pv_mm=8, inv_sum=8, y=8,
        yt_mm=8, yt=8, proj_mm=2, h_bias=2, h_attn=2,
        quant=7,
        xq_mm=1, xq=1, unit_mm=1, unit=1, hid_mm=8, hid=8, mid=8, left=8, right=8, silu=8, pad=1,
        hidt_mm=3, quant2=24,
        hq_mm=3, hq=3, out_mm=3, h_ffn=3,
        logit_mm=1, logit=1, xn_kept=1, base=1)
    assert 2 * len(SIGNALS) < 200

    cs = []
    for s in range(CTX):
        c = Bag()
        c.s, c.sem = s, {n: sem(f"{n}_{s}") for n in SIGNALS}
        c.ps = k.ps[:, 4 * s:4 * s + 4, :]
        c.h, c.hb, c.xh, c.qf = (sb(f"{n}{s}", [R, J, D]) for n in ("h", "hb", "xh", "qf"))
        c.base = c.qf
        c.st, c.mv = sb(f"st{s}", [R, J, 6]), sb(f"mv{s}", [R, J, 2])
        c.var, c.rstd = sb(f"var{s}", [R, J]), sb(f"rstd{s}", [R, J])
        c.xt = sb(f"xt{s}", [P, 2, NTP])
        c.qt = sb(f"qt{s}", [P, 2, NTP + 27])
        c.v = sb(f"v{s}", [GK, NI, H, DV])
        c.sc = sb(f"sc{s}", [P, HT])
        c.mx, c.rs = sb(f"mx{s}", [P, H]), sb(f"rs{s}", [P, H])
        c.pt = sb(f"pt{s}", [GK, G, P])
        c.y = sb(f"y{s}", [P, D])
        c.yt = sb(f"yt{s}", [P, 2, NTP])
        c.qb = sb(f"qb{s}", [R, J, D], BF16)
        c.am, c.unit_in = sb(f"am{s}", [R, J]), sb(f"unit_in{s}", [R, J])
        c.am2, c.unit2 = sb(f"am2{s}", [R, 1]), sb(f"unit2{s}", [R, J])
        words = max(4 * NT * 3 + 2 * NI * GK + 2 * NI * QH * T,
                    2 * MH * NTP + FH + FH // 2 + MH * NTP // 2 + NTP + NTP)
        region = sb(f"region{s}", [P, words])
        at = [0]

        def take(n, pattern=None, dt=F32, **dims):
            a = region[:, at[0]:at[0] + n]
            at[0] += n
            if dt != F32:
                a = a.bitcast(dt)
            return a.rearrange(pattern, **dims) if pattern else a

        c.qk = take(4 * NT, "p (i t) -> p i t", i=4)
        c.rc = take(4 * NT, "p (i t) -> p i t", i=4)
        c.rn = take(4 * NT, "p (i t) -> p i t", i=4)
        c.vr = take(2 * NI * GK, "p (f i r t) -> p f i r t", f=2, i=NI, r=GH)
        c.kd = take(2 * NI * QH * T, "p (f i o t) -> p f i o t", f=2, i=NI, o=QH)
        at[0] = 0
        c.t0 = take(MH * NTP, "p (m t) -> p m t", m=MH)
        c.a = take(MH * NTP, "p (m t) -> p m t", m=MH)
        c.qf2 = take(FH)
        c.qb2 = take(FH // 2, dt=BF16)
        c.hq = take(MH * NTP // 2, "p (m t) -> p m t", dt=BF16, m=MH)
        c.xq = take(NTP, "p (f t) -> p f t", dt=BF16, f=2)
        c.unit = take(NTP)
        cs.append(c)

    def wait(eng, c, it, name, n):
        eng.wait_ge(c.sem[name], it * SIGNALS[name] + n)

    images = "p (i t) -> p i t"
    img_bc = lambda table: table[:, :].unsqueeze(1).broadcast_to([P, NI, T])
    bft = lambda bank: bank.bitcast(BF16)

    def sync_program(sp):
        def load(c, it):
            row = it * (CTX * NT) + c.s * NT
            sp.dma_start(c.h[:, :, :], h0[bass.ds(row, NTP), :].rearrange("(j p) n -> p j n", p=R))\
                .then_inc(c.sem["h_loaded"], 16)

        for c in cs:
            load(c, 0)

        def body(it, last):
            for c in cs:
                wait(sp, c, it, "base", 1)
                sp.dma_start(base_d[bass.ds(it * (CTX * J) + c.s * J, J), :, :].rearrange("j p n -> p j n"),
                             c.base[:, :, :]).then_inc(c.sem["base_stored"], 16)
                wait(sp, c, it, "base_stored", 16)
                if not last:
                    load(c, it + 1)

        with sp.Fori(0, ITERS - 1) as it:
            body(it, False)
        body(ITERS - 1, True)

    def vector_program(v):
        for c in cs:
            v.memset(c.qt[:, :, NT:NTP + 27], 0.0)
            v.memset(c.yt[:, :, NT:NTP], 0.0)
            v.memset(c.pt[:, :, :], 1.0)
            for i in range(NI):
                v.tensor_copy(c.v[:, i, :, DH:DV], k.value_mask[:, :].unsqueeze(2))

        def layer_norm(c, it, n):
            if n == 0:
                wait(v, c, it, "h_loaded", 16)
            elif n == 2:
                wait(v, c, it, "h_ffn", 3)
            else:
                wait(v, c, it, "h_attn", (n + 1) // 2)
            for j in range(J):
                st = v.bn_stats(c.st[:, j, :], c.h[:, j, :])
            st.then_inc(c.sem["ln"], 1)
            wait(v, c, it, "ln", 4 * n + 1)
            v.nop(nofuse=True)
            for j in range(J):
                mv = v.bn_aggr(c.mv[:, j, :], c.st[:, j, :])
            mv.then_inc(c.sem["ln"], 1)
            wait(v, c, it, "ln", 4 * n + 2)
            v.tensor_scalar(c.var[:, :], c.mv[:, :, 1:2].rearrange("p j o -> p (j o)"), EPS, None, ALU.add)\
                .then_inc(c.sem["ln"], 1)

        def normalise(c, it, n):
            wait(v, c, it, "ln_power", n + 1)
            for j in range(J):
                xj = v.tensor_scalar(c.xh[:, j, :], c.h[:, j, :], c.mv[:, j, 0:1], c.rstd[:, j:j + 1],
                                     ALU.subtract, ALU.mult)
            xj.then_inc(c.sem["ln"], 1)

        def rotate(c, it):
            for i in range(4):
                wait(v, c, it, "rope_mm", i + 1)
                v.tensor_tensor(c.rn[:, i, :].rearrange(images, i=NI), c.ps[:, i, 0:NT].rearrange(images, i=NI),
                                img_bc(k.sin), ALU.mult).then_inc(c.sem["rope_sin"], 1)
            for i in range(4):
                wait(v, c, it, "rope_cos", i + 1)
                wait(v, c, it, "rope_sin", i + 1)
                dst = c.qt[:, i, 0:NT] if i < 2 else c.rn[:, i, :]
                v.tensor_tensor(dst, c.rc[:, i, :], c.rn[:, i, :], ALU.add).then_inc(c.sem["rope_sum"], 1)

        def spread_keys(c, it, l):
            for f in range(2):
                wait(v, c, it, *(("rope_sum", 3 + f) if l == 0 else ("q1", 3 + f)))
                for o in range(QH):
                    kd = v.tensor_scalar(c.kd[:, f, :, o, :], c.rn[:, 2 + f, :].rearrange(images, i=NI),
                                         k.head_mask[:, o:o + 1], None, ALU.mult)
                kd.then_inc(c.sem["keys"], 1)

        def values(c, it, l):
            for q in range(4):
                wait(v, c, it, "vt_mm", 4 * l + q + 1)
                src = c.ps[0:GK, (q + 2) % 4, :].rearrange("p (i h n) -> p i h n", i=2, h=H)
                for i in range(2):
                    vv = v.tensor_tensor(c.v[:, 2 * q + i, :, 0:DH], src[:, i, :, :],
                                         k.value_mask[:, :].unsqueeze(2).broadcast_to([GK, H, DH]), ALU.mult)
                vv.then_inc(c.sem["values"], 1)

        def bias_and_max(c, it, q):
            l = q // NPAIR
            wait(v, c, it, "score_mm", q + 1)
            if q > 0:
                wait(v, c, it, "probt_mm", q)
            by_bank = lambda table: table[:, :].rearrange("p (f r n) -> p r f n", f=2, r=2)
            v.tensor_tensor(by_bank(c.sc), c.ps[:, 0:2, 0:HT // 2].rearrange("p r (f n) -> p r f n", f=2),
                            by_bank(k.attn[l].bias), ALU.add)\
                .then_inc(c.sem["biased"], 1)
            wait(v, c, it, "biased", q + 1)
            v.tensor_reduce(c.mx[:, :], c.sc[:, :].rearrange("p (h t) -> p h t", h=H), AX.X, ALU.max)\
                .then_inc(c.sem["row_max"], 1)

        def divide(c, it, q):
            ysum = c.ps[:, 0, 0:H * DV].rearrange("p (h n) -> p h n", h=H)
            wait(v, c, it, "pv_mm", q + 1)
            v.reciprocal(c.rs[:, :], ysum[:, :, DH:DV].rearrange("p h o -> p (h o)")).then_inc(c.sem["inv_sum"], 1)
            wait(v, c, it, "inv_sum", q + 1)
            if q > 0:
                wait(v, c, it, "yt_mm", q)
            v.tensor_tensor(c.y[:, :].rearrange("p (h n) -> p h n", h=H), ysum[:, :, 0:DH],
                            c.rs[:, :].unsqueeze(2).broadcast_to([P, H, DH]), ALU.mult).then_inc(c.sem["y"], 1)

        def add_attention(c, it, l):
            wait(v, c, it, "proj_mm", l + 1)
            wait(v, c, it, "h_bias", l + 1)
            v.tensor_tensor(c.h[:, :, :].rearrange("p j n -> p (j n)"),
                            c.ps[0:R, 2:4, :].rearrange("p b n -> p (b n)")[:, 0:J * D],
                            c.hb[:, :, :].rearrange("p j n -> p (j n)"), ALU.add).then_inc(c.sem["h_attn"], 1)

        def quantise_input(c, it):
            def step(n):
                wait(v, c, it, "quant", n)
            wait(v, c, it, "ln", 8)
            v.tensor_reduce(c.am[:, :], c.xh[:, :, :], AX.X, ALU.max, apply_absolute_value=True)\
                .then_inc(c.sem["quant"], 1)
            step(1)
            v.tensor_scalar(c.am[:, :], c.am[:, :], 1e-5, None, ALU.max).then_inc(c.sem["quant"], 1)
            step(2)
            v.reciprocal(c.am[:, :], c.am[:, :]).then_inc(c.sem["quant"], 1)
            step(3)
            v.tensor_scalar(c.am[:, :], c.am[:, :], 127.0, None, ALU.mult).then_inc(c.sem["quant"], 1)
            step(4)
            v.reciprocal(c.unit_in[:, :], c.am[:, :]).then_inc(c.sem["quant"], 1)
            for j in range(J):
                qj = v.tensor_scalar(c.qf[:, j, :], c.xh[:, j, :], c.am[:, j:j + 1], MAGIC, ALU.mult, ALU.add)
            qj.then_inc(c.sem["quant"], 1)
            step(6)
            v.tensor_scalar(c.qb[:, :, :], c.qf[:, :, :], MAGIC, None, ALU.subtract).then_inc(c.sem["quant"], 1)

        def hidden(c, it, m):
            wait(v, c, it, "hid_mm", m + 1)
            if m == 0:
                wait(v, c, it, "unit", 1)
                v.memset(c.a[:, :, NT:NTP], 0.0).then_inc(c.sem["pad"], 1)
            v.tensor_tensor(c.t0[:, m, 0:NT], c.ps[:, (m + 2) % 4, 0:NT], c.unit[:, 0:NT], ALU.mult)\
                .then_inc(c.sem["hid"], 1)

        def convolve(c, it, m):
            am = c.a[:, m, 0:NT].rearrange(images, i=NI)
            tm = c.t0[:, m, 0:NT].rearrange(images, i=NI)
            wait(v, c, it, "mid", m + 1)
            v.scalar_tensor_tensor(am[:, :, 1:T], tm[:, :, 0:T - 1], k.conv[:, m, 0:1], am[:, :, 1:T],
                                   ALU.mult, ALU.add).then_inc(c.sem["left"], 1)
            wait(v, c, it, "left", m + 1)
            v.scalar_tensor_tensor(am[:, :, 0:T - 1], tm[:, :, 1:T], k.conv[:, m, 2:3], am[:, :, 0:T - 1],
                                   ALU.mult, ALU.add).then_inc(c.sem["right"], 1)

        def quantise_hidden(c, it, j):
            src = c.ps[0:R, 2 * (j % 2):2 * (j % 2) + 2, :].rearrange("p b n -> p (b n)")

            def step(n):
                wait(v, c, it, "quant2", 8 * j + n)
            wait(v, c, it, "hidt_mm", j + 1)
            v.tensor_reduce(c.am2[:, :], src, AX.X, ALU.max, apply_absolute_value=True).then_inc(c.sem["quant2"], 1)
            step(1)
            v.tensor_scalar(c.am2[:, :], c.am2[:, :], 1e-5, None, ALU.max).then_inc(c.sem["quant2"], 1)
            step(2)
            v.reciprocal(c.am2[:, :], c.am2[:, :]).then_inc(c.sem["quant2"], 1)
            step(3)
            v.tensor_scalar(c.am2[:, :], c.am2[:, :], 127.0, None, ALU.mult).then_inc(c.sem["quant2"], 1)
            step(4)
            v.reciprocal(c.unit2[:, j:j + 1], c.am2[:, :]).then_inc(c.sem["quant2"], 1)
            v.tensor_scalar(c.qf2[0:R, :], src, c.am2[:, :], MAGIC, ALU.mult, ALU.add).then_inc(c.sem["quant2"], 1)
            step(6)
            if j > 0:
                wait(v, c, it, "hq_mm", j)
            v.tensor_scalar(c.qb2[0:R, :], c.qf2[0:R, :], MAGIC, None, ALU.subtract).then_inc(c.sem["quant2"], 1)
            v.tensor_tensor(c.unit2[:, j:j + 1], c.unit2[:, j:j + 1], k.wunit[0:R, 1:2], ALU.mult)\
                .then_inc(c.sem["quant2"], 1)

        def add_ffn(c, it, j):
            wait(v, c, it, "out_mm", j + 1)
            wait(v, c, it, "quant2", 8 * j + 8)
            v.scalar_tensor_tensor(c.h[:, j, :], c.ps[0:R, 2 * (j % 2) + 1, 0:D], c.unit2[:, j:j + 1], c.h[:, j, :],
                                   ALU.mult, ALU.add).then_inc(c.sem["h_ffn"], 1)

        with v.Fori(0, ITERS) as it:
            def norm(n):
                for c in cs:
                    layer_norm(c, it, n)
                for c in cs:
                    normalise(c, it, n)

            def attention(l):
                for c in cs:
                    if l == 0:
                        rotate(c, it)
                    spread_keys(c, it, l)
                for c in cs:
                    values(c, it, l)
                for p in range(NPAIR):
                    for c in cs:
                        bias_and_max(c, it, NPAIR * l + p)
                    for c in cs:
                        divide(c, it, NPAIR * l + p)
                for c in cs:
                    add_attention(c, it, l)

            norm(0)
            attention(0)
            norm(1)
            for c in cs:
                quantise_input(c, it)
            for m in range(MH + 1):
                for c in cs:
                    if m < MH:
                        hidden(c, it, m)
                    if m > 0:
                        convolve(c, it, m - 1)
            for j in range(J):
                for c in cs:
                    quantise_hidden(c, it, j)
                for c in cs:
                    add_ffn(c, it, j)
            norm(2)
            attention(1)
            norm(3)
            for c in cs:
                wait(v, c, it, "logit_mm", 1)
                v.tensor_tensor(k.logits[:, bass.ds(it * (CTX * J) + c.s * J, J), :],
                                c.ps[0:R, 2, 0:J * E].rearrange("p (j e) -> p j e", j=J),
                                k.br[0:R, :].unsqueeze(1).broadcast_to([R, J, E]), ALU.add).then_inc(c.sem["logit"], 1)

    def gpsimd_program(g):
        def power(c, it, n):
            wait(g, c, it, "ln", 4 * n + 3)
            g.tensor_tensor(c.rstd[:, :], c.var[:, :], k.half[0:R, :], ALU.pow).then_inc(c.sem["ln_power"], 1)

        def add_bias(c, it, l):
            wait(g, c, it, "ln", 8 * l + 4)
            g.tensor_tensor(c.hb[:, :, :], c.h[:, :, :], k.attn[l].ob[0:R, :].unsqueeze(1).broadcast_to([R, J, D]),
                            ALU.add).then_inc(c.sem["h_bias"], 1)

        def rope_cos(c, it):
            for i in range(4):
                wait(g, c, it, "q0", i + 1)
                g.tensor_tensor(c.rc[:, i, :].rearrange(images, i=NI), c.qk[:, i, :].rearrange(images, i=NI),
                                img_bc(k.cos), ALU.mult).then_inc(c.sem["rope_cos"], 1)

        def shift(c, it, q):
            wait(g, c, it, "row_max", q + 1)
            s3 = c.sc[:, :].rearrange("p (h t) -> p h t", h=H)
            g.tensor_tensor(s3, s3, c.mx[:, :].unsqueeze(2).broadcast_to([P, H, T]), ALU.subtract)\
                .then_inc(c.sem["shifted"], 1)

        with g.Fori(0, ITERS) as it:
            def attention(l):
                for c in cs:
                    power(c, it, 2 * l)
                for c in cs:
                    if l == 0:
                        rope_cos(c, it)
                    add_bias(c, it, l)
                for p in range(NPAIR):
                    for c in cs:
                        shift(c, it, NPAIR * l + p)

            attention(0)
            for c in cs:
                power(c, it, 1)
            attention(1)
            for c in cs:
                power(c, it, 3)
            for c in cs:
                wait(g, c, it, "ln", 16)
                g.tensor_copy(k.xn[:, bass.ds(it * (CTX * J) + c.s * J, J), :], c.xh[:, :, :])\
                    .then_inc(c.sem["xn_kept"], 1)
                wait(g, c, it, "logit", 1)
                wait(g, c, it, "xn_kept", 1)
                g.tensor_tensor(c.base[:, :, :], c.h[:, :, :], c.xh[:, :, :], ALU.add).then_inc(c.sem["base"], 1)

    def scalar_program(a):
        def evacuate_x(c, it, n):
            wait(a, c, it, "xt_mm", max(n, 1))
            a.activation(c.xt[:, :, :], c.ps[:, 0:2, 0:NTP], ACT.Copy).then_inc(c.sem["xt"], 1)

        def queries_keys(c, it, l):
            w = k.attn[l]
            for i in range(4):
                wait(a, c, it, "qk_mm", 4 * l + i + 1)
                dst = c.qk[:, i, :] if l == 0 else c.qt[:, i, 0:NT] if i < 2 else c.rn[:, i, :]
                bias, scale = (w.qb, DH ** -0.5) if i < 2 else (w.kb, 1.0)
                a.activation(dst, c.ps[:, i, 0:NT], ACT.Identity, bias=bias[:, i % 2:i % 2 + 1], scale=scale)\
                    .then_inc(c.sem["q0" if l == 0 else "q1"], 1)

        def value_rows(c, it, l):
            for f in range(2):
                wait(a, c, it, "v_mm", 2 * l + f + 1)
                a.activation(c.vr[:, f, :, :, :],
                             c.ps[:, f, 0:NT].rearrange(images, i=NI).unsqueeze(2).broadcast_to([P, NI, GH, T]),
                             ACT.Identity, bias=k.attn[l].vb[:, f:f + 1]).then_inc(c.sem["v_ev"], 1)

        def exponent(c, it, q):
            wait(a, c, it, "shifted", q + 1)
            a.activation(c.sc[:, :], c.sc[:, :], ACT.Exp).then_inc(c.sem["prob"], 1)

        def evacuate_prob(c, it, q):
            wait(a, c, it, "probt_mm", q + 1)
            src = c.ps[0:GK, 2:4, :].rearrange("p b n -> p (b n)")[:, 0:G * P].rearrange("p (g i t) -> p g i t", g=G, i=2)
            for i in range(2):
                pt = a.activation(c.pt[:, :, 64 * i:64 * i + T], src[:, :, i, 0:T], ACT.Copy)
            pt.then_inc(c.sem["probt"], 1)

        def evacuate_y(c, it, q):
            wait(a, c, it, "yt_mm", q + 1)
            p = q % NPAIR
            src = c.ps[:, 1, 0:2 * P].rearrange("p (f i t) -> p f i t", f=2, i=2)
            dst = c.yt[:, :, 2 * T * p:2 * T * (p + 1)].rearrange("p f (i t) -> p f i t", i=2)
            a.activation(dst, src[:, :, :, 0:T], ACT.Copy).then_inc(c.sem["yt"], 1)

        with a.Fori(0, ITERS) as it:
            def attention(l):
                for c in cs:
                    evacuate_x(c, it, 2 * l)
                for c in cs:
                    queries_keys(c, it, l)
                for c in cs:
                    value_rows(c, it, l)
                for p in range(NPAIR):
                    q = NPAIR * l + p
                    for c in cs:
                        exponent(c, it, q)
                    for c in cs:
                        evacuate_prob(c, it, q)
                    for c in cs:
                        evacuate_y(c, it, q)

            attention(0)
            for c in cs:
                wait(a, c, it, "xq_mm", 1)
                src = bft(c.ps[:, 0, :])[:, 0:2 * J * (R + 1)].rearrange("p (f j t) -> p f j t", f=2, j=J)
                a.activation(c.xq[:, :, :].rearrange("p f (j t) -> p f j t", j=J), src[:, :, :, 0:R], ACT.Copy)\
                    .then_inc(c.sem["xq"], 1)
            for c in cs:
                wait(a, c, it, "unit_mm", 1)
                a.activation(c.unit, c.ps[:, 1, 0:NTP], ACT.Copy, scale=k.wunit[:, 0:1]).then_inc(c.sem["unit"], 1)
            for m in range(MH):
                for c in cs:
                    wait(a, c, it, "hid", m + 1)
                    a.activation(c.a[:, m, 0:NT], c.t0[:, m, 0:NT], ACT.Identity, bias=k.conv[:, m, 3:4],
                                 scale=k.conv[:, m, 1:2]).then_inc(c.sem["mid"], 1)
            for c in cs:
                for m in range(MH):
                    wait(a, c, it, "right", m + 1)
                    a.activation(c.a[:, m, 0:NT], c.a[:, m, 0:NT], ACT.Silu).then_inc(c.sem["silu"], 1)
            for j in range(J):
                for c in cs:
                    wait(a, c, it, "hq_mm", j + 1)
                    src = bft(c.ps[:, 2 * (j % 2), :])[:, 0:MH * (R + 1)].rearrange("p (m t) -> p m t", m=MH)
                    a.activation(c.hq[:, :, R * j:R * j + R], src[:, :, 0:R], ACT.Copy).then_inc(c.sem["hq"], 1)
            attention(1)
            for c in cs:
                evacuate_x(c, it, 3)

    def tensor_program(t):
        def transpose_x(c, it, n):
            wait(t, c, it, "ln", 4 * n + 4)
            for j in range(J):
                for f in range(2):
                    tr = t.transpose(c.ps[:, f, R * j:R * j + R], c.xh[:, j, P * f:P * f + P], k.ident[0:R, 0:R])
            tr.then_inc(c.sem["xt_mm"], 1)

        def project(c, which, l, f, bank):
            w = k.attn[l].w
            for i in range(2):
                mm = t.matmul(c.ps[:, bank, 0:NT], w[:, which, i, P * f:P * f + P], c.xt[:, i, 0:NT],
                              start=(i == 0), stop=(i == 1))
            return mm

        def queries_keys(c, it, l):
            wait(t, c, it, "xt", l + 1)
            for i in range(4):
                project(c, i // 2, l, i % 2, i).then_inc(c.sem["qk_mm"], 1)

        def rotate_pairs(c, it):
            for i in range(4):
                wait(t, c, it, "q0", i + 1)
                t.matmul(c.ps[:, i, 0:NT], k.rot[:, :], c.qk[:, i, :], start=True, stop=True)\
                    .then_inc(c.sem["rope_mm"], 1)

        def value_products(c, it, l):
            for f in range(2):
                wait(t, c, it, *(("rope_sin", f + 1) if l == 0 else ("q1", f + 1)))
                project(c, 2, l, f, f).then_inc(c.sem["v_mm"], 1)

        def value_transposes(c, it, l):
            for q in range(4):
                if q < 2:
                    wait(t, c, it, *(("rope_sin", 3 + q) if l == 0 else ("q1", 3 + q)))
                if q == 0:
                    wait(t, c, it, "v_ev", 2 * l + 2)
                for i in range(2):
                    for f in range(2):
                        tr = t.transpose(c.ps[0:GK, (q + 2) % 4, D * i + P * f:D * i + P * f + P],
                                         c.vr[:, f, 2 * q + i, :, :].rearrange("p r t -> p (r t)"), k.ident[:, :])
                tr.then_inc(c.sem["vt_mm"], 1)

        def scores(c, it, q):
            l, p = divmod(q, NPAIR)
            if p == 0:
                wait(t, c, it, *(("rope_sum", 2) if l == 0 else ("q1", 2)))
                wait(t, c, it, "keys", 2 * l + 2)
                wait(t, c, it, "values", 4 * l + 4)
            else:
                wait(t, c, it, "y", q)
                wait(t, c, it, "yt", q)
            t.nop(nofuse=True)
            for f in range(2):
                for r in range(2):
                    for i in range(2):
                        rows = slice(64 * r, 64 * r + 64)
                        n = 2 * p + i
                        mm = t.matmul(c.ps[64 * i:64 * i + 64, r, QH * T * f:QH * T * (f + 1)],
                                      c.qt[rows, f, T * n:T * n + 64],
                                      c.kd[rows, f, n, :, :].rearrange("p o t -> p (o t)"), start=True, stop=True,
                                      skip_group_check=True)
            mm.then_inc(c.sem["score_mm"], 1)

        def transpose_prob(c, it, q):
            wait(t, c, it, "prob", q + 1)
            if q % NPAIR:
                wait(t, c, it, "probt", q)
            dst = c.ps[0:GK, 2:4, :].rearrange("p b n -> p (b n)")
            for g in range(G):
                tr = t.transpose(dst[:, P * g:P * g + P], c.sc[:, group_col(g):group_col(g) + GK], k.ident[:, :])
            tr.then_inc(c.sem["probt_mm"], 1)

        def weigh_values(c, it, q):
            wait(t, c, it, "probt", q + 1)
            t.nop(nofuse=True)
            for i in range(2):
                for g in range(G):
                    h = GH * g
                    n = min(GH, H - h)
                    mm = t.matmul(c.ps[64 * i:64 * i + 64, 0, DV * h:DV * (h + n)], c.pt[:, g, 64 * i:64 * i + 64],
                                  c.v[:, 2 * (q % NPAIR) + i, h:h + n, :].rearrange("p h n -> p (h n)"),
                                  start=True, stop=True, skip_group_check=True)
            mm.then_inc(c.sem["pv_mm"], 1)

        def transpose_y(c, it, q):
            wait(t, c, it, "y", q + 1)
            for f in range(2):
                tr = t.transpose(c.ps[:, 1, P * f:P * f + P], c.y[:, P * f:P * f + P], k.ident[:, :])
            tr.then_inc(c.sem["yt_mm"], 1)

        def output_projection(c, it, l):
            wait(t, c, it, "yt", NPAIR * (l + 1))
            dst = c.ps[0:R, 2:4, :].rearrange("p b n -> p (b n)")
            for j in range(J):
                for f in range(2):
                    mm = t.matmul(dst[:, D * j:D * j + D], c.yt[:, f, R * j:R * j + R], k.attn[l].w[:, 3, f, :],
                                  start=(f == 0), stop=(f == 1))
            mm.then_inc(c.sem["proj_mm"], 1)

        with t.Fori(0, ITERS) as it:
            def attention(l):
                for c in cs:
                    transpose_x(c, it, 2 * l)
                for c in cs:
                    queries_keys(c, it, l)
                if l == 0:
                    for c in cs:
                        rotate_pairs(c, it)
                for c in cs:
                    value_products(c, it, l)
                for c in cs:
                    value_transposes(c, it, l)
                for p in range(NPAIR):
                    q = NPAIR * l + p
                    for c in cs:
                        scores(c, it, q)
                    for c in cs:
                        transpose_prob(c, it, q)
                    for c in cs:
                        weigh_values(c, it, q)
                    for c in cs:
                        transpose_y(c, it, q)
                for c in cs:
                    output_projection(c, it, l)

            attention(0)
            for c in cs:
                wait(t, c, it, "quant", 7)
                dst = bft(c.ps[:, 0, :])
                for j in range(J):
                    for f in range(2):
                        o = (R + 1) * (J * f + j)
                        tr = t.transpose(dst[:, o:o + R], c.qb[:, j, P * f:P * f + P], k.ident_bf[0:R, 0:R])
                tr.then_inc(c.sem["xq_mm"], 1)
                for j in range(J):
                    mm = t.matmul(c.ps[:, 1, R * j:R * j + R], c.unit_in[:, j:j + 1].broadcast_to([R, P]),
                                  k.ident[0:R, 0:R], start=True, stop=True)
                mm.then_inc(c.sem["unit_mm"], 1)
            for m in range(MH):
                for c in cs:
                    if m == 0:
                        wait(t, c, it, "xq", 1)
                        wait(t, c, it, "h_attn", 1)
                    if m == 3:
                        wait(t, c, it, "unit", 1)
                    if m >= 4:
                        wait(t, c, it, "hid", m - 3)
                    for f in range(2):
                        mm = t.matmul(c.ps[:, (m + 2) % 4, 0:NT], k.w1[:, f, P * m:P * m + P], c.xq[:, f, 0:NT],
                                      start=(f == 0), stop=(f == 1))
                    mm.then_inc(c.sem["hid_mm"], 1)

            def transpose_hidden(c, it, j):
                if j == 0:
                    wait(t, c, it, "silu", MH)
                    wait(t, c, it, "pad", 1)
                if j == 1:
                    wait(t, c, it, "hid", MH)
                if j == 2:
                    wait(t, c, it, "h_ffn", 1)
                dst = c.ps[0:R, 2 * (j % 2):2 * (j % 2) + 2, :].rearrange("p b n -> p (b n)")
                for m in range(MH):
                    tr = t.transpose(dst[:, P * m:P * m + P], c.a[:, m, R * j:R * j + R], k.ident[:, :])
                tr.then_inc(c.sem["hidt_mm"], 1)

            for c in cs:
                transpose_hidden(c, it, 0)
            for j in range(J):
                if j == 0:
                    for c in cs:
                        transpose_hidden(c, it, 1)
                for c in cs:
                    wait(t, c, it, "quant2", 8 * j + 7)
                    dst = bft(c.ps[:, 2 * (j % 2), :])
                    for m in range(MH):
                        tr = t.transpose(dst[:, (R + 1) * m:(R + 1) * m + R], c.qb2[0:R, P * m:P * m + P],
                                         k.ident_bf[0:R, 0:R])
                    tr.then_inc(c.sem["hq_mm"], 1)
                for c in cs:
                    wait(t, c, it, "hq", j + 1)
                    for m in range(MH):
                        mm = t.matmul(c.ps[0:R, 2 * (j % 2) + 1, 0:D], c.hq[:, m, R * j:R * j + R], k.w2[:, m, :],
                                      start=(m == 0), stop=(m == MH - 1))
                    mm.then_inc(c.sem["out_mm"], 1)
                if j == 0:
                    for c in cs:
                        transpose_hidden(c, it, 2)
            attention(1)
            for c in cs:
                transpose_x(c, it, 3)
            for c in cs:
                wait(t, c, it, "xt", 3)
                for j in range(J):
                    for f in range(2):
                        mm = t.matmul(c.ps[0:R, 2, E * j:E * j + E], c.xt[:, f, R * j:R * j + R], k.wr[:, f, :],
                                      start=(f == 0), stop=(f == 1))
                mm.then_inc(c.sem["logit_mm"], 1)

    with nc.Block() as block:
        block.sync(sync_program)
        block.vector(vector_program)
        block.gpsimd(gpsimd_program)
        block.scalar(scalar_program)
        block.tensor(tensor_program)



def experts(nc, ctx, sem, d, k, base_d, xs_d, os_d, b1_d, b2_d, out):
    def sb(name, shape, dt=F32):
        return ctx.enter_context(nc.sbuf_tensor(name, shape, dt))

    ew1 = sb("ew1", [P, E, 2, EH])
    ew2 = sb("ew2", [P, E, EH // P, D])
    eb1, eb2 = sb("eb1_rows", [3, E, EH], BF16), sb("eb2_rows", [3, E, D], BF16)
    ones_bf = sb("ones_bf", [P, P], BF16)
    w1, w2 = sb("weight1", [R, COLS]), sb("weight2", [R, COLS])
    dest = [sb("dest1", [R, COLS], U32), sb("dest2", [R, COLS], U32)]
    tile_expert = sb("tile_expert", [1, TILES], I32)
    ew_loaded, eb_loaded = sem("ew_loaded"), sem("eb_loaded")
    scattered = [sem("scattered1"), sem("scattered2")]
    ps = k.ps

    with ExitStack() as dctx:
        def sbd(name, shape, dt=F32):
            return dctx.enter_context(nc.sbuf_tensor(name, shape, dt))
        big = [R, COLS, E]
        pr, pr2, ta, tb = (sbd(n, big) for n in ("probs", "probs_rest", "tmp_a", "tmp_b"))
        oh = [sbd("choice1", big), sbd("choice2", big)]
        both = sbd("both", big, BF16)
        red, m1, m2, top = (sbd(n, [R, COLS]) for n in ("red", "m1", "m2", "top"))
        nt, na, nb_ = sbd("n_tiles", [R, E]), sbd("tiles_a", [R, E]), sbd("tiles_b", [R, E])
        tile_cmp, tile_sum = sbd("tile_cmp", [1, TILES, E]), sbd("tile_sum", [1, TILES])
        rank, upto, valid, spare, tile_no = (sbd("rank", [R, E]), sbd("upto", [R, R]), sbd("valid", [R, COLS]),
                                             sbd("spare", [R, 2, COLS]), sbd("tile_no", [1, TILES]))
        upto_bf = sbd("upto_bf", [R, R], BF16)
        t_loaded, step, expo, counted, dests = sem("t_loaded"), sem("step"), sem("expo"), sem("counted"), sem("dests")
        experts_known = sem("experts_known")
        tables = [(rank[:, :], d.rank), (upto[:, :], d.upto), (valid[:, :], d.valid), (spare[:, :, :], d.spare),
                  (tile_no[:, :], d.tile_no)]

        with nc.Block() as block:
            @block.sync
            def _(sp):
                for dst, src in tables:
                    sp.dma_start(dst, src).then_inc(t_loaded, 16)
                for n, (dst, src) in enumerate(((eb1, b1_d), (eb2, b2_d))):
                    sp.dma_start(dst[:, :, :].rearrange("i e n -> i (e n)"), src).then_inc(eb_loaded, 16)
                for e in range(E):
                    sp.dma_start(ew1[:, e, :, :], d.W1[e].rearrange("(k p) n -> p k n", p=P)).then_inc(ew_loaded, 16)
                for e in range(E):
                    sp.dma_start(ew2[:, e, :, :], d.W2[e].rearrange("(k p) n -> p k n", p=P)).then_inc(ew_loaded, 16)

            @block.scalar
            def _(a):
                a.wait_ge(step, 2)
                a.activation(pr[:, :, :], pr[:, :, :], ACT.Exp).then_inc(expo, 1)

            @block.tensor
            def _(t):
                t.wait_ge(t_loaded, 16 * len(tables))
                t.wait_ge(counted, 1)
                flat = both[:, :, :].rearrange("p c e -> p (c e)")
                t.matmul(ps[0:R, 0, 0:COLS * E], upto_bf[:, :], flat, start=True, stop=True).then_inc(counted, 1)
                t.matmul(ps[0:R, 1, 0:COLS * E], ones_bf[0:R, 0:R], flat, start=True, stop=True).then_inc(counted, 1)

            @block.vector
            def _(v):
                count = [0]

                def did(instruction):
                    instruction.then_inc(step, 1)
                    count[0] += 1
                    v.wait_ge(step, count[0])

                def over_e(table):
                    return table[:, :].unsqueeze(2).broadcast_to(big)

                def over_c(table):
                    return table[:, :].unsqueeze(1).broadcast_to(big)

                did(v.tensor_reduce(m1[:, :], k.logits[:, :, :], AX.X, ALU.max))
                did(v.tensor_tensor(pr[:, :, :], k.logits[:, :, :], over_e(m1), ALU.subtract))
                v.wait_ge(expo, 1)
                did(v.tensor_reduce(red[:, :], pr[:, :, :], AX.X, ALU.add))
                did(v.reciprocal(red[:, :], red[:, :]))
                did(v.tensor_tensor(pr[:, :, :], pr[:, :, :], over_e(red), ALU.mult))
                v.wait_ge(t_loaded, 16 * len(tables))
                for n, (src, m) in enumerate(((pr, m1), (pr2, m2))):
                    did(v.tensor_reduce(m[:, :], src[:, :, :], AX.X, ALU.max))
                    did(v.tensor_tensor(ta[:, :, :], src[:, :, :], over_e(m), ALU.is_ge))
                    did(v.tensor_tensor(ta[:, :, :], ta[:, :, :], over_c(rank), ALU.mult))
                    did(v.tensor_reduce(top[:, :], ta[:, :, :], AX.X, ALU.max))
                    did(v.tensor_tensor(oh[n][:, :, :], ta[:, :, :], over_e(top), ALU.is_ge))
                    if n == 0:
                        did(v.scalar_tensor_tensor(pr2[:, :, :].rearrange("p c e -> p (c e)"),
                                                   oh[0][:, :, :].rearrange("p c e -> p (c e)"), -2.0,
                                                   pr[:, :, :].rearrange("p c e -> p (c e)"), ALU.mult, ALU.add))
                did(v.tensor_add(red[:, :], m1[:, :], m2[:, :]))
                did(v.tensor_scalar(red[:, :], red[:, :], 1e-9, None, ALU.max))
                did(v.reciprocal(red[:, :], red[:, :]))
                did(v.tensor_mul(w1[:, :], m1[:, :], red[:, :]))
                did(v.tensor_mul(w2[:, :], m2[:, :], red[:, :]))
                for n in range(2):
                    did(v.tensor_tensor(oh[n][:, :, :], oh[n][:, :, :], over_e(valid), ALU.mult))
                did(v.memset(ones_bf[:, :], 1.0))
                did(v.tensor_copy(upto_bf[:, :], upto[:, :]))
                did(v.tensor_add(ta[:, :, :], oh[0][:, :, :], oh[1][:, :, :]))
                v.tensor_copy(both[:, :, :], ta[:, :, :]).then_inc(counted, 1)
                v.wait_ge(counted, 3)
                did(v.tensor_copy(ta[:, :, :].rearrange("p c e -> p (c e)"), ps[0:R, 1, 0:COLS * E]))
                src, dst = ta, tb
                s = 1
                while s < COLS:
                    did(v.tensor_copy(dst[:, 0:s, :], src[:, 0:s, :]))
                    did(v.tensor_add(dst[:, s:, :], src[:, s:, :], src[:, 0:COLS - s, :]))
                    src, dst = dst, src
                    s *= 2
                did(v.tensor_scalar(nt[:, :], src[:, COLS - 1, :], 1.0 / P, (P - 1) / P - 0.5 + 0.5 / P,
                                    ALU.mult, ALU.add))
                did(v.tensor_scalar(nt[:, :], nt[:, :], MAGIC, None, ALU.add))
                did(v.tensor_scalar(nt[:, :], nt[:, :], MAGIC, None, ALU.subtract))
                did(v.tensor_copy(na[:, :], nt[:, :]))
                a_, b_ = na, nb_
                s = 1
                while s < E:
                    did(v.tensor_copy(b_[:, 0:s], a_[:, 0:s]))
                    did(v.tensor_add(b_[:, s:], a_[:, s:], a_[:, 0:E - s]))
                    a_, b_ = b_, a_
                    s *= 2
                did(v.tensor_tensor(tile_cmp[:, :, :], tile_no[:, :].unsqueeze(2).broadcast_to([1, TILES, E]),
                                    a_[0:1, :].unsqueeze(1).broadcast_to([1, TILES, E]), ALU.is_ge))
                did(v.tensor_reduce(tile_sum[:, :], tile_cmp[:, :, :], AX.X, ALU.add))
                v.tensor_scalar(tile_expert[:, :], tile_sum[:, :], float(E - 1), None, ALU.min)\
                    .then_inc(experts_known, 1)
                did(v.tensor_tensor(b_[:, :], a_[:, :], nt[:, :], ALU.subtract))
                did(v.tensor_scalar(b_[:, :], b_[:, :], float(P), None, ALU.mult))
                did(v.tensor_tensor(dst[:, :, :].rearrange("p c e -> p (c e)"),
                                    src[:, :, :].rearrange("p c e -> p (c e)"), ps[0:R, 1, 0:COLS * E], ALU.subtract))
                did(v.tensor_tensor(src[:, :, :].rearrange("p c e -> p (c e)"),
                                    dst[:, :, :].rearrange("p c e -> p (c e)"), ps[0:R, 0, 0:COLS * E], ALU.add))
                did(v.tensor_tensor(src[:, :, :], src[:, :, :], over_c(b_), ALU.add))
                for n in range(2):
                    did(v.tensor_tensor(dst[:, :, :], src[:, :, :], oh[n][:, :, :], ALU.mult))
                    did(v.tensor_reduce(red[:, :], dst[:, :, :], AX.X, ALU.add))
                    v.tensor_tensor(dest[n][:, :], red[:, :], spare[:, n, :], ALU.add).then_inc(dests, 1)
                    v.wait_ge(dests, n + 1)

            @block.gpsimd
            def _(g):
                for n in range(2):
                    g.wait_ge(dests, n + 1)
                    for i in range(COLS):
                        g.indirect_dma_start(xs_d, bass.IndirectOffsetOnAxis(ap=dest[n][:, i:i + 1], axis=0),
                                             k.xn[:, i, :], None).then_inc(scattered[n], 16)
                for n in range(2):
                    g.wait_ge(scattered[n], 16 * COLS)

    cs = []
    for s in range(2):
        c = Bag()
        c.s = s
        c.x, c.xt = sb(f"mx{s}", [P, D]), sb(f"mxt{s}", [P, 2, P])
        c.h, c.ht, c.o = sb(f"mh{s}", [P, EH]), sb(f"mht{s}", [P, EH]), sb(f"mo{s}", [P, D])
        c.x_in, c.x_turned, c.xt_ready = sem(f"x_in{s}"), sem(f"x_turned{s}"), sem(f"xt_ready{s}")
        c.h_mm, c.gelu, c.h_turned, c.ht_ready = sem(f"h_mm{s}"), sem(f"gelu{s}"), sem(f"h_turned{s}"), sem(f"ht_ready{s}")
        c.o_mm, c.o_ready, c.o_out = sem(f"o_mm{s}"), sem(f"o_ready{s}"), sem(f"o_out{s}")
        c.ps = ps[:, 4 * s:4 * s + 4, :]
        cs.append(c)
    N = TILES // 2
    with nc.Block() as block:
        @block.sync
        def _(sp):
            def load(c, it):
                sp.dma_start(c.x[:, :], xs_d[bass.ds(it * (2 * P) + c.s * P, P), :]).then_inc(c.x_in, 16)

            for c in cs:
                load(c, 0)

            def body(it, last):
                for c in cs:
                    if not last:
                        sp.wait_ge(c.x_turned, it + 1)
                        load(c, it + 1)
                for c in cs:
                    sp.wait_ge(c.o_ready, it + 1)
                    sp.dma_start(os_d[bass.ds(it * (2 * P) + c.s * P, P), :], c.o[:, :]).then_inc(c.o_out, 16)

            with sp.Fori(0, N - 1) as it:
                body(it, False)
            body(N - 1, True)
            for c in cs:
                sp.wait_ge(c.o_out, 16 * N)

        @block.tensor
        def _(t):
            t.wait_ge(ew_loaded, 16 * 2 * E)
            t.wait_ge(eb_loaded, 32)

            def body(it, first):
                experts_of = []
                for c in cs:
                    t.wait_ge(c.x_in, it * 16 + 16)
                    for f in range(2):
                        tr = t.transpose(c.ps[:, 0, P * f:P * f + P], c.x[:, P * f:P * f + P], k.ident[:, :])
                    tr.then_inc(c.x_turned, 1)
                for c in cs:
                    e = t.value_load(tile_expert[0:1, bass.ds(it * 2 + c.s, 1)], min_val=0, max_val=E - 1)
                    experts_of.append(e)
                    t.matmul(c.ps[:, 1, :], ones_bf[0:3, :], eb1[:, bass.ds(e, 1), :].rearrange("i o n -> i (o n)"),
                             start=True, stop=False)
                    t.wait_ge(c.xt_ready, it + 1)
                    for f in range(2):
                        mm = t.matmul(c.ps[:, 1, :], c.xt[:, f, :],
                                      ew1[:, bass.ds(e, 1), f, :].rearrange("p o n -> p (o n)"),
                                      start=False, stop=(f == 1))
                    mm.then_inc(c.h_mm, 1)
                for c in cs:
                    t.wait_ge(c.gelu, it + 1)
                    for f in range(4):
                        tr = t.transpose(c.ps[:, 2, P * f:P * f + P], c.h[:, P * f:P * f + P], k.ident[:, :])
                    tr.then_inc(c.h_turned, 1)
                for c, e in zip(cs, experts_of):
                    if not first:
                        t.wait_ge(c.o_ready, it)
                    t.matmul(c.ps[:, 3, 0:D], ones_bf[0:3, :], eb2[:, bass.ds(e, 1), :].rearrange("i o n -> i (o n)"),
                             start=True, stop=False)
                    t.wait_ge(c.ht_ready, it + 1)
                    for f in range(4):
                        mm = t.matmul(c.ps[:, 3, 0:D], c.ht[:, P * f:P * f + P],
                                      ew2[:, bass.ds(e, 1), f, :].rearrange("p o n -> p (o n)"),
                                      start=False, stop=(f == 3))
                    mm.then_inc(c.o_mm, 1)

            body(0, True)
            with t.Fori(1, N) as it:
                body(it, False)

        @block.scalar
        def _(a):
            with a.Fori(0, N) as it:
                for c in cs:
                    a.wait_ge(c.h_mm, it + 1)
                    a.activation(c.h[:, :], c.ps[:, 1, :], ACT.Gelu).then_inc(c.gelu, 1)

        @block.vector
        def _(v):
            def body(it, first):
                for c in cs:
                    v.wait_ge(c.x_turned, it + 1)
                    v.tensor_copy(c.xt[:, :, :].rearrange("p f n -> p (f n)"), c.ps[:, 0, 0:2 * P]).then_inc(c.xt_ready, 1)
                for c in cs:
                    v.wait_ge(c.h_turned, it + 1)
                    v.tensor_copy(c.ht[:, :], c.ps[:, 2, :]).then_inc(c.ht_ready, 1)
                for c in cs:
                    v.wait_ge(c.o_mm, it + 1)
                    if not first:
                        v.wait_ge(c.o_out, it * 16)
                    v.tensor_copy(c.o[:, :], c.ps[:, 3, 0:D]).then_inc(c.o_ready, 1)

            body(0, True)
            with v.Fori(1, N) as it:
                body(it, False)

    NBUF = 6
    ob = [[ew1[0:R, i, n, 0:D] for i in range(NBUF)] for n in range(2)]
    res = [ew1[0:R, i, 0, D:2 * D] for i in range(NBUF)]
    got = [sem(f"got{i}") for i in range(NBUF)]
    based = [sem(f"based{i}") for i in range(NBUF)]
    first_add, summed = sem("first_add"), sem("summed")
    stored = [sem(f"final{i}") for i in range(NBUF)]
    out_rows = out.rearrange("b t n -> (b t) n")
    with nc.Block() as block:
        @block.gpsimd
        def _(g):
            for i in range(COLS):
                b = i % NBUF
                if i >= NBUF:
                    g.wait_ge(summed, i - NBUF + 1)
                for n in range(2):
                    g.indirect_dma_start(ob[n][b], None, os_d,
                                         bass.IndirectOffsetOnAxis(ap=dest[n][:, i:i + 1], axis=0)).then_inc(got[b], 16)

        @block.sync
        def _(sp):
            for i in range(COLS):
                b = i % NBUF
                if i >= NBUF:
                    sp.wait_ge(stored[b], 16 * (i // NBUF))
                sp.dma_start(res[b], base_d[i]).then_inc(based[b], 16)

        @block.vector
        def _(v):
            for i in range(COLS):
                b = i % NBUF
                v.wait_ge(based[b], 16 * (i // NBUF + 1))
                v.wait_ge(got[b], 32 * (i // NBUF + 1))
                v.scalar_tensor_tensor(res[b], ob[0][b], w1[:, i:i + 1], res[b], ALU.mult, ALU.add)\
                    .then_inc(first_add, 1)
                v.wait_ge(first_add, i + 1)
                v.scalar_tensor_tensor(res[b], ob[1][b], w2[:, i:i + 1], res[b], ALU.mult, ALU.add)\
                    .then_inc(summed, 1)

        @block.scalar
        def _(a):
            for i in range(COLS):
                b = i % NBUF
                rows = R if i % J < J - 1 else NT - (J - 1) * R
                start = NT * (i // J) + R * (i % J)
                a.wait_ge(summed, i + 1)
                a.dma_start(out_rows[start:start + rows, :], res[b][0:rows, :]).then_inc(stored[b], 16)
            for b in range(NBUF):
                a.wait_ge(stored[b], 16 * len(range(b, COLS, NBUF)))



def shape_constants():
    f = np.float32
    t = {}
    t["ident"] = np.eye(P, dtype=f)
    y, x = np.meshgrid(np.arange(HP), np.arange(HP), indexing="ij")
    omega = (f(1.0) / f(10000.0) ** (np.arange(D // 4, dtype=f) / f(D // 4 - 1))).astype(f)
    ya = (y.reshape(-1)[:, None].astype(f) * omega[None]).astype(f)
    xa = (x.reshape(-1)[:, None].astype(f) * omega[None]).astype(f)
    pe = np.concatenate((np.sin(xa), np.cos(xa), np.sin(ya), np.cos(ya)), axis=1).astype(f)
    t["pos"] = np.ascontiguousarray(pe[np.arange(NPB) % NP].reshape(J, RP, D).transpose(1, 0, 2))
    theta = (f(1.0) / f(10000.0) ** (f(2.0) * np.arange(DH // 2, dtype=f) / f(DH))).astype(f)
    ang = (np.arange(T, dtype=f)[None, :] * theta[(np.arange(P) % DH) // 2][:, None]).astype(f)
    t["cos"], t["sin"] = np.cos(ang).astype(f), np.sin(ang).astype(f)
    rot = np.zeros((P, P), f)
    for i in range(0, P, 2):
        rot[i + 1, i], rot[i, i + 1] = -1.0, 1.0
    t["rot"] = rot
    hm = np.zeros((P, QH), f)
    hm[np.arange(P), (np.arange(P) // DH) % QH] = 1.0
    t["head_mask"] = hm
    vm = np.zeros((GK, H), f)
    for h in range(H):
        r = h % GH if h < GH * (G - 1) else GH - 1
        vm[T * r:T * (r + 1), h] = 1.0
    t["value_mask"] = vm
    causal = np.zeros((P, H, T), f)
    for o in (0, 64):
        q, s = np.arange(T)[:, None], np.arange(T)[None]
        causal[o:o + T] = np.where(s <= q, 0.0, -1e10).astype(f)[:, None, :]
    t["causal"] = causal.reshape(P, HT)
    t["rank"] = np.ascontiguousarray(np.broadcast_to((E - np.arange(E)).astype(f)[None], (R, E)))
    t["upto"] = np.triu(np.ones((R, R), f), 1)
    valid = np.ones((R, COLS), f)
    valid[NT - (J - 1) * R:, J - 1::J] = 0.0
    t["valid"] = valid
    spare = np.zeros((R, 2, COLS), f)
    for n in range(2):
        spare[:, n, :] = (1.0 - valid) * (SLOTS + n * COLS + np.arange(COLS))
    t["spare"] = spare
    t["tile_no"] = np.arange(TILES, dtype=f)[None]
    return t


def kernel(**inputs):
    import concourse.bacc as bacc
    from concourse.bass_utils import run_bass_kernel_spmd

    a = {n: np.asarray(v) for n, v in inputs.items()}
    nc = bacc.Bacc("TRN2", target_bir_lowering=False, num_devices=1)
    arrays = {}

    def give(name, array):
        array = np.ascontiguousarray(array)
        name = "in_" + name
        arrays[name] = array
        return nc.dram_tensor(name, array.shape, mybir.dt.from_np(array.dtype), kind="ExternalInput").ap()

    def columns(v, n):
        return v.reshape(n, P).T

    d, t = Bag(), shape_constants()
    d.ident, d.pos, d.cos, d.sin, d.rot = (give(n, t[n]) for n in ("ident", "pos", "cos", "sin", "rot"))
    d.head_mask, d.value_mask, d.causal = (give(n, t[n]) for n in ("head_mask", "value_mask", "causal"))
    d.rank, d.upto, d.valid, d.spare, d.tile_no = (give(n, t[n]) for n in ("rank", "upto", "valid", "spare", "tile_no"))
    x = a["x"].reshape(B, C, HP, PATCH, HP, PATCH)
    d.x = give("x", x.transpose(3, 5, 1, 0, 2, 4).reshape(FP, B * NP))
    d.cls, d.cls_pos = give("cls", a["L0_tok_cls_token"].reshape(D)), give("cls_pos", a["L0_tok_cls_pos_embedding"].reshape(D))
    d.ln1_g, d.ln1_b = give("ln1_g", columns(a["L0_tok_ln1_g"], KF)), give("ln1_b", columns(a["L0_tok_ln1_b"], KF))
    d.W, d.tok_bias = give("W", a["L0_tok_W"]), give("tok_bias", a["L0_tok_bias"])
    d.ln2_g, d.ln2_b = give("ln2_g", a["L0_tok_ln2_g"]), give("ln2_b", a["L0_tok_ln2_b"])
    d.attn_w = [[give(f"L0_{n}", a[f"L0_attn_{n}"].T) for n in ("wq", "wk", "wv", "wp")],
                [give(f"L1_{n}", a[f"L1_attn_{n}"]) for n in ("Wq", "Wk", "Wv", "Wo")]]
    d.attn_b = [[give(f"L{l}_b{n}", columns(a[f"L{l}_attn_b{n}"], 2)) for n in "qkv"] for l in range(2)]
    d.attn_ob = [give("L0_bp", a["L0_attn_bp"]), give("L1_bo", a["L1_attn_bo"])]
    d.w1T, d.w2T = give("w1T", a["L0_ffn_w1"].T), give("w2T", a["L0_ffn_w2"].T)
    conv = np.concatenate((a["L0_ffn_conv_w"].reshape(FH, 3), a["L0_ffn_conv_b"].reshape(FH, 1)), axis=1)
    d.conv = give("conv", conv.reshape(MH, P, 4).transpose(1, 0, 2))
    d.relT = give("relT", a["L1_attn_rel_bias"].T)
    d.Wr, d.br = give("Wr", a["L1_ffn_Wr"]), give("br", a["L1_ffn_br"])
    d.W1, d.b1, d.W2, d.b2 = (give(n, a[f"L1_ffn_{n}"]) for n in ("W1", "b1", "W2", "b2"))
    out = nc.dram_tensor("out", (B, T, D), F32, kind="ExternalOutput").ap()
    build(nc, d, out)
    r = run_bass_kernel_spmd(nc, [arrays], core_ids=[0])
    return r.results[0]["out"]
```

```python
from contextlib import ExitStack

import numpy as np
import concourse.bass as bass
from concourse import mybir

F32 = mybir.dt.float32
BF16 = mybir.dt.bfloat16
U32 = mybir.dt.uint32
I32 = mybir.dt.int32
ALU = mybir.AluOpType
ACT = mybir.ActivationFunctionType
AX = mybir.AxisListType

P = 128
B, C, IMG, PATCH = 64, 3, 96, 16
HP = IMG // PATCH
NP = HP * HP
T = NP + 1
D = 256
FP = C * PATCH * PATCH
KF = FP // P
H, DH = 16, 16
QH = 64 // DH
FH = 1024
MH = FH // P
E, EH = 16, 512
EPS = 1e-5
MAGIC = 1.5 * 2.0 ** 23

NI = 8
NB = B // NI
CTX = 2
ITERS = NB // CTX
NT = NI * T
J = 3
R = (NT + J - 1) // J
NTP = J * R
NPB = NI * NP
RP = NPB // J
NPAIR = NI // 2
HT = H * T
GH = 3
G = 6
GK = GH * T
PR = 64 + T
Y0 = 2 * PR
DV = DH + 1
COLS = NB * J
PAIRS = 2 * B * T
TILES = (PAIRS + E * (P - 1)) // P
SLOTS = TILES * P
NROWS = SLOTS + P
XW = D + 2


class Bag:
    pass


def phase(nc, fn, *args):
    with ExitStack() as c:
        used = []

        def sem(name):
            used.append(c.enter_context(nc.semaphore(name)))
            return used[-1]
        fn(nc, c, sem, *args)
        numbers = sorted(s.num for s in used)
        with nc.Block() as block:
            @block.gpsimd
            def _(g):
                start = 0
                for i in range(1, len(numbers) + 1):
                    if i == len(numbers) or numbers[i] != numbers[i - 1] + 1:
                        g.sem_clear(range(numbers[start], numbers[i - 1] + 1))
                        start = i


def group_col(g):
    return GK * g if g < G - 1 else HT - GK


def build(nc, d, out):
    h0 = nc.dram_tensor("tokens_d", (B * T + P, D), F32, kind="Internal").ap()
    base_d = nc.dram_tensor("base_d", (COLS, R, D), F32, kind="Internal").ap()
    xs_d = nc.dram_tensor("xs_d", (NROWS, XW), F32, kind="Internal").ap()
    weighted_d = nc.dram_tensor("weighted_d", (2 * COLS * R + 2 * P, D), F32, kind="Internal").ap()
    b1_d = nc.dram_tensor("b1_d", (3, E * EH), BF16, kind="Internal").ap()
    b2_d = nc.dram_tensor("b2_d", (3, E * D), BF16, kind="Internal").ap()
    with ExitStack() as ctx:
        def sb(name, shape, dt=F32):
            return ctx.enter_context(nc.sbuf_tensor(name, shape, dt))
        k = Bag()
        k.ident = sb("ident", [P, P])
        k.ident_bf = sb("ident_bf", [P, P], BF16)
        k.ones = sb("ones", [P, P])
        k.xn = sb("xn", [R, COLS, XW])
        k.logits = sb("logits", [R, COLS, E])
        k.ps = ctx.enter_context(nc.psum_tensor("ps", [P, 8, 512], F32))
        with ExitStack() as tower_ctx:
            def sbt(name, shape, dt=F32):
                return tower_ctx.enter_context(nc.sbuf_tensor(name, shape, dt))
            k.half = sbt("half", [P, J])
            k.attn = []
            for l in range(2):
                a = Bag()
                a.w = sbt(f"attn_w{l}", [P, 4, 2, D])
                a.qb, a.kb, a.vb = (sbt(f"attn_{n}b{l}", [P, 2]) for n in "qkv")
                a.ob = sbt(f"attn_ob{l}", [P, D])
                a.bias = sbt(f"score_bias{l}", [P, HT])
                k.attn.append(a)
            k.rot = sbt("rot", [P, P])
            k.cos, k.sin = sbt("cos", [P, T]), sbt("sin", [P, T])
            k.head_mask = sbt("head_mask", [P, QH])
            k.value_mask = sbt("value_mask", [GK, H])
            k.w1 = sbt("w1", [P, 2, FH], BF16)
            k.w2 = sbt("w2", [P, MH, D], BF16)
            k.wunit = sbt("wunit", [P, 2])
            k.conv = sbt("conv", [P, MH, 4])
            k.wr = sbt("wr", [P, 2, E])
            k.br = sbt("br", [P, E])
            phase(nc, setup_embed, d, k, h0, xs_d, weighted_d, b1_d, b2_d)
            phase(nc, tower, k, h0, base_d)
        phase(nc, experts, d, k, base_d, xs_d, weighted_d, b1_d, b2_d, out)



def setup_embed(nc, ctx, sem, d, k, h0, xs_d, weighted_d, b1_d, b2_d):
    def sb(name, shape, dt=F32):
        return ctx.enter_context(nc.sbuf_tensor(name, shape, dt))

    wp = sb("wp", [P, KF, D])
    wc = sb("wc", [P, KF, D + 1])
    g1, b1 = sb("g1", [P, KF]), sb("b1", [P, KF])
    mean_w = sb("mean_w", [P, P])
    bias_row = sb("bias_row", [1, D])
    out_bias = sb("out_bias", [RP, D])
    g2, b2, pos = sb("g2", [RP, D]), sb("b2", [RP, D]), sb("pos", [RP, J, D])
    cls, cls_pos = sb("cls", [B, D]), sb("cls_pos", [B, D])
    zero, filler = sb("zero", [P, D]), sb("filler", [P, 2, XW])
    rel_rev = sb("rel_rev", [P, H, T])
    wt = [sb("w1_raw", [P, 2 * FH]), sb("w2_raw", [P, MH * D])]
    wq = [sb("w1_round", [P, 2 * FH]), sb("w2_round", [P, MH * D])]
    wsum, wscale = sb("wsum", [P, 2]), sb("wscale", [P, 2])
    eb = [sb("eb1", [E, EH]), sb("eb2", [E, D])]
    ebr = [sb("eb1_rest", [E, EH]), sb("eb2_rest", [E, D])]
    ebp = [[sb(f"eb{n + 1}_part{i}", [E, (EH, D)[n]], BF16) for i in range(3)] for n in range(2)]

    loads = [
        (k.ident[:, :], d.ident), (filler[:, :, :], d.filler), (wp[:, :, :], d.W.rearrange("(k p) n -> p k n", p=P)),
        (g1[:, :], d.ln1_g), (b1[:, :], d.ln1_b), (bias_row[:, :], d.tok_bias.unsqueeze(0)),
        (g2[:, :], d.ln2_g.unsqueeze(0).broadcast_to([RP, D])), (b2[:, :], d.ln2_b.unsqueeze(0).broadcast_to([RP, D])),
        (pos[:, :, :], d.pos), (cls[:, :], d.cls.unsqueeze(0).broadcast_to([B, D])),
        (cls_pos[:, :], d.cls_pos.unsqueeze(0).broadcast_to([B, D])),
        (wt[0][:, :].rearrange("p (k n) -> p k n", k=2), d.w1T.rearrange("(k p) n -> p k n", p=P)),
        (wt[1][:, :].rearrange("p (k n) -> p k n", k=MH), d.w2T.rearrange("(k p) n -> p k n", p=P)),
        (k.rot[:, :], d.rot), (k.cos[:, :], d.cos), (k.sin[:, :], d.sin), (k.head_mask[:, :], d.head_mask),
        (k.value_mask[:, :], d.value_mask), (k.conv[:, :, :], d.conv),
        (k.wr[:, :, :], d.Wr.rearrange("(k p) n -> p k n", p=P)), (k.br[:, :], d.br.unsqueeze(0).broadcast_to([P, E])),
        (k.attn[0].bias[:, :], d.causal), (eb[0][:, :], d.b1), (eb[1][:, :], d.b2),
    ]
    for l in range(2):
        for n in range(4):
            loads.append((k.attn[l].w[:, n, :, :], d.attn_w[l][n].rearrange("(k p) n -> p k n", p=P)))
        for dst, src in zip((k.attn[l].qb, k.attn[l].kb, k.attn[l].vb), d.attn_b[l]):
            loads.append((dst[:, :], src))
        loads.append((k.attn[l].ob[:, :], d.attn_ob[l].unsqueeze(0).broadcast_to([P, D])))

    loaded, rel_loaded, filled = sem("loaded"), sem("rel_loaded"), sem("filled")
    const_set, rel_clear = sem("const_set"), sem("rel_clear")
    gained, mean_mm, centred, bias_mm = sem("gained"), sem("mean_mm"), sem("centred"), sem("bias_mm")
    pos_done, cls_done, rel_done = sem("pos_done"), sem("cls_done"), sem("rel_done")
    wsum_done, wsum_mm, wq_step = sem("wsum_done"), sem("wsum_mm"), sem("wq_step")
    split, split_out = sem("split"), sem("split_out")
    q_scaled = sem("q_scaled")

    with nc.Block() as block:
        @block.sync
        def _(sp):
            for dst, src in loads:
                sp.dma_start(dst, src).then_inc(loaded, 16)
            sp.wait_ge(rel_clear, 1)
            rel = bass.AP(d.relT.tensor, 128 - (T - 1), [[1, T], [2 * 128 + 1, H], [1, T]])
            for o in (0, 64):
                sp.dma_start(rel_rev[o:o + T, :, :], rel).then_inc(rel_loaded, 16)
            sp.wait_ge(loaded, 16 * len(loads))
            sp.wait_ge(const_set, 5)
            sp.dma_start(h0[B * T:B * T + P, :], zero[:, :]).then_inc(filled, 16)
            for s in range(2):
                sp.dma_start(xs_d[0:SLOTS, :].rearrange("(a s p) n -> p s a n", s=2, p=P)[:, s, :, :],
                             filler[:, s:s + 1, :].broadcast_to([P, TILES // 2, XW])).then_inc(filled, 16)
            sp.dma_start(xs_d[SLOTS:NROWS, :], filler[:, 0, :]).then_inc(filled, 16)
            sp.dma_start(weighted_d[0:2 * COLS * R, :].rearrange("(a b) n -> a b n", b=J * R)[:, J * R - 1, :],
                         zero[0:2 * NB, :]).then_inc(filled, 16)
            sp.wait_ge(cls_done, 1)
            sp.dma_start(h0[0:B * T, :].rearrange("(b t) n -> b t n", t=T)[:, 0, :], cls[:, :]).then_inc(filled, 16)
            for n, dst in enumerate((b1_d, b2_d)):
                for i in range(3):
                    sp.wait_ge(split, 5 * n + (1, 3, 5)[i])
                    sp.dma_start(dst[i, :].rearrange("(e n) -> e n", e=E), ebp[n][i][:, :]).then_inc(split_out, 16)
            sp.wait_ge(filled, 16 * 6)
            sp.wait_ge(split_out, 16 * 6)

        @block.gpsimd
        def _(g):
            g.memset(rel_rev[:, :, :], 0.0).then_inc(rel_clear, 1)
            g.memset(k.ones[:, :], 1.0).then_inc(const_set, 1)
            g.memset(mean_w[:, :], 1.0 / FP).then_inc(const_set, 1)
            g.memset(zero[:, :], 0.0).then_inc(const_set, 1)
            g.memset(k.half[:, :], -0.5).then_inc(const_set, 1)
            g.wait_ge(rel_loaded, 32)
            rr = rel_rev[:, :, :]
            back = bass.AP(rr.tensor, T - 1, [list(rr.ap[0]), [T, H], [-1, T]])
            g.tensor_copy(k.attn[1].bias[:, :].rearrange("p (h t) -> p h t", h=H), back).then_inc(rel_done, 1)

        @block.vector
        def _(v):
            v.wait_ge(loaded, 16 * len(loads))
            v.tensor_copy(k.ident_bf[:, :], k.ident[:, :]).then_inc(const_set, 1)
            for i in range(KF):
                v.tensor_scalar(wc[:, i, 0:D], wp[:, i, :], g1[:, i:i + 1], None, ALU.mult).then_inc(gained, 1)
            v.memset(wc[:, :, D:D + 1], 1.0).then_inc(gained, 1)
            v.tensor_add(cls[:, :], cls[:, :], cls_pos[:, :]).then_inc(cls_done, 1)
            v.tensor_tensor(pos[:, :, :], pos[:, :, :], b2[:, :].unsqueeze(1).broadcast_to([RP, J, D]), ALU.add)\
                .then_inc(pos_done, 1)
            for n in range(2):
                v.tensor_reduce(wsum[:, n:n + 1], wt[n][:, :], AX.X, ALU.add, apply_absolute_value=True)\
                    .then_inc(wsum_done, 1)
            v.wait_ge(mean_mm, 1)
            v.tensor_tensor(wc[:, :, 0:D], wc[:, :, 0:D], k.ps[:, 0, 0:D].unsqueeze(1).broadcast_to([P, KF, D]),
                            ALU.subtract).then_inc(centred, 1)
            v.wait_ge(bias_mm, 1)
            v.tensor_copy(out_bias[:, :], k.ps[0:RP, 1, 0:D]).then_inc(centred, 1)
            v.wait_ge(wsum_mm, 1)
            v.tensor_scalar(wsum[:, :], k.ps[:, 2, 0:2], 1.0 / (D * FH), 1e-5, ALU.mult, ALU.max).then_inc(wq_step, 1)
            v.wait_ge(wq_step, 1)
            v.reciprocal(wscale[:, :], wsum[:, :]).then_inc(wq_step, 1)
            v.wait_ge(wq_step, 2)
            v.reciprocal(k.wunit[:, :], wscale[:, :]).then_inc(wq_step, 1)
            for n, dst in enumerate((k.w1[:, :, :], k.w2[:, :, :])):
                v.tensor_scalar(wq[n][:, :], wt[n][:, :], wscale[:, n:n + 1], MAGIC, ALU.mult, ALU.add)\
                    .then_inc(wq_step, 1)
                v.wait_ge(wq_step, 4 + 3 * n)
                v.tensor_scalar(wq[n][:, :], wq[n][:, :], MAGIC, -1.0, ALU.subtract, ALU.max).then_inc(wq_step, 1)
                v.wait_ge(wq_step, 5 + 3 * n)
                v.tensor_scalar(dst.rearrange("p k n -> p (k n)"), wq[n][:, :], 1.0, None, ALU.min)\
                    .then_inc(wq_step, 1)
            for n in range(2):
                v.tensor_copy(ebp[n][0][:, :], eb[n][:, :]).then_inc(split, 1)
                v.wait_ge(split, 5 * n + 1)
                v.tensor_tensor(ebr[n][:, :], eb[n][:, :], ebp[n][0][:, :], ALU.subtract).then_inc(split, 1)
                v.wait_ge(split, 5 * n + 2)
                v.tensor_copy(ebp[n][1][:, :], ebr[n][:, :]).then_inc(split, 1)
                v.wait_ge(split, 5 * n + 3)
                v.tensor_tensor(ebr[n][:, :], ebr[n][:, :], ebp[n][1][:, :], ALU.subtract).then_inc(split, 1)
                v.wait_ge(split, 5 * n + 4)
                v.tensor_copy(ebp[n][2][:, :], ebr[n][:, :]).then_inc(split, 1)

        @block.scalar
        def _(a):
            a.wait_ge(loaded, 16 * len(loads))
            for l in range(2):
                a.mul(k.attn[l].qb[:, :], k.attn[l].qb[:, :], DH ** -0.5).then_inc(q_scaled, 1)

        @block.tensor
        def _(t):
            t.wait_ge(const_set, 5)
            t.wait_ge(loaded, 16 * len(loads))
            t.wait_ge(gained, KF)
            for i in range(KF):
                mm = t.matmul(k.ps[:, 0, 0:D], mean_w[:, :], wc[:, i, 0:D], start=(i == 0), stop=(i == KF - 1))
            mm.then_inc(mean_mm, 1)
            for i in range(KF):
                t.matmul(k.ps[0:RP, 1, 0:D], b1[:, i:i + 1].broadcast_to([P, RP]), wp[:, i, :],
                         start=(i == 0), stop=False)
            t.matmul(k.ps[0:RP, 1, 0:D], k.ones[0:1, 0:RP], bias_row[:, :], start=False, stop=True)\
                .then_inc(bias_mm, 1)
            t.wait_ge(wsum_done, 2)
            t.matmul(k.ps[:, 2, 0:2], k.ones[:, :], wsum[:, :], start=True, stop=True).then_inc(wsum_mm, 1)

    cs = []
    for s in range(CTX):
        c = Bag()
        c.s = s
        c.x = sb(f"x{s}", [P, KF, NPB])
        c.xx = sb(f"xx{s}", [P, KF, NPB])
        c.z = sb(f"z{s}", [RP, J, D])
        c.tok = sb(f"tok{s}", [RP, J, D])
        c.mean, c.var, c.rstd = (sb(f"{n}{s}", [RP, J]) for n in ("e_mean", "e_var", "e_rstd"))
        c.st, c.mv = sb(f"e_st{s}", [RP, J, 6]), sb(f"e_mv{s}", [RP, J, 2])
        c.x_loaded, c.squared, c.prod_mm = sem(f"x_loaded{s}"), sem(f"squared{s}"), sem(f"prod_mm{s}")
        c.norm, c.powers, c.stored = sem(f"e_norm{s}"), sem(f"e_powers{s}"), sem(f"stored{s}")
        c.z_done, c.tok_done = sem(f"z_done{s}"), sem(f"tok_done{s}")
        cs.append(c)
    ps = k.ps
    NORM = 9
    PIECES = 10

    def pieces(j):
        r, end = RP * j, RP * (j + 1)
        while r < end:
            n = min(end, (r // NP + 1) * NP) - r
            yield r - RP * j, n, r // NP, r % NP
            r += n

    with nc.Block() as block:
        @block.sync
        def _(sp):
            def load(c, it):
                sp.dma_start(c.x[:, :, :], d.x[:, bass.ds(it * (CTX * NPB) + c.s * NPB, NPB)]
                             .rearrange("(k p) n -> p k n", p=P)).then_inc(c.x_loaded, 16)

            for c in cs:
                load(c, 0)

            def body(it, last):
                for c in cs:
                    if not last:
                        sp.wait_ge(c.prod_mm, it + 1)
                        load(c, it + 1)
                for c in cs:
                    sp.wait_ge(c.tok_done, it + 1)
                    for j in range(J):
                        for row, n, img, s in pieces(j):
                            sp.dma_start(h0[bass.ds(it * (CTX * NI * T) + ((c.s * NI + img) * T + 1 + s), n), :],
                                         c.tok[row:row + n, j, :]).then_inc(c.stored, 16)

            with sp.Fori(0, ITERS - 1) as it:
                body(it, False)
            body(ITERS - 1, True)
            for c in cs:
                sp.wait_ge(c.stored, 16 * PIECES * ITERS)

        @block.scalar
        def _(a):
            with a.Fori(0, ITERS) as it:
                for c in cs:
                    a.wait_ge(c.x_loaded, it * 16 + 16)
                    for i in range(KF):
                        a.activation(c.xx[:, i, :], c.x[:, i, :], ACT.Square).then_inc(c.squared, 1)

        @block.tensor
        def _(t):
            def body(it, first):
                for c in cs:
                    t.wait_ge(c.x_loaded, it * 16 + 16)
                    if not first:
                        t.wait_ge(c.z_done, it)
                    for j in range(J):
                        for i in range(KF):
                            t.matmul(ps[0:RP, 4 * c.s + j, 0:D + 1], c.x[:, i, RP * j:RP * j + RP], wc[:, i, :],
                                     start=(i == 0), stop=(i == KF - 1))
                    t.wait_ge(c.squared, it * KF + KF)
                    for j in range(J):
                        for i in range(KF):
                            mm = t.matmul(ps[0:RP, 4 * c.s + 3, j:j + 1], c.xx[:, i, RP * j:RP * j + RP],
                                          k.ones[:, 0:1], start=(i == 0), stop=(i == KF - 1))
                    mm.then_inc(c.prod_mm, 1)

            body(0, True)
            with t.Fori(1, ITERS) as it:
                body(it, False)

        @block.gpsimd
        def _(g):
            def body(it, first):
                for c in cs:
                    g.wait_ge(c.norm, it * NORM + 4)
                    g.tensor_tensor(c.rstd[:, :], c.var[:, :], k.half[0:RP, :], ALU.pow).then_inc(c.powers, 1)
                for c in cs:
                    g.wait_ge(c.norm, it * NORM + 7)
                    g.tensor_tensor(c.rstd[:, :], c.var[:, :], k.half[0:RP, :], ALU.pow).then_inc(c.powers, 1)
                for c in cs:
                    g.wait_ge(c.norm, it * NORM + 9)
                    if not first:
                        g.wait_ge(c.stored, it * (16 * PIECES))
                    g.tensor_tensor(c.tok[:, :, :], c.z[:, :, :], pos[:, :, :], ALU.add).then_inc(c.tok_done, 1)

            body(0, True)
            with g.Fori(1, ITERS) as it:
                body(it, False)

        @block.vector
        def _(v):
            def body(it, first):
                for c in cs:
                    sums = ps[0:RP, 4 * c.s:4 * c.s + J, D:D + 1].rearrange("p j o -> p (j o)")
                    squares = ps[0:RP, 4 * c.s + 3, 0:J]
                    v.wait_ge(c.prod_mm, it + 1)
                    v.tensor_scalar(c.mean[:, :], sums, 1.0 / FP, None, ALU.mult).then_inc(c.norm, 1)
                    v.wait_ge(c.norm, it * NORM + 1)
                    v.scalar_tensor_tensor(c.mean[:, :], c.mean[:, :], -1.0, c.mean[:, :], ALU.mult, ALU.mult)\
                        .then_inc(c.norm, 1)
                    v.wait_ge(c.norm, it * NORM + 2)
                    v.scalar_tensor_tensor(c.var[:, :], squares, 1.0 / FP, c.mean[:, :], ALU.mult, ALU.add)\
                        .then_inc(c.norm, 1)
                    v.wait_ge(c.norm, it * NORM + 3)
                    v.tensor_scalar(c.var[:, :], c.var[:, :], EPS, None, ALU.add).then_inc(c.norm, 1)
                for c in cs:
                    v.wait_ge(c.powers, it * 2 + 1)
                    if not first:
                        v.wait_ge(c.tok_done, it)
                    for j in range(J):
                        zj = v.scalar_tensor_tensor(c.z[:, j, :], ps[0:RP, 4 * c.s + j, 0:D], c.rstd[:, j:j + 1],
                                                    out_bias[:, :], ALU.mult, ALU.add)
                    zj.then_inc(c.z_done, 1)
                    v.wait_ge(c.z_done, it + 1)
                    for j in range(J):
                        st = v.bn_stats(c.st[:, j, :], c.z[:, j, :])
                    st.then_inc(c.norm, 1)
                    v.wait_ge(c.norm, it * NORM + 5)
                    v.nop(nofuse=True)
                    for j in range(J):
                        mv = v.bn_aggr(c.mv[:, j, :], c.st[:, j, :])
                    mv.then_inc(c.norm, 1)
                    v.wait_ge(c.norm, it * NORM + 6)
                    v.tensor_scalar(c.var[:, :], c.mv[:, :, 1:2].rearrange("p j o -> p (j o)"), EPS, None, ALU.add)\
                        .then_inc(c.norm, 1)
                for c in cs:
                    v.wait_ge(c.powers, it * 2 + 2)
                    for j in range(J):
                        zj = v.tensor_scalar(c.z[:, j, :], c.z[:, j, :], c.mv[:, j, 0:1], c.rstd[:, j:j + 1],
                                             ALU.subtract, ALU.mult)
                    zj.then_inc(c.norm, 1)
                    v.wait_ge(c.norm, it * NORM + 8)
                    v.tensor_tensor(c.z[:, :, :], c.z[:, :, :], g2[:, :].unsqueeze(1).broadcast_to([RP, J, D]), ALU.mult)\
                        .then_inc(c.norm, 1)

            body(0, True)
            with v.Fori(1, ITERS) as it:
                body(it, False)



def tower(nc, ctx, sem, k, h0, base_d):
    def sb(name, shape, dt=F32):
        return ctx.enter_context(nc.sbuf_tensor("t_" + name, shape, dt))

    SIGNALS = dict(
        h_loaded=16, base_stored=16,
        ln=16,
        ln_power=4, xt_mm=3, xt=3,
        qk_mm=8, q0=4, rope_mm=4, rope_cos=4, rope_sin=4, rope_sum=4, q1=4, keys=4,
        v_mm=4, v_ev=4, vt_mm=8, values=8,
        score_mm=8, biased=8, row_max=8, shifted=8, prob=8, probt_mm=8, probt=8, pv_mm=8, inv_sum=8, y=8,
        yt_mm=8, yt=8, proj_mm=2, h_bias=2, h_attn=2,
        quant=7,
        xq_mm=1, xq=1, unit_mm=1, unit=1, hid_mm=8, hid=8, mid=8, left=8, right=8, silu=8, pad=1,
        hidt_mm=3, quant2=24,
        hq_mm=3, hq=3, out_mm=3, h_ffn=3,
        logit_mm=1, logit=1, xn_kept=1, base=1)
    assert 2 * len(SIGNALS) < 200

    cs = []
    for s in range(CTX):
        c = Bag()
        c.s, c.sem = s, {n: sem(f"{n}_{s}") for n in SIGNALS}
        c.ps = k.ps[:, 4 * s:4 * s + 4, :]
        c.h, c.hb, c.xh, c.qf = (sb(f"{n}{s}", [R, J, D]) for n in ("h", "hb", "xh", "qf"))
        c.h_in = sb(f"h_in{s}", [R, J, D])
        c.base = c.qf
        c.st, c.mv = sb(f"st{s}", [R, J, 6]), sb(f"mv{s}", [R, J, 2])
        c.var, c.rstd = sb(f"var{s}", [R, J]), sb(f"rstd{s}", [R, J])
        c.xt = sb(f"xt{s}", [P, 2, NTP])
        c.qt = sb(f"qt{s}", [P, 2, NT])
        c.v = sb(f"v{s}", [GK, NI, H, DV])
        c.sc2 = sb(f"sc{s}", [P, 2, HT])
        c.mx2, c.rs = sb(f"mx{s}", [P, 2, H]), sb(f"rs{s}", [P, H])
        c.pt = sb(f"pt{s}", [GK, G, PR])
        c.y = sb(f"y{s}", [P, D])
        c.yt = sb(f"yt{s}", [P, 2, NTP])
        c.qb = sb(f"qb{s}", [R, J, D], BF16)
        c.am, c.unit_in = sb(f"am{s}", [R, J]), sb(f"unit_in{s}", [R, J])
        c.am2, c.unit2 = sb(f"am2{s}", [R, 1]), sb(f"unit2{s}", [R, J])
        words = max(4 * NT * 3 + 2 * NI * GK + 2 * NI * QH * T,
                    2 * MH * NTP + FH + FH // 2 + MH * NTP // 2 + NTP + NTP)
        region = sb(f"region{s}", [P, words])
        at = [0]

        def take(n, pattern=None, dt=F32, **dims):
            a = region[:, at[0]:at[0] + n]
            at[0] += n
            if dt != F32:
                a = a.bitcast(dt)
            return a.rearrange(pattern, **dims) if pattern else a

        c.qk = take(4 * NT, "p (i t) -> p i t", i=4)
        c.rc = take(4 * NT, "p (i t) -> p i t", i=4)
        c.rn = take(4 * NT, "p (i t) -> p i t", i=4)
        c.vr = take(2 * NI * GK, "p (f i r t) -> p f i r t", f=2, i=NI, r=GH)
        c.kd = take(2 * NI * QH * T, "p (f i o t) -> p f i o t", f=2, i=NI, o=QH)
        at[0] = 0
        c.t0 = take(MH * NTP, "p (m t) -> p m t", m=MH)
        c.a = take(MH * NTP, "p (m t) -> p m t", m=MH)
        c.qf2 = take(FH)
        c.qb2 = take(FH // 2, dt=BF16)
        c.hq = take(MH * NTP // 2, "p (m t) -> p m t", dt=BF16, m=MH)
        c.xq = take(NTP, "p (f t) -> p f t", dt=BF16, f=2)
        c.unit = take(NTP)
        cs.append(c)

    def wait(eng, c, it, name, n):
        eng.wait_ge(c.sem[name], it * SIGNALS[name] + n)

    images = "p (i t) -> p i t"
    img_bc = lambda table: table[:, :].unsqueeze(1).broadcast_to([P, NI, T])
    bft = lambda bank: bank.bitcast(BF16)

    LENGTH = dict(project0=30.0, attend0=38.0, ffn=50.0, project1=27.3, attend1=42.4)
    STAGES = tuple(LENGTH)

    def run(eng, stage):
        def stages(c, todo, start=0.0):
            for name, it in todo:
                for point in stage(name, c, it):
                    yield start + LENGTH[name] * point
                start += LENGTH[name]

        def together(*steps):
            steps = list(steps)
            due = [next(g) for g in steps]
            while steps:
                n = due.index(min(due))
                time = next(steps[n], None)
                if time is None:
                    steps.pop(n)
                    due.pop(n)
                else:
                    due[n] = time

        first, last = STAGES[0], STAGES[-1]
        together(stages(cs[0], [(n, 0) for n in STAGES]),
                 stages(cs[1], [(n, 0) for n in STAGES[:-1]], LENGTH[first]))
        with eng.Fori(1, ITERS) as it:
            together(stages(cs[0], [(n, it) for n in STAGES]),
                     stages(cs[1], [(last, it - 1)] + [(n, it) for n in STAGES[:-1]]))
        together(stages(cs[1], [(last, ITERS - 1)]))

    PAIR_SPAN = NPAIR + 2.5

    def sync_program(sp):
        def load(c, it):
            row = it * (CTX * NT) + c.s * NT
            sp.dma_start(c.h_in[:, :, :], h0[bass.ds(row, NTP), :].rearrange("(j p) n -> p j n", p=R))\
                .then_inc(c.sem["h_loaded"], 16)

        def store(c, it):
            wait(sp, c, it, "base", 1)
            sp.dma_start(base_d[bass.ds(it * (CTX * J) + c.s * J, J), :, :].rearrange("j p n -> p j n"),
                         c.base[:, :, :]).then_inc(c.sem["base_stored"], 16)

        a, b = cs

        def body(it, first, last):
            for c in cs:
                if c is b and not first:
                    store(b, it - 1)
                if not last:
                    wait(sp, c, it, "h_bias", 1)
                    load(c, it + 1)
            store(a, it)

        load(a, 0)
        load(b, 0)
        body(0, True, False)
        with sp.Fori(1, ITERS - 1) as it:
            body(it, False, False)
        body(ITERS - 1, False, True)
        store(b, ITERS - 1)
        for c in cs:
            sp.wait_ge(c.sem["base_stored"], 16 * (ITERS + 1))

    def vector_program(v):
        for c in cs:
            v.memset(c.am2[:, :], 0.0).then_inc(c.sem["base_stored"], 16)
            v.memset(c.yt[:, :, NT:NTP], 0.0)
            for i in range(NI):
                v.tensor_copy(c.v[:, i, :, DH:DV], k.value_mask[:, :].unsqueeze(2))

        def layer_norm(c, it, n):
            if n == 0:
                wait(v, c, it, "h_loaded", 16)
            elif n == 2:
                wait(v, c, it, "h_ffn", 3)
            else:
                wait(v, c, it, "h_attn", (n + 1) // 2)
            h = c.h_in if n == 0 else c.h
            for j in range(J):
                st = v.bn_stats(c.st[:, j, :], h[:, j, :])
            st.then_inc(c.sem["ln"], 1)
            wait(v, c, it, "ln", 4 * n + 1)
            v.nop(nofuse=True)
            for j in range(J):
                mv = v.bn_aggr(c.mv[:, j, :], c.st[:, j, :])
            mv.then_inc(c.sem["ln"], 1)
            wait(v, c, it, "ln", 4 * n + 2)
            v.tensor_scalar(c.var[:, :], c.mv[:, :, 1:2].rearrange("p j o -> p (j o)"), EPS, None, ALU.add)\
                .then_inc(c.sem["ln"], 1)

        def normalise(c, it, n):
            wait(v, c, it, "ln_power", n + 1)
            h = c.h_in if n == 0 else c.h
            for j in range(J):
                xj = v.tensor_scalar(c.xh[:, j, :], h[:, j, :], c.mv[:, j, 0:1], c.rstd[:, j:j + 1],
                                     ALU.subtract, ALU.mult)
            xj.then_inc(c.sem["ln"], 1)

        def rotate(c, it):
            for i in range(4):
                yield 0.42 + 0.04 * i
                wait(v, c, it, "rope_mm", i + 1)
                v.tensor_tensor(c.rn[:, i, :].rearrange(images, i=NI), c.ps[:, i, 0:NT].rearrange(images, i=NI),
                                img_bc(k.sin), ALU.mult).then_inc(c.sem["rope_sin"], 1)
            for i in range(4):
                yield 0.56 + 0.03 * i
                wait(v, c, it, "rope_cos", i + 1)
                wait(v, c, it, "rope_sin", i + 1)
                dst = c.qt[:, i, 0:NT] if i < 2 else c.rn[:, i, :]
                v.tensor_tensor(dst, c.rc[:, i, :], c.rn[:, i, :], ALU.add).then_inc(c.sem["rope_sum"], 1)

        def spread_keys(c, it, l):
            for f in range(2):
                yield 0.713 + 0.04 * f
                wait(v, c, it, *(("rope_sum", 3 + f) if l == 0 else ("q1", 3 + f)))
                for o in range(QH):
                    kd = v.tensor_scalar(c.kd[:, f, :, o, :], c.rn[:, 2 + f, :].rearrange(images, i=NI),
                                         k.head_mask[:, o:o + 1], None, ALU.mult)
                kd.then_inc(c.sem["keys"], 1)

        def values(c, it, l):
            for q in range(4):
                yield 0.8 + 0.05 * q
                wait(v, c, it, "vt_mm", 4 * l + q + 1)
                src = c.ps[0:GK, (q + 2) % 4, :].rearrange("p (i h n) -> p i h n", i=2, h=H)
                for i in range(2):
                    vv = v.tensor_tensor(c.v[:, 2 * q + i, :, 0:DH], src[:, i, :, :],
                                         k.value_mask[:, :].unsqueeze(2).broadcast_to([GK, H, DH]), ALU.mult)
                vv.then_inc(c.sem["values"], 1)

        def bias_and_max(c, it, q):
            l = q // NPAIR
            wait(v, c, it, "score_mm", q + 1)
            if q > 1:
                wait(v, c, it, "probt_mm", q - 1)
            sc, mx = c.sc2[:, q % 2, :], c.mx2[:, q % 2, :]
            by_bank = lambda table: table[0:PR, :].rearrange("p (f r n) -> p r f n", f=2, r=2)
            v.tensor_tensor(by_bank(sc), c.ps[0:PR, 0:2, 0:HT // 2].rearrange("p r (f n) -> p r f n", f=2),
                            by_bank(k.attn[l].bias), ALU.add)\
                .then_inc(c.sem["biased"], 1)
            wait(v, c, it, "biased", q + 1)
            v.tensor_reduce(mx[0:PR, :], sc[0:PR, :].rearrange("p (h t) -> p h t", h=H), AX.X, ALU.max)\
                .then_inc(c.sem["row_max"], 1)

        def divide(c, it, q):
            ysum = c.ps[0:PR, 3, Y0:Y0 + H * DV].rearrange("p (h n) -> p h n", h=H)
            wait(v, c, it, "pv_mm", q + 1)
            v.reciprocal(c.rs[0:PR, :], ysum[:, :, DH:DV].rearrange("p h o -> p (h o)")).then_inc(c.sem["inv_sum"], 1)
            wait(v, c, it, "inv_sum", q + 1)
            if q > 0:
                wait(v, c, it, "yt_mm", q)
            v.tensor_tensor(c.y[0:PR, :].rearrange("p (h n) -> p h n", h=H), ysum[:, :, 0:DH],
                            c.rs[0:PR, :].unsqueeze(2).broadcast_to([PR, H, DH]), ALU.mult).then_inc(c.sem["y"], 1)

        def add_attention(c, it, l):
            wait(v, c, it, "proj_mm", l + 1)
            wait(v, c, it, "h_bias", l + 1)
            v.tensor_tensor(c.h[:, :, :].rearrange("p j n -> p (j n)"),
                            c.ps[0:R, 2:4, :].rearrange("p b n -> p (b n)")[:, 0:J * D],
                            c.hb[:, :, :].rearrange("p j n -> p (j n)"), ALU.add).then_inc(c.sem["h_attn"], 1)

        def quantise_input(c, it):
            def step(n):
                wait(v, c, it, "quant", n)
            wait(v, c, it, "base_stored", 16)
            wait(v, c, it, "ln", 8)
            v.tensor_reduce(c.am[:, :], c.xh[:, :, :], AX.X, ALU.max, apply_absolute_value=True)\
                .then_inc(c.sem["quant"], 1)
            step(1)
            v.tensor_scalar(c.am[:, :], c.am[:, :], 1e-5, None, ALU.max).then_inc(c.sem["quant"], 1)
            step(2)
            v.reciprocal(c.am[:, :], c.am[:, :]).then_inc(c.sem["quant"], 1)
            step(3)
            v.tensor_scalar(c.am[:, :], c.am[:, :], 127.0, None, ALU.mult).then_inc(c.sem["quant"], 1)
            step(4)
            v.reciprocal(c.unit_in[:, :], c.am[:, :]).then_inc(c.sem["quant"], 1)
            for j in range(J):
                qj = v.tensor_scalar(c.qf[:, j, :], c.xh[:, j, :], c.am[:, j:j + 1], MAGIC, ALU.mult, ALU.add)
            qj.then_inc(c.sem["quant"], 1)
            step(6)
            v.tensor_scalar(c.qb[:, :, :], c.qf[:, :, :], MAGIC, None, ALU.subtract).then_inc(c.sem["quant"], 1)

        def hidden(c, it, m):
            wait(v, c, it, "hid_mm", m + 1)
            if m == 0:
                wait(v, c, it, "unit", 1)
                v.memset(c.a[:, :, NT:NTP], 0.0).then_inc(c.sem["pad"], 1)
            v.tensor_tensor(c.t0[:, m, 0:NT], c.ps[:, (m + 2) % 4, 0:NT], c.unit[:, 0:NT], ALU.mult)\
                .then_inc(c.sem["hid"], 1)

        def convolve_left(c, it, m):
            am = c.a[:, m, 0:NT].rearrange(images, i=NI)
            tm = c.t0[:, m, 0:NT].rearrange(images, i=NI)
            wait(v, c, it, "mid", m + 1)
            v.scalar_tensor_tensor(am[:, :, 1:T], tm[:, :, 0:T - 1], k.conv[:, m, 0:1], am[:, :, 1:T],
                                   ALU.mult, ALU.add).then_inc(c.sem["left"], 1)

        def convolve_right(c, it, m):
            am = c.a[:, m, 0:NT].rearrange(images, i=NI)
            tm = c.t0[:, m, 0:NT].rearrange(images, i=NI)
            wait(v, c, it, "left", m + 1)
            v.scalar_tensor_tensor(am[:, :, 0:T - 1], tm[:, :, 1:T], k.conv[:, m, 2:3], am[:, :, 0:T - 1],
                                   ALU.mult, ALU.add).then_inc(c.sem["right"], 1)

        def quantise_hidden(c, it, j):
            src = c.ps[0:R, 2 * (j % 2):2 * (j % 2) + 2, :].rearrange("p b n -> p (b n)")

            def step(n):
                wait(v, c, it, "quant2", 8 * j + n)
            wait(v, c, it, "hidt_mm", j + 1)
            v.tensor_reduce(c.am2[:, :], src, AX.X, ALU.max, apply_absolute_value=True).then_inc(c.sem["quant2"], 1)
            step(1)
            v.tensor_scalar(c.am2[:, :], c.am2[:, :], 1e-5, None, ALU.max).then_inc(c.sem["quant2"], 1)
            step(2)
            v.reciprocal(c.am2[:, :], c.am2[:, :]).then_inc(c.sem["quant2"], 1)
            step(3)
            v.tensor_scalar(c.am2[:, :], c.am2[:, :], 127.0, None, ALU.mult).then_inc(c.sem["quant2"], 1)
            step(4)
            v.reciprocal(c.unit2[:, j:j + 1], c.am2[:, :]).then_inc(c.sem["quant2"], 1)
            v.tensor_scalar(c.qf2[0:R, :], src, c.am2[:, :], MAGIC, ALU.mult, ALU.add).then_inc(c.sem["quant2"], 1)
            step(6)
            if j > 0:
                wait(v, c, it, "hq_mm", j)
            v.tensor_scalar(c.qb2[0:R, :], c.qf2[0:R, :], MAGIC, None, ALU.subtract).then_inc(c.sem["quant2"], 1)
            v.tensor_tensor(c.unit2[:, j:j + 1], c.unit2[:, j:j + 1], k.wunit[0:R, 1:2], ALU.mult)\
                .then_inc(c.sem["quant2"], 1)

        def add_ffn(c, it, j):
            wait(v, c, it, "out_mm", j + 1)
            wait(v, c, it, "quant2", 8 * j + 8)
            v.scalar_tensor_tensor(c.h[:, j, :], c.ps[0:R, 2 * (j % 2) + 1, 0:D], c.unit2[:, j:j + 1], c.h[:, j, :],
                                   ALU.mult, ALU.add).then_inc(c.sem["h_ffn"], 1)

        def stage(name, c, it):
            if name == "ffn":
                yield 0.001
                layer_norm(c, it, 1)
                yield 0.05
                normalise(c, it, 1)
                yield 0.098
                quantise_input(c, it)
                for m in range(MH + 1):
                    yield 0.18 + 0.035 * m
                    if m > 0:
                        convolve_left(c, it, m - 1)
                    if m < MH:
                        hidden(c, it, m)
                    if m > 0:
                        convolve_right(c, it, m - 1)
                yield 0.58
                quantise_hidden(c, it, 0)
                yield 0.68
                quantise_hidden(c, it, 1)
                yield 0.76
                add_ffn(c, it, 0)
                yield 0.82
                quantise_hidden(c, it, 2)
                yield 0.885
                add_ffn(c, it, 1)
                yield 0.97
                add_ffn(c, it, 2)
                return
            l = int(name[-1])
            if name.startswith("project"):
                yield 0.0
                layer_norm(c, it, 2 * l)
                yield 0.08
                normalise(c, it, 2 * l)
                if l == 0:
                    yield from rotate(c, it)
                yield from spread_keys(c, it, l)
                yield from values(c, it, l)
                return
            for p in range(-2, NPAIR):
                if p + 2 < NPAIR:
                    yield (0.25, 0.55, p + 1.45)[min(p + 2, 2)] / PAIR_SPAN
                    bias_and_max(c, it, NPAIR * l + p + 2)
                if p >= 0:
                    yield (p + 1.55) / PAIR_SPAN
                    divide(c, it, NPAIR * l + p)
            yield (NPAIR + 1.4) / PAIR_SPAN
            add_attention(c, it, l)
            if l == 1:
                layer_norm(c, it, 3)
                yield (NPAIR + 1.9) / PAIR_SPAN
                normalise(c, it, 3)
                yield 0.975
                wait(v, c, it, "logit_mm", 1)
                v.tensor_tensor(k.logits[:, bass.ds(it * (CTX * J) + c.s * J, J), :],
                                c.ps[0:R, 2, 0:J * E].rearrange("p (j e) -> p j e", j=J),
                                k.br[0:R, :].unsqueeze(1).broadcast_to([R, J, E]), ALU.add).then_inc(c.sem["logit"], 1)

        run(v, stage)

    def gpsimd_program(g):
        def power(c, it, n):
            wait(g, c, it, "ln", 4 * n + 3)
            g.tensor_tensor(c.rstd[:, :], c.var[:, :], k.half[0:R, :], ALU.pow).then_inc(c.sem["ln_power"], 1)

        def add_bias(c, it, l):
            wait(g, c, it, "ln", 8 * l + 4)
            h = c.h_in if l == 0 else c.h
            g.tensor_tensor(c.hb[:, :, :], h[:, :, :], k.attn[l].ob[0:R, :].unsqueeze(1).broadcast_to([R, J, D]),
                            ALU.add).then_inc(c.sem["h_bias"], 1)

        def rope_cos(c, it):
            for i in range(4):
                yield 0.28 + 0.04 * i
                wait(g, c, it, "q0", i + 1)
                g.tensor_tensor(c.rc[:, i, :].rearrange(images, i=NI), c.qk[:, i, :].rearrange(images, i=NI),
                                img_bc(k.cos), ALU.mult).then_inc(c.sem["rope_cos"], 1)

        def shift(c, it, q):
            wait(g, c, it, "row_max", q + 1)
            s3 = c.sc2[0:PR, q % 2, :].rearrange("p (h t) -> p h t", h=H)
            g.tensor_tensor(s3, s3, c.mx2[0:PR, q % 2, :].unsqueeze(2).broadcast_to([PR, H, T]), ALU.subtract)\
                .then_inc(c.sem["shifted"], 1)

        def stage(name, c, it):
            if name == "ffn":
                yield 0.02
                power(c, it, 1)
                return
            l = int(name[-1])
            if name.startswith("project"):
                yield 0.05
                power(c, it, 2 * l)
                if l == 0:
                    yield from rope_cos(c, it)
                yield 0.5
                add_bias(c, it, l)
                return
            for p in range(NPAIR):
                yield (0.5, 0.8, p - 0.25)[min(p, 2)] / PAIR_SPAN
                shift(c, it, NPAIR * l + p)
            if l == 1:
                yield (NPAIR + 1.8) / PAIR_SPAN
                power(c, it, 3)
                yield 1.0
                wait(g, c, it, "ln", 16)
                g.tensor_copy(k.xn[:, bass.ds(it * (CTX * J) + c.s * J, J), 0:D], c.xh[:, :, :])\
                    .then_inc(c.sem["xn_kept"], 1)
                wait(g, c, it, "logit", 1)
                wait(g, c, it, "xn_kept", 1)
                g.tensor_tensor(c.base[:, :, :], c.h[:, :, :], c.xh[:, :, :], ALU.add).then_inc(c.sem["base"], 1)

        run(g, stage)

    def scalar_program(a):
        def evacuate_x(c, it, n):
            wait(a, c, it, "xt_mm", max(n, 1))
            a.activation(c.xt[:, :, :], c.ps[:, 0:2, 0:NTP], ACT.Copy).then_inc(c.sem["xt"], 1)

        def queries_keys(c, it, l):
            w = k.attn[l]
            for i in range(4):
                yield 0.227 + 0.04 * i
                wait(a, c, it, "qk_mm", 4 * l + i + 1)
                dst = c.qk[:, i, :] if l == 0 else c.qt[:, i, 0:NT] if i < 2 else c.rn[:, i, :]
                bias, scale = (w.qb, DH ** -0.5) if i < 2 else (w.kb, 1.0)
                a.activation(dst, c.ps[:, i, 0:NT], ACT.Identity, bias=bias[:, i % 2:i % 2 + 1], scale=scale)\
                    .then_inc(c.sem["q0" if l == 0 else "q1"], 1)

        def value_rows(c, it, l):
            for f in range(2):
                yield 0.62 + 0.05 * f
                wait(a, c, it, "v_mm", 2 * l + f + 1)
                a.activation(c.vr[:, f, :, :, :],
                             c.ps[:, f, 0:NT].rearrange(images, i=NI).unsqueeze(2).broadcast_to([P, NI, GH, T]),
                             ACT.Identity, bias=k.attn[l].vb[:, f:f + 1]).then_inc(c.sem["v_ev"], 1)

        def exponent(c, it, q):
            wait(a, c, it, "shifted", q + 1)
            a.activation(c.sc2[0:PR, q % 2, :], c.sc2[0:PR, q % 2, :], ACT.Exp).then_inc(c.sem["prob"], 1)

        def evacuate_prob(c, it, q):
            wait(a, c, it, "probt_mm", q + 1)
            for b, (g, n) in enumerate(((0, 4), (4, 2))):
                src = c.ps[0:GK, 2 + b, 0:n * PR].rearrange("p (g t) -> p g t", g=n)
                pt = a.activation(c.pt[:, g:g + n, 0:PR], src, ACT.Copy)
            pt.then_inc(c.sem["probt"], 1)

        def evacuate_y(c, it, q):
            wait(a, c, it, "yt_mm", q + 1)
            p = q % NPAIR
            src = c.ps[:, 2, 0:2 * P].rearrange("p (f i t) -> p f i t", f=2, i=2)
            dst = c.yt[:, :, 2 * T * p:2 * T * (p + 1)].rearrange("p f (i t) -> p f i t", i=2)
            a.activation(dst, src[:, :, :, 0:T], ACT.Copy).then_inc(c.sem["yt"], 1)

        def ffn(c, it):
            yield 0.13
            wait(a, c, it, "xq_mm", 1)
            src = bft(c.ps[:, 0, :])[:, 0:2 * J * (R + 1)].rearrange("p (f j t) -> p f j t", f=2, j=J)
            a.activation(c.xq[:, :, :].rearrange("p f (j t) -> p f j t", j=J), src[:, :, :, 0:R], ACT.Copy)\
                .then_inc(c.sem["xq"], 1)
            wait(a, c, it, "unit_mm", 1)
            a.activation(c.unit, c.ps[:, 1, 0:NTP], ACT.Copy, scale=k.wunit[:, 0:1]).then_inc(c.sem["unit"], 1)
            for m in range(MH):
                yield 0.2 + 0.035 * m
                wait(a, c, it, "hid", m + 1)
                a.activation(c.a[:, m, 0:NT], c.t0[:, m, 0:NT], ACT.Identity, bias=k.conv[:, m, 3:4],
                             scale=k.conv[:, m, 1:2]).then_inc(c.sem["mid"], 1)
            for m in range(MH):
                yield 0.49 + 0.0 * m
                wait(a, c, it, "right", m + 1)
                a.activation(c.a[:, m, 0:NT], c.a[:, m, 0:NT], ACT.Silu).then_inc(c.sem["silu"], 1)
            for j in range(J):
                yield (0.67, 0.77, 0.91)[j]
                wait(a, c, it, "hq_mm", j + 1)
                src = bft(c.ps[:, 2 * (j % 2), :])[:, 0:MH * (R + 1)].rearrange("p (m t) -> p m t", m=MH)
                a.activation(c.hq[:, :, R * j:R * j + R], src[:, :, 0:R], ACT.Copy).then_inc(c.sem["hq"], 1)

        def stage(name, c, it):
            if name == "ffn":
                yield from ffn(c, it)
                return
            l = int(name[-1])
            if name.startswith("project"):
                yield 0.15
                evacuate_x(c, it, 2 * l)
                yield from queries_keys(c, it, l)
                yield from value_rows(c, it, l)
                return
            for p in range(-2, NPAIR):
                q = NPAIR * l + p
                if p >= 0:
                    yield (p + 1.15) / PAIR_SPAN
                    evacuate_prob(c, it, q)
                    yield (p + 1.7) / PAIR_SPAN
                    evacuate_y(c, it, q)
                if p + 2 < NPAIR:
                    yield (0.75, 1.283, p + 1.9)[min(p + 2, 2)] / PAIR_SPAN
                    exponent(c, it, q + 2)
            if l == 1:
                yield (NPAIR + 2.2) / PAIR_SPAN
                evacuate_x(c, it, 3)

        run(a, stage)

    def tensor_program(t):
        def transpose_x(c, it, n):
            wait(t, c, it, "ln", 4 * n + 4)
            for j in range(J):
                for f in range(2):
                    tr = t.transpose(c.ps[:, f, R * j:R * j + R], c.xh[:, j, P * f:P * f + P], k.ident[0:R, 0:R])
            tr.then_inc(c.sem["xt_mm"], 1)

        def project(c, which, l, f, bank):
            w = k.attn[l].w
            for i in range(2):
                mm = t.matmul(c.ps[:, bank, 0:NT], w[:, which, i, P * f:P * f + P], c.xt[:, i, 0:NT],
                              start=(i == 0), stop=(i == 1))
            return mm

        def queries_keys(c, it, l):
            for i in range(4):
                yield 0.2 + 0.04 * i
                if i == 0:
                    wait(t, c, it, "xt", l + 1)
                project(c, i // 2, l, i % 2, i).then_inc(c.sem["qk_mm"], 1)

        def rotate_pairs(c, it):
            for i in range(4):
                yield 0.336 + 0.04 * i
                wait(t, c, it, "q0", i + 1)
                t.matmul(c.ps[:, i, 0:NT], k.rot[:, :], c.qk[:, i, :], start=True, stop=True)\
                    .then_inc(c.sem["rope_mm"], 1)

        def value_products(c, it, l):
            for f in range(2):
                yield 0.543 + 0.054 * f
                wait(t, c, it, *(("rope_sin", f + 1) if l == 0 else ("q1", f + 1)))
                project(c, 2, l, f, f).then_inc(c.sem["v_mm"], 1)

        def value_transposes(c, it, l):
            for q in range(4):
                yield 0.76 + 0.05 * q
                if q < 2:
                    wait(t, c, it, *(("rope_sin", 3 + q) if l == 0 else ("q1", 3 + q)))
                if q == 0:
                    wait(t, c, it, "v_ev", 2 * l + 2)
                for i in range(2):
                    for f in range(2):
                        tr = t.transpose(c.ps[0:GK, (q + 2) % 4, D * i + P * f:D * i + P * f + P],
                                         c.vr[:, f, 2 * q + i, :, :].rearrange("p r t -> p (r t)"), k.ident[:, :])
                tr.then_inc(c.sem["vt_mm"], 1)

        def scores(c, it, q):
            l, p = divmod(q, NPAIR)
            if p == 0:
                wait(t, c, it, *(("rope_sum", 2) if l == 0 else ("q1", 2)))
                wait(t, c, it, "keys", 2 * l + 2)
                wait(t, c, it, "values", 4 * l + 4)
            else:
                wait(t, c, it, "biased", q)
            t.nop(nofuse=True)
            for f in range(2):
                for r in range(2):
                    for i in range(2):
                        rows = slice(64 * r, 64 * r + 64)
                        n = 2 * p + i
                        m = (64, T)[i]
                        mm = t.matmul(c.ps[64 * i:64 * i + m, r, QH * T * f:QH * T * (f + 1)],
                                      c.qt[rows, f, T * n:T * n + m],
                                      c.kd[rows, f, n, :, :].rearrange("p o t -> p (o t)"), start=True, stop=True,
                                      skip_group_check=True)
            mm.then_inc(c.sem["score_mm"], 1)

        def transpose_prob(c, it, q):
            wait(t, c, it, "prob", q + 1)
            if q % NPAIR:
                wait(t, c, it, "yt", q)
            for g in range(G):
                tr = t.transpose(c.ps[0:GK, 2 + g // 4, PR * (g % 4):PR * (g % 4 + 1)],
                                 c.sc2[0:PR, q % 2, group_col(g):group_col(g) + GK], k.ident[0:PR, 0:PR])
            tr.then_inc(c.sem["probt_mm"], 1)

        def weigh_values(c, it, q):
            wait(t, c, it, "probt", q + 1)
            t.nop(nofuse=True)
            for i in range(2):
                for g in range(G):
                    h = GH * g
                    n = min(GH, H - h)
                    m = (64, T)[i]
                    mm = t.matmul(c.ps[64 * i:64 * i + m, 3, Y0 + DV * h:Y0 + DV * (h + n)],
                                  c.pt[:, g, 64 * i:64 * i + m],
                                  c.v[:, 2 * (q % NPAIR) + i, h:h + n, :].rearrange("p h n -> p (h n)"),
                                  start=True, stop=True, skip_group_check=True)
            mm.then_inc(c.sem["pv_mm"], 1)

        def transpose_y(c, it, q):
            wait(t, c, it, "y", q + 1)
            for f in range(2):
                tr = t.transpose(c.ps[:, 2, P * f:P * f + PR], c.y[0:PR, P * f:P * f + P], k.ident[0:PR, 0:PR])
            tr.then_inc(c.sem["yt_mm"], 1)

        def output_projection(c, it, l):
            wait(t, c, it, "yt", NPAIR * (l + 1))
            dst = c.ps[0:R, 2:4, :].rearrange("p b n -> p (b n)")
            for j in range(J):
                for f in range(2):
                    mm = t.matmul(dst[:, D * j:D * j + D], c.yt[:, f, R * j:R * j + R], k.attn[l].w[:, 3, f, :],
                                  start=(f == 0), stop=(f == 1))
            mm.then_inc(c.sem["proj_mm"], 1)

        def transpose_hidden(c, it, j):
            if j == 0:
                wait(t, c, it, "silu", MH)
                wait(t, c, it, "pad", 1)
            if j == 1:
                wait(t, c, it, "hid", MH)
            if j == 2:
                wait(t, c, it, "h_ffn", 1)
            dst = c.ps[0:R, 2 * (j % 2):2 * (j % 2) + 2, :].rearrange("p b n -> p (b n)")
            for m in range(MH):
                tr = t.transpose(dst[:, P * m:P * m + P], c.a[:, m, R * j:R * j + R], k.ident[:, :])
            tr.then_inc(c.sem["hidt_mm"], 1)

        def ffn(c, it):
            yield 0.12
            wait(t, c, it, "quant", 7)
            dst = bft(c.ps[:, 0, :])
            for j in range(J):
                for f in range(2):
                    o = (R + 1) * (J * f + j)
                    tr = t.transpose(dst[:, o:o + R], c.qb[:, j, P * f:P * f + P], k.ident_bf[0:R, 0:R])
            tr.then_inc(c.sem["xq_mm"], 1)
            for j in range(J):
                mm = t.matmul(c.ps[:, 1, R * j:R * j + R], c.unit_in[:, j:j + 1].broadcast_to([R, P]),
                              k.ident[0:R, 0:R], start=True, stop=True)
            mm.then_inc(c.sem["unit_mm"], 1)
            for m in range(MH):
                yield 0.121 + 0.035 * m
                if m == 0:
                    wait(t, c, it, "xq", 1)
                    wait(t, c, it, "h_attn", 1)
                if m == 3:
                    wait(t, c, it, "unit", 1)
                if m >= 4:
                    wait(t, c, it, "hid", m - 3)
                for f in range(2):
                    mm = t.matmul(c.ps[:, (m + 2) % 4, 0:NT], k.w1[:, f, P * m:P * m + P], c.xq[:, f, 0:NT],
                                  start=(f == 0), stop=(f == 1))
                mm.then_inc(c.sem["hid_mm"], 1)
            yield 0.56
            transpose_hidden(c, it, 0)
            yield 0.57
            transpose_hidden(c, it, 1)
            for j in range(J):
                yield (0.66, 0.768, 0.905)[j]
                wait(t, c, it, "quant2", 8 * j + 7)
                dst = bft(c.ps[:, 2 * (j % 2), :])
                for m in range(MH):
                    tr = t.transpose(dst[:, (R + 1) * m:(R + 1) * m + R], c.qb2[0:R, P * m:P * m + P],
                                     k.ident_bf[0:R, 0:R])
                tr.then_inc(c.sem["hq_mm"], 1)
                yield (0.69, 0.79, 0.93)[j]
                wait(t, c, it, "hq", j + 1)
                for m in range(MH):
                    mm = t.matmul(c.ps[0:R, 2 * (j % 2) + 1, 0:D], c.hq[:, m, R * j:R * j + R], k.w2[:, m, :],
                                  start=(m == 0), stop=(m == MH - 1))
                mm.then_inc(c.sem["out_mm"], 1)
                if j == 0:
                    yield 0.764
                    transpose_hidden(c, it, 2)

        def stage(name, c, it):
            if name == "ffn":
                yield from ffn(c, it)
                return
            l = int(name[-1])
            if name.startswith("project"):
                yield 0.12
                transpose_x(c, it, 2 * l)
                yield from queries_keys(c, it, l)
                if l == 0:
                    yield from rotate_pairs(c, it)
                yield from value_products(c, it, l)
                yield from value_transposes(c, it, l)
                return
            for p in range(-2, NPAIR):
                q = NPAIR * l + p
                if p >= 0:
                    yield (p + 1.0) / PAIR_SPAN
                    transpose_prob(c, it, q)
                if p + 2 < NPAIR:
                    yield (0.0, 0.071, p + 1.2)[min(p + 2, 2)] / PAIR_SPAN
                    scores(c, it, q + 2)
                if p >= 0:
                    yield (p + 1.3) / PAIR_SPAN
                    weigh_values(c, it, q)
                    yield (p + 1.6) / PAIR_SPAN
                    transpose_y(c, it, q)
            yield (NPAIR + 1.082) / PAIR_SPAN
            output_projection(c, it, l)
            if l == 1:
                yield (NPAIR + 2.166) / PAIR_SPAN
                transpose_x(c, it, 3)
                yield (NPAIR + 2.3) / PAIR_SPAN
                wait(t, c, it, "xt", 3)
                for j in range(J):
                    for f in range(2):
                        mm = t.matmul(c.ps[0:R, 2, E * j:E * j + E], c.xt[:, f, R * j:R * j + R], k.wr[:, f, :],
                                      start=(f == 0), stop=(f == 1))
                mm.then_inc(c.sem["logit_mm"], 1)

        run(t, stage)

    with nc.Block() as block:
        block.sync(sync_program)
        block.vector(vector_program)
        block.gpsimd(gpsimd_program)
        block.scalar(scalar_program)
        block.tensor(tensor_program)



def experts(nc, ctx, sem, d, k, base_d, xs_d, weighted_d, b1_d, b2_d, out):
    def sb(name, shape, dt=F32):
        return ctx.enter_context(nc.sbuf_tensor(name, shape, dt))

    ew1 = sb("ew1", [P, E, 2, EH])
    ew2 = sb("ew2", [P, E, EH // P, D])
    eb1, eb2 = sb("eb1_rows", [3, E, EH], BF16), sb("eb2_rows", [3, E, D], BF16)
    ones_bf = sb("ones_bf", [P, P], BF16)
    tile_expert = sb("tile_expert", [1, TILES], I32)
    ew_loaded, eb_loaded = sem("ew_loaded"), sem("eb_loaded")
    ps = k.ps

    with ExitStack() as dctx:
        def sbd(name, shape, dt=F32):
            return dctx.enter_context(nc.sbuf_tensor(name, shape, dt))
        w1, w2 = sbd("weight1", [R, COLS]), sbd("weight2", [R, COLS])
        dest = [sbd("dest1", [R, COLS], U32), sbd("dest2", [R, COLS], U32)]
        row_ids = sbd("row_ids", [R, 2, COLS])
        scattered, tagged = [sem("scattered1"), sem("scattered2")], sem("rows_tagged")
        big = [R, COLS, E]
        pr, pr2, ta, tb = (sbd(n, big) for n in ("probs", "probs_rest", "tmp_a", "tmp_b"))
        oh = [sbd("choice1", big), sbd("choice2", big)]
        both = sbd("both", big, BF16)
        red, m1, m2, top = (sbd(n, [R, COLS]) for n in ("red", "m1", "m2", "top"))
        nt, na, nb_ = sbd("n_tiles", [R, E]), sbd("tiles_a", [R, E]), sbd("tiles_b", [R, E])
        tile_cmp, tile_sum = sbd("tile_cmp", [1, TILES, E]), sbd("tile_sum", [1, TILES])
        rank, upto, valid, spare, tile_no = (sbd("rank", [R, E]), sbd("upto", [R, R]), sbd("valid", [R, COLS]),
                                             sbd("spare", [R, 2, COLS]), sbd("tile_no", [1, TILES]))
        upto_bf = sbd("upto_bf", [R, R], BF16)
        t_loaded, step, expo, counted, dests = sem("t_loaded"), sem("step"), sem("expo"), sem("counted"), sem("dests")
        experts_known = sem("experts_known")
        tables = [(rank[:, :], d.rank), (upto[:, :], d.upto), (valid[:, :], d.valid), (spare[:, :, :], d.spare),
                  (tile_no[:, :], d.tile_no), (row_ids[:, :, :], d.row_ids)]

        with nc.Block() as block:
            @block.sync
            def _(sp):
                for dst, src in tables:
                    sp.dma_start(dst, src).then_inc(t_loaded, 16)
                for n, (dst, src) in enumerate(((eb1, b1_d), (eb2, b2_d))):
                    sp.dma_start(dst[:, :, :].rearrange("i e n -> i (e n)"), src).then_inc(eb_loaded, 16)
                for e in range(E):
                    sp.dma_start(ew1[:, e, :, :], d.W1[e].rearrange("(k p) n -> p k n", p=P)).then_inc(ew_loaded, 16)
                for e in range(E):
                    sp.dma_start(ew2[:, e, :, :], d.W2[e].rearrange("(k p) n -> p k n", p=P)).then_inc(ew_loaded, 16)

            @block.scalar
            def _(a):
                a.wait_ge(step, 2)
                a.activation(pr[:, :, :], pr[:, :, :], ACT.Exp).then_inc(expo, 1)

            @block.tensor
            def _(t):
                t.wait_ge(t_loaded, 16 * len(tables))
                t.wait_ge(counted, 1)
                flat = both[:, :, :].rearrange("p c e -> p (c e)")
                t.matmul(ps[0:R, 0, 0:COLS * E], upto_bf[:, :], flat, start=True, stop=True).then_inc(counted, 1)
                t.matmul(ps[0:R, 1, 0:COLS * E], ones_bf[0:R, 0:R], flat, start=True, stop=True).then_inc(counted, 1)

            @block.vector
            def _(v):
                count = [0]

                def did(instruction):
                    instruction.then_inc(step, 1)
                    count[0] += 1
                    v.wait_ge(step, count[0])

                def over_e(table):
                    return table[:, :].unsqueeze(2).broadcast_to(big)

                def over_c(table):
                    return table[:, :].unsqueeze(1).broadcast_to(big)

                did(v.tensor_reduce(m1[:, :], k.logits[:, :, :], AX.X, ALU.max))
                did(v.tensor_tensor(pr[:, :, :], k.logits[:, :, :], over_e(m1), ALU.subtract))
                v.wait_ge(expo, 1)
                did(v.tensor_reduce(red[:, :], pr[:, :, :], AX.X, ALU.add))
                did(v.reciprocal(red[:, :], red[:, :]))
                did(v.tensor_tensor(pr[:, :, :], pr[:, :, :], over_e(red), ALU.mult))
                v.wait_ge(t_loaded, 16 * len(tables))
                for n, (src, m) in enumerate(((pr, m1), (pr2, m2))):
                    did(v.tensor_reduce(m[:, :], src[:, :, :], AX.X, ALU.max))
                    did(v.tensor_tensor(ta[:, :, :], src[:, :, :], over_e(m), ALU.is_ge))
                    did(v.tensor_tensor(ta[:, :, :], ta[:, :, :], over_c(rank), ALU.mult))
                    did(v.tensor_reduce(top[:, :], ta[:, :, :], AX.X, ALU.max))
                    did(v.tensor_tensor(oh[n][:, :, :], ta[:, :, :], over_e(top), ALU.is_ge))
                    if n == 0:
                        did(v.scalar_tensor_tensor(pr2[:, :, :].rearrange("p c e -> p (c e)"),
                                                   oh[0][:, :, :].rearrange("p c e -> p (c e)"), -2.0,
                                                   pr[:, :, :].rearrange("p c e -> p (c e)"), ALU.mult, ALU.add))
                did(v.tensor_add(red[:, :], m1[:, :], m2[:, :]))
                did(v.tensor_scalar(red[:, :], red[:, :], 1e-9, None, ALU.max))
                did(v.reciprocal(red[:, :], red[:, :]))
                did(v.tensor_mul(w1[:, :], m1[:, :], red[:, :]))
                did(v.tensor_mul(w2[:, :], m2[:, :], red[:, :]))
                for n in range(2):
                    did(v.tensor_tensor(oh[n][:, :, :], oh[n][:, :, :], over_e(valid), ALU.mult))
                did(v.memset(ones_bf[:, :], 1.0))
                did(v.tensor_copy(upto_bf[:, :], upto[:, :]))
                did(v.tensor_add(ta[:, :, :], oh[0][:, :, :], oh[1][:, :, :]))
                v.tensor_copy(both[:, :, :], ta[:, :, :]).then_inc(counted, 1)
                v.wait_ge(counted, 3)
                did(v.tensor_copy(ta[:, :, :].rearrange("p c e -> p (c e)"), ps[0:R, 1, 0:COLS * E]))
                src, dst = ta, tb
                s = 1
                while s < COLS:
                    did(v.tensor_copy(dst[:, 0:s, :], src[:, 0:s, :]))
                    did(v.tensor_add(dst[:, s:, :], src[:, s:, :], src[:, 0:COLS - s, :]))
                    src, dst = dst, src
                    s *= 2
                did(v.tensor_scalar(nt[:, :], src[:, COLS - 1, :], 1.0 / P, (P - 1) / P - 0.5 + 0.5 / P,
                                    ALU.mult, ALU.add))
                did(v.tensor_scalar(nt[:, :], nt[:, :], MAGIC, None, ALU.add))
                did(v.tensor_scalar(nt[:, :], nt[:, :], MAGIC, None, ALU.subtract))
                did(v.tensor_copy(na[:, :], nt[:, :]))
                a_, b_ = na, nb_
                s = 1
                while s < E:
                    did(v.tensor_copy(b_[:, 0:s], a_[:, 0:s]))
                    did(v.tensor_add(b_[:, s:], a_[:, s:], a_[:, 0:E - s]))
                    a_, b_ = b_, a_
                    s *= 2
                did(v.tensor_tensor(tile_cmp[:, :, :], tile_no[:, :].unsqueeze(2).broadcast_to([1, TILES, E]),
                                    a_[0:1, :].unsqueeze(1).broadcast_to([1, TILES, E]), ALU.is_ge))
                did(v.tensor_reduce(tile_sum[:, :], tile_cmp[:, :, :], AX.X, ALU.add))
                v.tensor_scalar(tile_expert[:, :], tile_sum[:, :], float(E - 1), None, ALU.min)\
                    .then_inc(experts_known, 1)
                did(v.tensor_tensor(b_[:, :], a_[:, :], nt[:, :], ALU.subtract))
                did(v.tensor_scalar(b_[:, :], b_[:, :], float(P), None, ALU.mult))
                did(v.tensor_tensor(dst[:, :, :].rearrange("p c e -> p (c e)"),
                                    src[:, :, :].rearrange("p c e -> p (c e)"), ps[0:R, 1, 0:COLS * E], ALU.subtract))
                did(v.tensor_tensor(src[:, :, :].rearrange("p c e -> p (c e)"),
                                    dst[:, :, :].rearrange("p c e -> p (c e)"), ps[0:R, 0, 0:COLS * E], ALU.add))
                did(v.tensor_tensor(src[:, :, :], src[:, :, :], over_c(b_), ALU.add))
                for n in range(2):
                    did(v.tensor_tensor(dst[:, :, :], src[:, :, :], oh[n][:, :, :], ALU.mult))
                    did(v.tensor_reduce(red[:, :], dst[:, :, :], AX.X, ALU.add))
                    v.tensor_tensor(dest[n][:, :], red[:, :], spare[:, n, :], ALU.add).then_inc(dests, 1)
                    v.wait_ge(dests, n + 1)

            @block.gpsimd
            def _(g):
                g.wait_ge(t_loaded, 16 * len(tables))
                for n, w in enumerate((w1, w2)):
                    g.wait_ge(dests, n + 1)
                    if n == 1:
                        g.wait_ge(scattered[0], 16 * COLS)
                    g.tensor_copy(k.xn[:, :, D:D + 1], row_ids[:, n, :].unsqueeze(2)).then_inc(tagged, 1)
                    g.tensor_copy(k.xn[:, :, D + 1:XW], w[:, :].unsqueeze(2)).then_inc(tagged, 1)
                    g.wait_ge(tagged, 2 * n + 2)
                    for i in range(COLS):
                        g.indirect_dma_start(xs_d, bass.IndirectOffsetOnAxis(ap=dest[n][:, i:i + 1], axis=0),
                                             k.xn[:, i, :], None).then_inc(scattered[n], 16)
                g.wait_ge(scattered[1], 16 * COLS)

    cs = []
    for s in range(2):
        c = Bag()
        c.s = s
        c.x, c.xt = sb(f"mx{s}", [P, XW]), sb(f"mxt{s}", [P, 2, P])
        c.h, c.ht, c.o = sb(f"mh{s}", [P, EH]), sb(f"mht{s}", [P, EH]), sb(f"mo{s}", [P, D])
        c.tag = sb(f"tag{s}", [P, 2])
        c.to, c.weight = sb(f"result_row{s}", [P, 1], U32), sb(f"pair_weight{s}", [P, 1])
        c.x_in, c.x_turned, c.xt_ready = sem(f"x_in{s}"), sem(f"x_turned{s}"), sem(f"xt_ready{s}")
        c.h_mm, c.gelu, c.h_turned, c.ht_ready = sem(f"h_mm{s}"), sem(f"gelu{s}"), sem(f"h_turned{s}"), sem(f"ht_ready{s}")
        c.o_mm, c.o_ready, c.o_out = sem(f"o_mm{s}"), sem(f"o_ready{s}"), sem(f"o_out{s}")
        c.tag_kept, c.tags = sem(f"tag_kept{s}"), sem(f"tags{s}")
        c.ps = ps[:, 4 * s:4 * s + 4, :]
        cs.append(c)
    base_in = sem("base_in")
    N = TILES // 2
    warm = sb("warm", [P, N])
    with nc.Block() as block:
        @block.sync
        def _(sp):
            def load(c, it):
                sp.dma_start(c.x[:, :], xs_d[bass.ds(it * (2 * P) + c.s * P, P), :]).then_inc(c.x_in, 16)

            for c in cs:
                load(c, 0)
            sp.dma_start(k.xn[:, :, 0:D], base_d.rearrange("c r n -> r c n")).then_inc(base_in, 16)
            with sp.Fori(1, N) as it:
                for c in cs:
                    sp.wait_ge(c.x_turned, it)
                    sp.nop(nofuse=True)
                    sp.wait_ge(c.tag_kept, it)
                    sp.nop(nofuse=True)
                    load(c, it)
            sp.wait_ge(base_in, 16)

        @block.gpsimd
        def _(g):
            def body(it, first):
                for c in cs:
                    g.wait_ge(c.tag_kept, it + 1)
                    if not first:
                        g.wait_ge(c.o_out, it * 16)
                    g.nop(nofuse=True)
                    g.tensor_copy(c.to[:, :], c.tag[:, 0:1]).then_inc(c.tags, 1)
                    g.tensor_copy(c.weight[:, :], c.tag[:, 1:2]).then_inc(c.tags, 1)
                for c in cs:
                    g.wait_ge(c.tags, it * 2 + 2)
                    g.wait_ge(c.o_ready, it + 1)
                    g.nop(nofuse=True)
                    g.indirect_dma_start(weighted_d, bass.IndirectOffsetOnAxis(ap=c.to[:, 0:1], axis=0),
                                         c.o[:, :], None).then_inc(c.o_out, 16)

            body(0, True)
            with g.Fori(1, N) as it:
                body(it, False)
            for c in cs:
                g.wait_ge(c.o_out, 16 * N)

        @block.tensor
        def _(t):
            t.wait_ge(ew_loaded, 16 * 2 * E)
            t.wait_ge(eb_loaded, 32)

            def turn_x(c, it):
                t.wait_ge(c.x_in, it * 16 + 16)
                for f in range(2):
                    tr = t.transpose(c.ps[:, 0, P * f:P * f + P], c.x[:, P * f:P * f + P], k.ident[:, :])
                tr.then_inc(c.x_turned, 1)

            def body(it, first, last):
                experts_of = []
                for c in cs:
                    e = t.value_load(tile_expert[0:1, bass.ds(it * 2 + c.s, 1)], min_val=0, max_val=E - 1)
                    experts_of.append(e)
                    t.matmul(c.ps[:, 1, :], ones_bf[0:3, :], eb1[:, bass.ds(e, 1), :].rearrange("i o n -> i (o n)"),
                             start=True, stop=False)
                    t.wait_ge(c.xt_ready, it + 1)
                    for f in range(2):
                        mm = t.matmul(c.ps[:, 1, :], c.xt[:, f, :],
                                      ew1[:, bass.ds(e, 1), f, :].rearrange("p o n -> p (o n)"),
                                      start=False, stop=(f == 1))
                    mm.then_inc(c.h_mm, 1)
                for c in cs:
                    if not last:
                        turn_x(c, it + 1)
                    t.wait_ge(c.gelu, it + 1)
                    for f in range(4):
                        tr = t.transpose(c.ps[:, 2, P * f:P * f + P], c.h[:, P * f:P * f + P], k.ident[:, :])
                    tr.then_inc(c.h_turned, 1)
                for c, e in zip(cs, experts_of):
                    if not first:
                        t.wait_ge(c.o_ready, it)
                    t.matmul(c.ps[:, 3, 0:D], ones_bf[0:3, :], eb2[:, bass.ds(e, 1), :].rearrange("i o n -> i (o n)"),
                             start=True, stop=False)
                    t.wait_ge(c.ht_ready, it + 1)
                    for f in range(4):
                        mm = t.matmul(c.ps[:, 3, 0:D], c.ht[:, P * f:P * f + P],
                                      ew2[:, bass.ds(e, 1), f, :].rearrange("p o n -> p (o n)"),
                                      start=False, stop=(f == 3))
                    mm.then_inc(c.o_mm, 1)

            for c in cs:
                turn_x(c, 0)
            body(0, True, False)
            with t.Fori(1, N - 1) as it:
                body(it, False, False)
            body(N - 1, False, True)

        @block.scalar
        def _(a):
            with a.Fori(0, N) as it:
                a.activation(warm[:, bass.ds(it, 1)], k.ones[:, 0:1], ACT.Gelu)
                for c in cs:
                    a.wait_ge(c.h_mm, it + 1)
                    a.activation(c.h[:, :], c.ps[:, 1, :], ACT.Gelu).then_inc(c.gelu, 1)

        @block.vector
        def _(v):
            def turned_x(c, it, first):
                v.wait_ge(c.x_turned, it + 1)
                if not first:
                    v.wait_ge(c.h_mm, it)
                v.tensor_copy(c.xt[:, :, :].rearrange("p f n -> p (f n)"), c.ps[:, 0, 0:2 * P]).then_inc(c.xt_ready, 1)
                if not first:
                    v.wait_ge(c.tags, it * 2)
                v.tensor_copy(c.tag[:, :], c.x[:, D:XW]).then_inc(c.tag_kept, 1)

            def body(it, first, last):
                for c in cs:
                    if not last:
                        turned_x(c, it + 1, False)
                    v.wait_ge(c.h_turned, it + 1)
                    v.tensor_copy(c.ht[:, :], c.ps[:, 2, :]).then_inc(c.ht_ready, 1)
                for c in cs:
                    v.wait_ge(c.tags, it * 2 + 2)
                    if not first:
                        v.wait_ge(c.o_out, it * 16)
                    v.wait_ge(c.o_mm, it + 1)
                    v.tensor_scalar(c.o[:, :], c.ps[:, 3, 0:D], c.weight[:, :], None, ALU.mult).then_inc(c.o_ready, 1)

            for c in cs:
                turned_x(c, 0, True)
            body(0, True, False)
            with v.Fori(1, N - 1) as it:
                body(it, False, False)
            body(N - 1, False, True)

    taken = ew1[0:R, :, :, :].rearrange("p e f n -> p (e f n)")
    got = [[taken[:, (2 * b + n) * J * D:(2 * b + n + 1) * J * D] for n in range(2)] for b in range(NB)]
    got_in = [sem(f"got_in{b}") for b in range(NB)]
    added, stored = sem("added"), sem("out_stored")
    out_rows = out.rearrange("b t n -> (b t) n")
    last_rows = NT - (J - 1) * R
    with nc.Block() as block:
        def load(eng, b, n):
            rows = (n * COLS + J * b) * R
            eng.dma_start(got[b][n].rearrange("p (j n) -> p j n", j=J),
                          weighted_d[rows:rows + J * R, :].rearrange("(j p) n -> p j n", p=R)).then_inc(got_in[b], 16)

        @block.sync
        def _(sp):
            for b in range(NB):
                load(sp, b, 0)
            sp.wait_ge(stored, 16 * 2 * NB)

        @block.vector
        def _(v):
            for b in range(NB):
                sums = k.xn[:, J * b:J * b + J, 0:D]
                v.wait_ge(got_in[b], 32)
                for n in range(2):
                    v.tensor_tensor(sums, got[b][n].rearrange("p (j n) -> p j n", j=J), sums, ALU.add)\
                        .then_inc(added, 1)
                    if n == 0:
                        v.wait_ge(added, 2 * b + 1)

        @block.scalar
        def _(a):
            for b in range(NB):
                load(a, b, 1)
            for b in range(NB):
                a.wait_ge(added, 2 * b + 2)
                start = NT * b
                a.dma_start(out_rows[start:start + (J - 1) * R, :].rearrange("(j p) n -> p j n", p=R),
                            k.xn[:, J * b:J * b + J - 1, 0:D]).then_inc(stored, 16)
                start += (J - 1) * R
                a.dma_start(out_rows[start:start + last_rows, :], k.xn[0:last_rows, J * b + J - 1, 0:D])\
                    .then_inc(stored, 16)



def shape_constants():
    f = np.float32
    t = {}
    t["ident"] = np.eye(P, dtype=f)
    y, x = np.meshgrid(np.arange(HP), np.arange(HP), indexing="ij")
    omega = (f(1.0) / f(10000.0) ** (np.arange(D // 4, dtype=f) / f(D // 4 - 1))).astype(f)
    ya = (y.reshape(-1)[:, None].astype(f) * omega[None]).astype(f)
    xa = (x.reshape(-1)[:, None].astype(f) * omega[None]).astype(f)
    pe = np.concatenate((np.sin(xa), np.cos(xa), np.sin(ya), np.cos(ya)), axis=1).astype(f)
    t["pos"] = np.ascontiguousarray(pe[np.arange(NPB) % NP].reshape(J, RP, D).transpose(1, 0, 2))
    theta = (f(1.0) / f(10000.0) ** (f(2.0) * np.arange(DH // 2, dtype=f) / f(DH))).astype(f)
    ang = (np.arange(T, dtype=f)[None, :] * theta[(np.arange(P) % DH) // 2][:, None]).astype(f)
    t["cos"], t["sin"] = np.cos(ang).astype(f), np.sin(ang).astype(f)
    rot = np.zeros((P, P), f)
    for i in range(0, P, 2):
        rot[i + 1, i], rot[i, i + 1] = -1.0, 1.0
    t["rot"] = rot
    hm = np.zeros((P, QH), f)
    hm[np.arange(P), (np.arange(P) // DH) % QH] = 1.0
    t["head_mask"] = hm
    vm = np.zeros((GK, H), f)
    for h in range(H):
        r = h % GH if h < GH * (G - 1) else GH - 1
        vm[T * r:T * (r + 1), h] = 1.0
    t["value_mask"] = vm
    causal = np.zeros((P, H, T), f)
    for o in (0, 64):
        q, s = np.arange(T)[:, None], np.arange(T)[None]
        causal[o:o + T] = np.where(s <= q, 0.0, -1e10).astype(f)[:, None, :]
    t["causal"] = causal.reshape(P, HT)
    t["rank"] = np.ascontiguousarray(np.broadcast_to((E - np.arange(E)).astype(f)[None], (R, E)))
    t["upto"] = np.triu(np.ones((R, R), f), 1)
    valid = np.ones((R, COLS), f)
    valid[NT - (J - 1) * R:, J - 1::J] = 0.0
    t["valid"] = valid
    spare = np.zeros((R, 2, COLS), f)
    for n in range(2):
        spare[:, n, :] = (1.0 - valid) * (SLOTS + n * COLS + np.arange(COLS))
    t["spare"] = spare
    t["row_ids"] = ((np.arange(2)[None, :, None] * COLS + np.arange(COLS)[None, None]) * R
                    + np.arange(R)[:, None, None]).astype(f)
    t["filler"] = np.zeros((P, 2, XW), f)
    t["filler"][:, :, D] = 2 * COLS * R + np.arange(2)[None] * P + np.arange(P)[:, None]
    t["tile_no"] = np.arange(TILES, dtype=f)[None]
    return t


def kernel(**inputs):
    import concourse.bacc as bacc
    from concourse.bass_utils import run_bass_kernel_spmd

    a = {n: np.asarray(v) for n, v in inputs.items()}
    nc = bacc.Bacc("TRN2", target_bir_lowering=False, num_devices=1)
    arrays = {}

    def give(name, array):
        array = np.ascontiguousarray(array)
        name = "in_" + name
        arrays[name] = array
        return nc.dram_tensor(name, array.shape, mybir.dt.from_np(array.dtype), kind="ExternalInput").ap()

    def columns(v, n):
        return v.reshape(n, P).T

    d, t = Bag(), shape_constants()
    d.ident, d.pos, d.cos, d.sin, d.rot = (give(n, t[n]) for n in ("ident", "pos", "cos", "sin", "rot"))
    d.head_mask, d.value_mask, d.causal = (give(n, t[n]) for n in ("head_mask", "value_mask", "causal"))
    d.rank, d.upto, d.valid, d.spare, d.tile_no = (give(n, t[n]) for n in ("rank", "upto", "valid", "spare", "tile_no"))
    d.row_ids, d.filler = give("row_ids", t["row_ids"]), give("filler", t["filler"])
    x = a["x"].reshape(B, C, HP, PATCH, HP, PATCH)
    d.x = give("x", x.transpose(3, 5, 1, 0, 2, 4).reshape(FP, B * NP))
    d.cls, d.cls_pos = give("cls", a["L0_tok_cls_token"].reshape(D)), give("cls_pos", a["L0_tok_cls_pos_embedding"].reshape(D))
    d.ln1_g, d.ln1_b = give("ln1_g", columns(a["L0_tok_ln1_g"], KF)), give("ln1_b", columns(a["L0_tok_ln1_b"], KF))
    d.W, d.tok_bias = give("W", a["L0_tok_W"]), give("tok_bias", a["L0_tok_bias"])
    d.ln2_g, d.ln2_b = give("ln2_g", a["L0_tok_ln2_g"]), give("ln2_b", a["L0_tok_ln2_b"])
    d.attn_w = [[give(f"L0_{n}", a[f"L0_attn_{n}"].T) for n in ("wq", "wk", "wv", "wp")],
                [give(f"L1_{n}", a[f"L1_attn_{n}"]) for n in ("Wq", "Wk", "Wv", "Wo")]]
    d.attn_b = [[give(f"L{l}_b{n}", columns(a[f"L{l}_attn_b{n}"], 2)) for n in "qkv"] for l in range(2)]
    d.attn_ob = [give("L0_bp", a["L0_attn_bp"]), give("L1_bo", a["L1_attn_bo"])]
    d.w1T, d.w2T = give("w1T", a["L0_ffn_w1"].T), give("w2T", a["L0_ffn_w2"].T)
    conv = np.concatenate((a["L0_ffn_conv_w"].reshape(FH, 3), a["L0_ffn_conv_b"].reshape(FH, 1)), axis=1)
    d.conv = give("conv", conv.reshape(MH, P, 4).transpose(1, 0, 2))
    d.relT = give("relT", a["L1_attn_rel_bias"].T)
    d.Wr, d.br = give("Wr", a["L1_ffn_Wr"]), give("br", a["L1_ffn_br"])
    d.W1, d.b1, d.W2, d.b2 = (give(n, a[f"L1_ffn_{n}"]) for n in ("W1", "b1", "W2", "b2"))
    out = nc.dram_tensor("out", (B, T, D), F32, kind="ExternalOutput").ap()
    build(nc, d, out)
    r = run_bass_kernel_spmd(nc, [arrays], core_ids=[0])
    return r.results[0]["out"]
```

```python
from contextlib import ExitStack

import numpy as np
import concourse.bass as bass
from concourse import mybir

F32 = mybir.dt.float32
BF16 = mybir.dt.bfloat16
U32 = mybir.dt.uint32
I32 = mybir.dt.int32
ALU = mybir.AluOpType
ACT = mybir.ActivationFunctionType
AX = mybir.AxisListType

P = 128
B, C, IMG, PATCH = 64, 3, 96, 16
HP = IMG // PATCH
NP = HP * HP
T = NP + 1
D = 256
FP = C * PATCH * PATCH
KF = FP // P
H, DH = 16, 16
QH = 64 // DH
FH = 1024
MH = FH // P
E, EH = 16, 512
EPS = 1e-5
MAGIC = 1.5 * 2.0 ** 23

NI = 8
NB = B // NI
CTX = 2
ITERS = NB // CTX
NT = NI * T
J = 3
R = (NT + J - 1) // J
NTP = J * R
NPB = NI * NP
RP = NPB // J
NPAIR = NI // 2
HT = H * T
GH = 3
G = 6
GK = GH * T
PR = 64 + T
Y0 = 2 * PR
DV = DH + 1
COLS = NB * J
PAIRS = 2 * B * T
TILES = (PAIRS + E * (P - 1)) // P
SLOTS = TILES * P
NROWS = SLOTS + P
XW = D + 2


class Bag:
    pass


def phase(nc, fn, *args):
    with ExitStack() as c:
        used = []

        def sem(name):
            used.append(c.enter_context(nc.semaphore(name)))
            return used[-1]
        fn(nc, c, sem, *args)
        numbers = sorted(s.num for s in used)
        with nc.Block() as block:
            @block.gpsimd
            def _(g):
                start = 0
                for i in range(1, len(numbers) + 1):
                    if i == len(numbers) or numbers[i] != numbers[i - 1] + 1:
                        g.sem_clear(range(numbers[start], numbers[i - 1] + 1))
                        start = i


def group_col(g):
    return GK * g if g < G - 1 else HT - GK


def build(nc, d, out):
    h0 = nc.dram_tensor("tokens_d", (B * T + P, D), F32, kind="Internal").ap()
    base_d = nc.dram_tensor("base_d", (COLS, R, D), F32, kind="Internal").ap()
    xs_d = nc.dram_tensor("xs_d", (NROWS, XW), F32, kind="Internal").ap()
    weighted_d = nc.dram_tensor("weighted_d", (2 * COLS * R + 2 * P, D), F32, kind="Internal").ap()
    b1_d = nc.dram_tensor("b1_d", (3, E * EH), BF16, kind="Internal").ap()
    b2_d = nc.dram_tensor("b2_d", (3, E * D), BF16, kind="Internal").ap()
    with ExitStack() as ctx:
        def sb(name, shape, dt=F32):
            return ctx.enter_context(nc.sbuf_tensor(name, shape, dt))
        k = Bag()
        k.ident = sb("ident", [P, P])
        k.ident_bf = sb("ident_bf", [P, P], BF16)
        k.ones = sb("ones", [P, P])
        k.xn = sb("xn", [R, COLS, XW])
        k.logits = sb("logits", [R, COLS, E])
        k.ps = ctx.enter_context(nc.psum_tensor("ps", [P, 8, 512], F32))
        with ExitStack() as tower_ctx:
            def sbt(name, shape, dt=F32):
                return tower_ctx.enter_context(nc.sbuf_tensor(name, shape, dt))
            k.half = sbt("half", [P, J])
            k.filler = sbt("filler", [P, 2, XW])
            k.attn = []
            for l in range(2):
                a = Bag()
                a.w = sbt(f"attn_w{l}", [P, 4, 2, D])
                a.qb, a.kb, a.vb = (sbt(f"attn_{n}b{l}", [P, 2]) for n in "qkv")
                a.ob = sbt(f"attn_ob{l}", [P, D])
                a.bias = sbt(f"score_bias{l}", [P, HT])
                k.attn.append(a)
            k.rot = sbt("rot", [P, P])
            k.cos, k.sin = sbt("cos", [P, T]), sbt("sin", [P, T])
            k.head_mask = sbt("head_mask", [P, QH])
            k.value_mask = sbt("value_mask", [GK, H])
            k.w1 = sbt("w1", [P, 2, FH], BF16)
            k.w2 = sbt("w2", [P, MH, D], BF16)
            k.wunit = sbt("wunit", [P, 2])
            k.conv = sbt("conv", [P, MH, 4])
            k.wr = sbt("wr", [P, 2, E])
            k.br = sbt("br", [P, E])
            phase(nc, setup_embed, d, k, h0, xs_d, weighted_d, b1_d, b2_d)
            phase(nc, tower, k, h0, base_d, xs_d)
        phase(nc, experts, d, k, base_d, xs_d, weighted_d, b1_d, b2_d, out)



def setup_embed(nc, ctx, sem, d, k, h0, xs_d, weighted_d, b1_d, b2_d):
    def sb(name, shape, dt=F32):
        return ctx.enter_context(nc.sbuf_tensor(name, shape, dt))

    wp = sb("wp", [P, KF, D])
    wc = sb("wc", [P, KF, D + 1])
    g1, b1 = sb("g1", [P, KF]), sb("b1", [P, KF])
    mean_w = sb("mean_w", [P, P])
    bias_row = sb("bias_row", [1, D])
    out_bias = sb("out_bias", [RP, D])
    g2, b2, pos = sb("g2", [RP, D]), sb("b2", [RP, D]), sb("pos", [RP, J, D])
    cls, cls_pos = sb("cls", [B, D]), sb("cls_pos", [B, D])
    zero = sb("zero", [P, D])
    rel_rev = sb("rel_rev", [P, H, T])
    wt = [sb("w1_raw", [P, 2 * FH]), sb("w2_raw", [P, MH * D])]
    wq = [sb("w1_round", [P, 2 * FH]), sb("w2_round", [P, MH * D])]
    wsum, wscale = sb("wsum", [P, 2]), sb("wscale", [P, 2])
    eb = [sb("eb1", [E, EH]), sb("eb2", [E, D])]
    ebr = [sb("eb1_rest", [E, EH]), sb("eb2_rest", [E, D])]
    ebp = [[sb(f"eb{n + 1}_part{i}", [E, (EH, D)[n]], BF16) for i in range(3)] for n in range(2)]

    rows = lambda v, n: v.unsqueeze(0).broadcast_to([n, D])
    front_loads = [
        (wp[:, :, :], d.W.rearrange("(k p) n -> p k n", p=P)), (g1[:, :], d.ln1_g), (b1[:, :], d.ln1_b),
        (bias_row[:, :], d.tok_bias.unsqueeze(0))]
    mid_loads = [
        (wt[0][:, :].rearrange("p (k n) -> p k n", k=2), d.w1T.rearrange("(k p) n -> p k n", p=P)),
        (wt[1][:, :].rearrange("p (k n) -> p k n", k=MH), d.w2T.rearrange("(k p) n -> p k n", p=P)),
        (g2[:, :], rows(d.ln2_g, RP)), (b2[:, :], rows(d.ln2_b, RP)), (pos[:, :, :], d.pos),
        (cls[:, :], rows(d.cls, B)), (cls_pos[:, :], rows(d.cls_pos, B)), (eb[0][:, :], d.b1), (eb[1][:, :], d.b2),
        (k.ident[:, :], d.ident), (k.filler[:, :, :], d.filler)]
    late_loads = [
        (k.rot[:, :], d.rot), (k.cos[:, :], d.cos), (k.sin[:, :], d.sin), (k.head_mask[:, :], d.head_mask),
        (k.value_mask[:, :], d.value_mask), (k.conv[:, :, :], d.conv),
        (k.wr[:, :, :], d.Wr.rearrange("(k p) n -> p k n", p=P)), (k.br[:, :], d.br.unsqueeze(0).broadcast_to([P, E])),
        (k.attn[0].bias[:, :], d.causal)]
    for l in range(2):
        for n in range(4):
            late_loads.append((k.attn[l].w[:, n, :, :], d.attn_w[l][n].rearrange("(k p) n -> p k n", p=P)))
        for dst, src in zip((k.attn[l].qb, k.attn[l].kb, k.attn[l].vb), d.attn_b[l]):
            late_loads.append((dst[:, :], src))
        late_loads.append((k.attn[l].ob[:, :], rows(d.attn_ob[l], P)))

    front_loaded, mid_loaded, late_loaded = sem("front_loaded"), sem("mid_loaded"), sem("late_loaded")
    rel_loaded, filled = sem("rel_loaded"), sem("filled")
    ones_set, zero_set, rel_clear = sem("ones_set"), sem("zero_set"), sem("rel_clear")
    gained, mean_mm, centred, bias_mm = sem("gained"), sem("mean_mm"), sem("centred"), sem("bias_mm")
    pos_done, cls_done, rel_done = sem("pos_done"), sem("cls_done"), sem("rel_done")
    wsum_done, wsum_mm, wq_step = sem("wsum_done"), sem("wsum_mm"), sem("wq_step")
    split, split_out = sem("split"), sem("split_out")
    q_scaled = sem("q_scaled")

    def start_loads(sp):
        for dst, src in front_loads:
            sp.dma_start(dst, src).then_inc(front_loaded, 16)

    def fill_dram(sp):
        sp.wait_ge(rel_clear, 1)
        rel = bass.AP(d.relT.tensor, 128 - (T - 1), [[1, T], [2 * 128 + 1, H], [1, T]])
        for o in (0, 64):
            sp.dma_start(rel_rev[o:o + T, :, :], rel).then_inc(rel_loaded, 16)
        sp.wait_ge(zero_set, 1)
        sp.dma_start(h0[B * T:B * T + P, :], zero[:, :]).then_inc(filled, 16)
        sp.dma_start(weighted_d[0:2 * COLS * R, :].rearrange("(a b) n -> a b n", b=J * R)[:, J * R - 1, :],
                     zero[0:2 * NB, :]).then_inc(filled, 16)

    def store_small(sp):
        sp.wait_ge(cls_done, 1)
        sp.dma_start(h0[0:B * T, :].rearrange("(b t) n -> b t n", t=T)[:, 0, :], cls[:, :]).then_inc(filled, 16)
        for n, dst in enumerate((b1_d, b2_d)):
            for i in range(3):
                sp.wait_ge(split, 5 * n + (1, 3, 5)[i])
                sp.dma_start(dst[i, :].rearrange("(e n) -> e n", e=E), ebp[n][i][:, :]).then_inc(split_out, 16)

    def start_gpsimd(g):
        g.memset(mean_w[:, :], 1.0 / FP).then_inc(ones_set, 1)
        g.memset(k.ones[:, :], 1.0).then_inc(ones_set, 1)
        g.memset(k.half[:, :], -0.5).then_inc(ones_set, 1)
        g.memset(rel_rev[:, :, :], 0.0).then_inc(rel_clear, 1)
        g.memset(zero[:, :], 0.0).then_inc(zero_set, 1)

    def reverse_rel(g):
        g.wait_ge(rel_loaded, 32)
        rr = rel_rev[:, :, :]
        back = bass.AP(rr.tensor, T - 1, [list(rr.ap[0]), [T, H], [-1, T]])
        g.tensor_copy(k.attn[1].bias[:, :].rearrange("p (h t) -> p h t", h=H), back).then_inc(rel_done, 1)

    def start_vector(v):
        v.wait_ge(front_loaded, 16 * len(front_loads))
        for i in range(KF):
            v.tensor_scalar(wc[:, i, 0:D], wp[:, i, :], g1[:, i:i + 1], None, ALU.mult).then_inc(gained, 1)
        v.memset(wc[:, :, D:D + 1], 1.0).then_inc(gained, 1)
        v.wait_ge(mean_mm, 1)
        v.tensor_tensor(wc[:, :, 0:D], wc[:, :, 0:D], k.ps[:, 0, 0:D].unsqueeze(1).broadcast_to([P, KF, D]),
                        ALU.subtract).then_inc(centred, 1)
        v.wait_ge(bias_mm, 1)
        v.tensor_copy(out_bias[:, :], k.ps[0:RP, 7, 0:D]).then_inc(centred, 1)
        v.wait_ge(mid_loaded, 16 * len(mid_loads))
        for n in range(2):
            v.tensor_reduce(wsum[:, n:n + 1], wt[n][:, :], AX.X, ALU.add, apply_absolute_value=True)\
                .then_inc(wsum_done, 1)
        v.tensor_tensor(pos[:, :, :], pos[:, :, :], b2[:, :].unsqueeze(1).broadcast_to([RP, J, D]), ALU.add)\
            .then_inc(pos_done, 1)

    def prepare_ternary(v):
        v.wait_ge(wsum_mm, 1)
        v.tensor_scalar(wsum[:, :], k.ps[:, 7, 0:2], 1.0 / (D * FH), 1e-5, ALU.mult, ALU.max).then_inc(wq_step, 1)
        v.wait_ge(wq_step, 1)
        v.reciprocal(wscale[:, :], wsum[:, :]).then_inc(wq_step, 1)
        v.wait_ge(wq_step, 2)
        v.reciprocal(k.wunit[:, :], wscale[:, :]).then_inc(wq_step, 1)

    def small_vector(v):
        v.tensor_add(cls[:, :], cls[:, :], cls_pos[:, :]).then_inc(cls_done, 1)
        v.tensor_copy(k.ident_bf[:, :], k.ident[:, :])
        for n in range(2):
            v.tensor_copy(ebp[n][0][:, :], eb[n][:, :]).then_inc(split, 1)
            v.wait_ge(split, 5 * n + 1)
            v.tensor_tensor(ebr[n][:, :], eb[n][:, :], ebp[n][0][:, :], ALU.subtract).then_inc(split, 1)
            v.wait_ge(split, 5 * n + 2)
            v.tensor_copy(ebp[n][1][:, :], ebr[n][:, :]).then_inc(split, 1)
            v.wait_ge(split, 5 * n + 3)
            v.tensor_tensor(ebr[n][:, :], ebr[n][:, :], ebp[n][1][:, :], ALU.subtract).then_inc(split, 1)
            v.wait_ge(split, 5 * n + 4)
            v.tensor_copy(ebp[n][2][:, :], ebr[n][:, :]).then_inc(split, 1)

    TCOLS = 2 * FH // ITERS

    def ternary(v, it):
        part = bass.ds(it * TCOLS, TCOLS)
        w_done = (k.w1[:, :, :].rearrange("p k n -> p (k n)"), k.w2[:, :, :].rearrange("p k n -> p (k n)"))
        for n in range(2):
            v.tensor_scalar(wq[n][:, part], wt[n][:, part], wscale[:, n:n + 1], MAGIC, ALU.mult, ALU.add)\
                .then_inc(wq_step, 1)
        v.wait_ge(wq_step, it * 6 + 5)
        for n in range(2):
            v.tensor_scalar(wq[n][:, part], wq[n][:, part], MAGIC, -1.0, ALU.subtract, ALU.max).then_inc(wq_step, 1)
        v.wait_ge(wq_step, it * 6 + 7)
        for n in range(2):
            v.tensor_scalar(w_done[n][:, part], wq[n][:, part], 1.0, None, ALU.min).then_inc(wq_step, 1)

    def start_tensor(t):
        t.wait_ge(ones_set, 3)
        t.wait_ge(gained, KF)
        for i in range(KF):
            mm = t.matmul(k.ps[:, 0, 0:D], mean_w[:, :], wc[:, i, 0:D], start=(i == 0), stop=(i == KF - 1))
        mm.then_inc(mean_mm, 1)
        for i in range(KF):
            t.matmul(k.ps[0:RP, 7, 0:D], b1[:, i:i + 1].broadcast_to([P, RP]), wp[:, i, :],
                     start=(i == 0), stop=False)
        t.matmul(k.ps[0:RP, 7, 0:D], k.ones[0:1, 0:RP], bias_row[:, :], start=False, stop=True)\
            .then_inc(bias_mm, 1)

    cs = []
    for s in range(CTX):
        c = Bag()
        c.s = s
        c.x = sb(f"x{s}", [P, KF, NPB])
        c.xx = sb(f"xx{s}", [P, KF, NPB])
        c.z = sb(f"z{s}", [RP, J, D])
        c.tok = sb(f"tok{s}", [RP, J, D])
        c.mean, c.var, c.rstd = (sb(f"{n}{s}", [RP, J]) for n in ("e_mean", "e_var", "e_rstd"))
        c.st, c.mv = sb(f"e_st{s}", [RP, J, 6]), sb(f"e_mv{s}", [RP, J, 2])
        c.x_loaded, c.squared, c.prod_mm = sem(f"x_loaded{s}"), sem(f"squared{s}"), sem(f"prod_mm{s}")
        c.norm, c.powers, c.stored = sem(f"e_norm{s}"), sem(f"e_powers{s}"), sem(f"stored{s}")
        c.paired = sem(f"paired{s}")
        c.z_done, c.tok_done = sem(f"z_done{s}"), sem(f"tok_done{s}")
        cs.append(c)
    ps = k.ps
    NORM = 9
    PIECES = 10

    def pieces(j):
        r, end = RP * j, RP * (j + 1)
        while r < end:
            n = min(end, (r // NP + 1) * NP) - r
            yield r - RP * j, n, r // NP, r % NP
            r += n

    with nc.Block() as block:
        @block.sync
        def _(sp):
            def load(c, it):
                sp.dma_start(c.x[:, :, :], d.x[:, bass.ds(it * (CTX * NPB) + c.s * NPB, NPB)]
                             .rearrange("(k p) n -> p k n", p=P)).then_inc(c.x_loaded, 16)

            start_loads(sp)
            for c in cs:
                load(c, 0)
            for dst, src in mid_loads:
                sp.dma_start(dst, src).then_inc(mid_loaded, 16)
            fill_dram(sp)

            def body(it, last, between=lambda: None):
                for c in cs:
                    if not last:
                        sp.wait_ge(c.prod_mm, it + 1)
                        load(c, it + 1)
                between()
                for c in cs:
                    sp.wait_ge(c.tok_done, it + 1)
                    for j in range(J):
                        for row, n, img, s in pieces(j):
                            sp.dma_start(h0[bass.ds(it * (CTX * NI * T) + ((c.s * NI + img) * T + 1 + s), n), :],
                                         c.tok[row:row + n, j, :]).then_inc(c.stored, 16)

            body(0, False, lambda: store_small(sp))
            with sp.Fori(1, ITERS - 1) as it:
                body(it, False)
            body(ITERS - 1, True)
            for c in cs:
                sp.wait_ge(c.stored, 16 * PIECES * ITERS)
            sp.wait_ge(filled, 16 * 3)
            sp.wait_ge(split_out, 16 * 6)

        @block.scalar
        def _(a):
            def square(c, it):
                a.wait_ge(c.x_loaded, it * 16 + 16)
                for i in range(KF):
                    a.activation(c.xx[:, i, :], c.x[:, i, :], ACT.Square).then_inc(c.squared, 1)

            square(cs[0], 0)
            for dst, src in late_loads:
                a.dma_start(dst, src).then_inc(late_loaded, 16)
            square(cs[1], 0)
            with a.Fori(1, ITERS) as it:
                for c in cs:
                    square(c, it)
            a.wait_ge(late_loaded, 16 * len(late_loads))
            for l in range(2):
                a.mul(k.attn[l].qb[:, :], k.attn[l].qb[:, :], DH ** -0.5).then_inc(q_scaled, 1)

        @block.tensor
        def _(t):
            def products(c, it, first):
                t.wait_ge(c.x_loaded, it * 16 + 16)
                if not first:
                    t.wait_ge(c.z_done, it)
                for j in range(J):
                    for i in range(KF):
                        t.matmul(ps[0:RP, 4 * c.s + j, 0:D + 1], c.x[:, i, RP * j:RP * j + RP], wc[:, i, :],
                                 start=(i == 0), stop=(i == KF - 1))

            def sum_squares(c, it):
                t.wait_ge(c.paired, it + 1)
                for j in range(J):
                    for i in range(KF // 2):
                        mm = t.matmul(ps[0:RP, 4 * c.s + 3, j:j + 1], c.xx[:, i, RP * j:RP * j + RP],
                                      k.ones[:, 0:1], start=(i == 0), stop=(i == KF // 2 - 1))
                mm.then_inc(c.prod_mm, 1)

            start_tensor(t)
            t.wait_ge(centred, 1)
            t.wait_ge(gained, KF + 1)
            products(cs[0], 0, True)
            sum_squares(cs[0], 0)
            products(cs[1], 0, True)
            t.wait_ge(centred, 2)
            t.wait_ge(wsum_done, 2)
            t.matmul(k.ps[:, 7, 0:2], k.ones[:, :], wsum[:, :], start=True, stop=True).then_inc(wsum_mm, 1)
            t.wait_ge(wq_step, 1)
            sum_squares(cs[1], 0)
            with t.Fori(1, ITERS) as it:
                for c in cs:
                    products(c, it, False)
                    sum_squares(c, it)

        @block.gpsimd
        def _(g):
            def pair(c, it, first):
                g.wait_ge(c.squared, it * KF + KF)
                g.tensor_tensor(c.xx[:, 0:KF // 2, :], c.xx[:, 0:KF // 2, :], c.xx[:, KF // 2:KF, :], ALU.add)\
                    .then_inc(c.paired, 1)

            def power(c, it, n):
                g.wait_ge(c.norm, it * NORM + (4, 7)[n])
                g.tensor_tensor(c.rstd[:, :], c.var[:, :], k.half[0:RP, :], ALU.pow).then_inc(c.powers, 1)

            def block_steps(c, it, first, then):
                power(c, it, 0)
                power(c, it, 1)
                then()
                g.wait_ge(c.norm, it * NORM + 9)
                if not first:
                    g.wait_ge(c.stored, it * (16 * PIECES))
                g.tensor_tensor(c.tok[:, :, :], c.z[:, :, :], pos[:, :, :], ALU.add).then_inc(c.tok_done, 1)

            a, b = cs
            start_gpsimd(g)
            pair(a, 0, True)
            g.wait_ge(pos_done, 1)
            block_steps(a, 0, True, lambda: pair(b, 0, True))
            block_steps(b, 0, True, lambda: pair(a, 1, False))
            reverse_rel(g)
            with g.Fori(1, ITERS - 1) as it:
                block_steps(a, it, False, lambda: pair(b, it, False))
                block_steps(b, it, False, lambda: pair(a, it + 1, False))
            last = ITERS - 1
            block_steps(a, last, False, lambda: pair(b, last, False))
            block_steps(b, last, False, lambda: None)

        @block.vector
        def _(v):
            def variance(c, it):
                sums = ps[0:RP, 4 * c.s:4 * c.s + J, D:D + 1].rearrange("p j o -> p (j o)")
                squares = ps[0:RP, 4 * c.s + 3, 0:J]
                v.wait_ge(c.prod_mm, it + 1)
                v.tensor_scalar(c.mean[:, :], sums, 1.0 / FP, None, ALU.mult).then_inc(c.norm, 1)
                v.wait_ge(c.norm, it * NORM + 1)
                v.scalar_tensor_tensor(c.mean[:, :], c.mean[:, :], -1.0, c.mean[:, :], ALU.mult, ALU.mult)\
                    .then_inc(c.norm, 1)
                v.wait_ge(c.norm, it * NORM + 2)
                v.scalar_tensor_tensor(c.var[:, :], squares, 1.0 / FP, c.mean[:, :], ALU.mult, ALU.add)\
                    .then_inc(c.norm, 1)
                v.wait_ge(c.norm, it * NORM + 3)
                v.tensor_scalar(c.var[:, :], c.var[:, :], EPS, None, ALU.add).then_inc(c.norm, 1)

            def project(c, it, first):
                v.wait_ge(c.powers, it * 2 + 1)
                if not first:
                    v.wait_ge(c.tok_done, it)
                for j in range(J):
                    zj = v.scalar_tensor_tensor(c.z[:, j, :], ps[0:RP, 4 * c.s + j, 0:D], c.rstd[:, j:j + 1],
                                                out_bias[:, :], ALU.mult, ALU.add)
                zj.then_inc(c.z_done, 1)
                v.wait_ge(c.z_done, it + 1)
                for j in range(J):
                    st = v.bn_stats(c.st[:, j, :], c.z[:, j, :])
                st.then_inc(c.norm, 1)
                v.wait_ge(c.norm, it * NORM + 5)
                v.nop(nofuse=True)
                for j in range(J):
                    mv = v.bn_aggr(c.mv[:, j, :], c.st[:, j, :])
                mv.then_inc(c.norm, 1)
                v.wait_ge(c.norm, it * NORM + 6)
                v.tensor_scalar(c.var[:, :], c.mv[:, :, 1:2].rearrange("p j o -> p (j o)"), EPS, None, ALU.add)\
                    .then_inc(c.norm, 1)

            def normalise(c, it):
                v.wait_ge(c.powers, it * 2 + 2)
                for j in range(J):
                    zj = v.tensor_scalar(c.z[:, j, :], c.z[:, j, :], c.mv[:, j, 0:1], c.rstd[:, j:j + 1],
                                         ALU.subtract, ALU.mult)
                zj.then_inc(c.norm, 1)
                v.wait_ge(c.norm, it * NORM + 8)
                v.tensor_tensor(c.z[:, :, :], c.z[:, :, :], g2[:, :].unsqueeze(1).broadcast_to([RP, J, D]), ALU.mult)\
                    .then_inc(c.norm, 1)

            start_vector(v)
            for c in cs:
                variance(c, 0)
                project(c, 0, True)
                if c.s == 0:
                    prepare_ternary(v)
                normalise(c, 0)
            small_vector(v)
            ternary(v, 0)
            with v.Fori(1, ITERS) as it:
                for c in cs:
                    variance(c, it)
                    project(c, it, False)
                    normalise(c, it)
                ternary(v, it)



def tower(nc, ctx, sem, k, h0, base_d, xs_d):
    def sb(name, shape, dt=F32):
        return ctx.enter_context(nc.sbuf_tensor("t_" + name, shape, dt))

    SIGNALS = dict(
        h_loaded=16, base_stored=16,
        ln=16,
        ln_power=4, xt_mm=3, xt=3,
        qk_mm=8, q0=4, rope_mm=4, rope_cos=4, rope_sin=4, rope_sum=4, q1=4, keys=4,
        v_mm=4, v_ev=4, vt_mm=8, values=8,
        score_mm=8, biased=8, row_max=8, shifted=8, prob=8, probt_mm=8, probt=8, pv_mm=8, inv_sum=8, y=8,
        yt_mm=8, yt=8, proj_mm=2, h_bias=2, h_attn=2,
        quant=7,
        xq_mm=1, xq=1, unit_mm=1, unit=1, hid_mm=8, hid=8, mid=8, left=8, right=8, silu=8,
        quant2=13, colmax_mm=1, scale_mm=1, out_mm=3, h_ffn=3,
        logit_mm=1, logit=1, xn_kept=1, base=1)
    filled = sem("filled_slots")

    cs = []
    for s in range(CTX):
        c = Bag()
        c.s, c.sem = s, {n: sem(f"{n}_{s}") for n in SIGNALS}
        c.ps = k.ps[:, 4 * s:4 * s + 4, :]
        c.h, c.hb, c.xh, c.qf = (sb(f"{n}{s}", [R, J, D]) for n in ("h", "hb", "xh", "qf"))
        c.h_in = sb(f"h_in{s}", [R, J, D])
        c.base = c.qf
        c.st, c.mv = sb(f"st{s}", [R, J, 6]), sb(f"mv{s}", [R, J, 2])
        c.var, c.rstd = sb(f"var{s}", [R, J]), sb(f"rstd{s}", [R, J])
        c.xt = sb(f"xt{s}", [P, 2, NTP])
        c.qt = sb(f"qt{s}", [P, 2, NT])
        c.v = sb(f"v{s}", [GK, NI, H, DV])
        c.sc2 = sb(f"sc{s}", [P, 2, HT])
        c.mx2, c.rs = sb(f"mx{s}", [P, 2, H]), sb(f"rs{s}", [P, H])
        c.pt = sb(f"pt{s}", [GK, G, PR])
        c.y = sb(f"y{s}", [P, D])
        c.yt = sb(f"yt{s}", [P, 2, NTP])
        c.qb = sb(f"qb{s}", [R, J, D], BF16)
        c.am, c.unit_in = sb(f"am{s}", [R, J]), sb(f"unit_in{s}", [R, J])
        c.am2, c.unit2 = sb(f"am2{s}", [R, J]), sb(f"unit2{s}", [R, J])
        words = max(4 * NT * 3 + 2 * NI * GK + 2 * NI * QH * T,
                    2 * MH * NTP + MH * NTP // 2 + NTP + NTP)
        region = sb(f"region{s}", [P, words])
        at = [0]

        def take(n, pattern=None, dt=F32, **dims):
            a = region[:, at[0]:at[0] + n]
            at[0] += n
            if dt != F32:
                a = a.bitcast(dt)
            return a.rearrange(pattern, **dims) if pattern else a

        c.qk = take(4 * NT, "p (i t) -> p i t", i=4)
        c.rc = take(4 * NT, "p (i t) -> p i t", i=4)
        c.rn = take(4 * NT, "p (i t) -> p i t", i=4)
        c.vr = take(2 * NI * GK, "p (f i r t) -> p f i r t", f=2, i=NI, r=GH)
        c.kd = take(2 * NI * QH * T, "p (f i o t) -> p f i o t", f=2, i=NI, o=QH)
        at[0] = 0
        c.t0 = take(MH * NTP, "p (m t) -> p m t", m=MH)
        c.a = take(MH * NTP, "p (m t) -> p m t", m=MH)
        c.hq = take(MH * NTP // 2, "p (m t) -> p m t", dt=BF16, m=MH)
        c.xq = take(NTP, "p (f t) -> p f t", dt=BF16, f=2)
        c.unit = take(NTP)
        cs.append(c)

    def wait(eng, c, it, name, n):
        eng.wait_ge(c.sem[name], it * SIGNALS[name] + n)

    OUT_BANK = (2, 3, 0)
    images = "p (i t) -> p i t"
    img_bc = lambda table: table[:, :].unsqueeze(1).broadcast_to([P, NI, T])
    bft = lambda bank: bank.bitcast(BF16)

    LENGTH = dict(project0=28.5, attend0=42.3, ffn=32.6, project1=27.4, attend1=42.4)
    STAGES = tuple(LENGTH)

    def run(eng, stage):
        def stages(c, todo, start=0.0):
            for name, it in todo:
                for point in stage(name, c, it):
                    yield start + LENGTH[name] * point
                start += LENGTH[name]

        def together(*steps):
            steps = list(steps)
            due = [next(g) for g in steps]
            while steps:
                n = due.index(min(due))
                after = next(steps[n], None)
                if after is None:
                    steps.pop(n)
                    due.pop(n)
                else:
                    due[n] = after

        first, last = STAGES[0], STAGES[-1]
        together(stages(cs[0], [(n, 0) for n in STAGES]),
                 stages(cs[1], [(n, 0) for n in STAGES[:-1]], LENGTH[first]))
        with eng.Fori(1, ITERS) as it:
            together(stages(cs[0], [(n, it) for n in STAGES]),
                     stages(cs[1], [(last, it - 1)] + [(n, it) for n in STAGES[:-1]]))
        together(stages(cs[1], [(last, ITERS - 1)]))

    PAIR_SPAN = NPAIR + 2.5

    def sync_program(sp):
        def load(c, it):
            row = it * (CTX * NT) + c.s * NT
            sp.dma_start(c.h_in[:, :, :], h0[bass.ds(row, NTP), :].rearrange("(j p) n -> p j n", p=R))\
                .then_inc(c.sem["h_loaded"], 16)

        def store(c, it):
            wait(sp, c, it, "base", 1)
            sp.dma_start(base_d[bass.ds(it * (CTX * J) + c.s * J, J), :, :].rearrange("j p n -> p j n"),
                         c.base[:, :, :]).then_inc(c.sem["base_stored"], 16)

        a, b = cs

        def body(it, first, last):
            for c in cs:
                if c is b and not first:
                    store(b, it - 1)
                if not last:
                    wait(sp, c, it, "h_bias", 1)
                    load(c, it + 1)
            store(a, it)

        load(a, 0)
        load(b, 0)
        for s in range(2):
            sp.dma_start(xs_d[0:SLOTS, :].rearrange("(a s p) n -> p s a n", s=2, p=P)[:, s, :, :],
                         k.filler[:, s:s + 1, :].broadcast_to([P, TILES // 2, XW])).then_inc(filled, 16)
        sp.dma_start(xs_d[SLOTS:NROWS, :], k.filler[:, 0, :]).then_inc(filled, 16)
        body(0, True, False)
        with sp.Fori(1, ITERS - 1) as it:
            body(it, False, False)
        body(ITERS - 1, False, True)
        store(b, ITERS - 1)
        sp.wait_ge(filled, 16 * 3)
        for c in cs:
            sp.wait_ge(c.sem["base_stored"], 16 * (ITERS + 1))

    def vector_program(v):
        for c in cs:
            v.memset(c.am2[:, :], 0.0).then_inc(c.sem["base_stored"], 16)
            v.memset(c.yt[:, :, NT:NTP], 0.0)
            for i in range(NI):
                v.tensor_copy(c.v[:, i, :, DH:DV], k.value_mask[:, :].unsqueeze(2))

        def layer_norm(c, it, n):
            if n == 0:
                wait(v, c, it, "h_loaded", 16)
            elif n == 2:
                wait(v, c, it, "h_ffn", 3)
            else:
                wait(v, c, it, "h_attn", (n + 1) // 2)
            h = c.h_in if n == 0 else c.h
            for j in range(J):
                st = v.bn_stats(c.st[:, j, :], h[:, j, :])
            st.then_inc(c.sem["ln"], 1)
            wait(v, c, it, "ln", 4 * n + 1)
            v.nop(nofuse=True)
            for j in range(J):
                mv = v.bn_aggr(c.mv[:, j, :], c.st[:, j, :])
            mv.then_inc(c.sem["ln"], 1)
            wait(v, c, it, "ln", 4 * n + 2)
            v.tensor_scalar(c.var[:, :], c.mv[:, :, 1:2].rearrange("p j o -> p (j o)"), EPS, None, ALU.add)\
                .then_inc(c.sem["ln"], 1)

        def normalise(c, it, n):
            wait(v, c, it, "ln_power", n + 1)
            h = c.h_in if n == 0 else c.h
            for j in range(J):
                xj = v.tensor_scalar(c.xh[:, j, :], h[:, j, :], c.mv[:, j, 0:1], c.rstd[:, j:j + 1],
                                     ALU.subtract, ALU.mult)
            xj.then_inc(c.sem["ln"], 1)

        def rotate(c, it):
            for i in range(4):
                yield 0.367 + 0.04 * i
                wait(v, c, it, "rope_mm", i + 1)
                v.tensor_tensor(c.rn[:, i, :].rearrange(images, i=NI), c.ps[:, i, 0:NT].rearrange(images, i=NI),
                                img_bc(k.sin), ALU.mult).then_inc(c.sem["rope_sin"], 1)
            for i in range(4):
                yield 0.56 + 0.031 * i
                wait(v, c, it, "rope_cos", i + 1)
                wait(v, c, it, "rope_sin", i + 1)
                dst = c.qt[:, i, 0:NT] if i < 2 else c.rn[:, i, :]
                v.tensor_tensor(dst, c.rc[:, i, :], c.rn[:, i, :], ALU.add).then_inc(c.sem["rope_sum"], 1)

        def spread_keys(c, it, l):
            for f in range(2):
                yield 0.711 + 0.034 * f
                wait(v, c, it, *(("rope_sum", 3 + f) if l == 0 else ("q1", 3 + f)))
                for o in range(QH):
                    kd = v.tensor_scalar(c.kd[:, f, :, o, :], c.rn[:, 2 + f, :].rearrange(images, i=NI),
                                         k.head_mask[:, o:o + 1], None, ALU.mult)
                kd.then_inc(c.sem["keys"], 1)

        def values(c, it, l):
            for q in range(4):
                yield 0.8 + 0.05 * q
                wait(v, c, it, "vt_mm", 4 * l + q + 1)
                src = c.ps[0:GK, (q + 2) % 4, :].rearrange("p (i h n) -> p i h n", i=2, h=H)
                for i in range(2):
                    vv = v.tensor_tensor(c.v[:, 2 * q + i, :, 0:DH], src[:, i, :, :],
                                         k.value_mask[:, :].unsqueeze(2).broadcast_to([GK, H, DH]), ALU.mult)
                vv.then_inc(c.sem["values"], 1)

        def bias_and_max(c, it, q):
            l = q // NPAIR
            wait(v, c, it, "score_mm", q + 1)
            if q > 1:
                wait(v, c, it, "probt_mm", q - 1)
            sc, mx = c.sc2[:, q % 2, :], c.mx2[:, q % 2, :]
            by_bank = lambda table: table[0:PR, :].rearrange("p (f r n) -> p r f n", f=2, r=2)
            v.tensor_tensor(by_bank(sc), c.ps[0:PR, 0:2, 0:HT // 2].rearrange("p r (f n) -> p r f n", f=2),
                            by_bank(k.attn[l].bias), ALU.add)\
                .then_inc(c.sem["biased"], 1)
            wait(v, c, it, "biased", q + 1)
            v.tensor_reduce(mx[0:PR, :], sc[0:PR, :].rearrange("p (h t) -> p h t", h=H), AX.X, ALU.max)\
                .then_inc(c.sem["row_max"], 1)

        def divide(c, it, q):
            ysum = c.ps[0:PR, 3, Y0:Y0 + H * DV].rearrange("p (h n) -> p h n", h=H)
            wait(v, c, it, "pv_mm", q + 1)
            v.reciprocal(c.rs[0:PR, :], ysum[:, :, DH:DV].rearrange("p h o -> p (h o)")).then_inc(c.sem["inv_sum"], 1)
            wait(v, c, it, "inv_sum", q + 1)
            if q > 0:
                wait(v, c, it, "yt_mm", q)
            v.tensor_tensor(c.y[0:PR, :].rearrange("p (h n) -> p h n", h=H), ysum[:, :, 0:DH],
                            c.rs[0:PR, :].unsqueeze(2).broadcast_to([PR, H, DH]), ALU.mult).then_inc(c.sem["y"], 1)

        def add_attention(c, it, l):
            wait(v, c, it, "proj_mm", l + 1)
            wait(v, c, it, "h_bias", l + 1)
            v.tensor_tensor(c.h[:, :, :].rearrange("p j n -> p (j n)"),
                            c.ps[0:R, 2:4, :].rearrange("p b n -> p (b n)")[:, 0:J * D],
                            c.hb[:, :, :].rearrange("p j n -> p (j n)"), ALU.add).then_inc(c.sem["h_attn"], 1)

        def quantise_input(c, it):
            def step(n):
                wait(v, c, it, "quant", n)
            wait(v, c, it, "base_stored", 16)
            wait(v, c, it, "ln", 8)
            v.tensor_reduce(c.am[:, :], c.xh[:, :, :], AX.X, ALU.max, apply_absolute_value=True)\
                .then_inc(c.sem["quant"], 1)
            step(1)
            v.tensor_scalar(c.am[:, :], c.am[:, :], 1e-5, None, ALU.max).then_inc(c.sem["quant"], 1)
            step(2)
            v.reciprocal(c.am[:, :], c.am[:, :]).then_inc(c.sem["quant"], 1)
            step(3)
            v.tensor_scalar(c.am[:, :], c.am[:, :], 127.0, None, ALU.mult).then_inc(c.sem["quant"], 1)
            step(4)
            v.reciprocal(c.unit_in[:, :], c.am[:, :]).then_inc(c.sem["quant"], 1)
            for j in range(J):
                qj = v.tensor_scalar(c.qf[:, j, :], c.xh[:, j, :], c.am[:, j:j + 1], MAGIC, ALU.mult, ALU.add)
            qj.then_inc(c.sem["quant"], 1)
            step(6)
            v.tensor_scalar(c.qb[:, :, :], c.qf[:, :, :], MAGIC, None, ALU.subtract).then_inc(c.sem["quant"], 1)

        def hidden(c, it, m):
            wait(v, c, it, "hid_mm", m + 1)
            if m == 0:
                wait(v, c, it, "unit", 1)
                v.memset(c.a[:, :, NT:NTP], 0.0)
            v.tensor_tensor(c.t0[:, m, 0:NT], c.ps[:, (m + 2) % 4, 0:NT], c.unit[:, 0:NT], ALU.mult)\
                .then_inc(c.sem["hid"], 1)

        def convolve_left(c, it, m):
            am = c.a[:, m, 0:NT].rearrange(images, i=NI)
            tm = c.t0[:, m, 0:NT].rearrange(images, i=NI)
            wait(v, c, it, "mid", m + 1)
            v.scalar_tensor_tensor(am[:, :, 1:T], tm[:, :, 0:T - 1], k.conv[:, m, 0:1], am[:, :, 1:T],
                                   ALU.mult, ALU.add).then_inc(c.sem["left"], 1)

        def convolve_right(c, it, m):
            am = c.a[:, m, 0:NT].rearrange(images, i=NI)
            tm = c.t0[:, m, 0:NT].rearrange(images, i=NI)
            wait(v, c, it, "left", m + 1)
            v.scalar_tensor_tensor(am[:, :, 0:T - 1], tm[:, :, 1:T], k.conv[:, m, 2:3], am[:, :, 0:T - 1],
                                   ALU.mult, ALU.add).then_inc(c.sem["right"], 1)

        def hidden_scale(c, it):
            def step(n):
                wait(v, c, it, "quant2", n)
            wait(v, c, it, "silu", MH)
            v.tensor_reduce(c.t0[:, 0, :], c.a[:, :, :].rearrange("p m t -> p t m"), AX.X, ALU.max,
                            apply_absolute_value=True).then_inc(c.sem["quant2"], 1)
            yield 0.61
            wait(v, c, it, "colmax_mm", 1)
            v.tensor_reduce(c.am2[:, :], c.ps[0:R, 0, 0:J * P].rearrange("p (j n) -> p j n", j=J), AX.X, ALU.max)\
                .then_inc(c.sem["quant2"], 1)
            step(2)
            v.tensor_scalar(c.am2[:, :], c.am2[:, :], 1e-5, None, ALU.max).then_inc(c.sem["quant2"], 1)
            step(3)
            v.reciprocal(c.am2[:, :], c.am2[:, :]).then_inc(c.sem["quant2"], 1)
            step(4)
            v.tensor_scalar(c.am2[:, :], c.am2[:, :], 127.0, None, ALU.mult).then_inc(c.sem["quant2"], 1)
            step(5)
            v.reciprocal(c.unit2[:, :], c.am2[:, :]).then_inc(c.sem["quant2"], 1)
            step(6)
            v.tensor_scalar(c.unit2[:, :], c.unit2[:, :], k.wunit[0:R, 1:2], None, ALU.mult)\
                .then_inc(c.sem["quant2"], 1)

        def quantise_hidden(c, it, j):
            cols = slice(R * j, R * j + R)
            if j == 0:
                wait(v, c, it, "scale_mm", 1)
            v.tensor_tensor(c.a[:, :, cols], c.a[:, :, cols],
                            c.ps[:, 1, cols].unsqueeze(1).broadcast_to([P, MH, R]), ALU.mult)\
                .then_inc(c.sem["quant2"], 1)
            wait(v, c, it, "quant2", 8 + 2 * j)
            v.tensor_scalar(c.hq[:, :, cols], c.a[:, :, cols], MAGIC, MAGIC, ALU.add, ALU.subtract)\
                .then_inc(c.sem["quant2"], 1)

        def add_ffn(c, it, j):
            wait(v, c, it, "out_mm", j + 1)
            wait(v, c, it, "quant2", 7)
            v.scalar_tensor_tensor(c.h[:, j, :], c.ps[0:R, OUT_BANK[j], 0:D], c.unit2[:, j:j + 1], c.h[:, j, :],
                                   ALU.mult, ALU.add).then_inc(c.sem["h_ffn"], 1)

        def stage(name, c, it):
            if name == "ffn":
                yield 0.001
                layer_norm(c, it, 1)
                yield 0.05
                normalise(c, it, 1)
                yield 0.056
                quantise_input(c, it)
                for m in range(MH + 1):
                    yield 0.18 + 0.035 * m
                    if m > 0:
                        convolve_left(c, it, m - 1)
                    if m < MH:
                        hidden(c, it, m)
                    if m > 0:
                        convolve_right(c, it, m - 1)
                yield 0.55
                yield from hidden_scale(c, it)
                for j in range(J):
                    yield 0.71 + 0.06 * j
                    quantise_hidden(c, it, j)
                for j in range(J):
                    yield 0.87 + 0.05 * j
                    add_ffn(c, it, j)
                return
            l = int(name[-1])
            if name.startswith("project"):
                yield 0.0
                layer_norm(c, it, 2 * l)
                yield 0.084
                normalise(c, it, 2 * l)
                if l == 0:
                    yield from rotate(c, it)
                yield from spread_keys(c, it, l)
                yield from values(c, it, l)
                return
            for p in range(-2, NPAIR):
                if p + 2 < NPAIR:
                    yield (0.25, 0.55, p + 1.45)[min(p + 2, 2)] / PAIR_SPAN
                    bias_and_max(c, it, NPAIR * l + p + 2)
                if p >= 0:
                    yield (p + 1.55) / PAIR_SPAN
                    divide(c, it, NPAIR * l + p)
            yield (NPAIR + 1.4) / PAIR_SPAN
            add_attention(c, it, l)
            if l == 1:
                layer_norm(c, it, 3)
                yield (NPAIR + 2.316) / PAIR_SPAN
                normalise(c, it, 3)
                yield 0.975
                wait(v, c, it, "logit_mm", 1)
                v.tensor_tensor(k.logits[:, bass.ds(it * (CTX * J) + c.s * J, J), :],
                                c.ps[0:R, 2, 0:J * E].rearrange("p (j e) -> p j e", j=J),
                                k.br[0:R, :].unsqueeze(1).broadcast_to([R, J, E]), ALU.add).then_inc(c.sem["logit"], 1)

        run(v, stage)

    def gpsimd_program(g):
        def power(c, it, n):
            wait(g, c, it, "ln", 4 * n + 3)
            g.tensor_tensor(c.rstd[:, :], c.var[:, :], k.half[0:R, :], ALU.pow).then_inc(c.sem["ln_power"], 1)

        def add_bias(c, it, l):
            wait(g, c, it, "ln", 8 * l + 4)
            h = c.h_in if l == 0 else c.h
            g.tensor_tensor(c.hb[:, :, :], h[:, :, :], k.attn[l].ob[0:R, :].unsqueeze(1).broadcast_to([R, J, D]),
                            ALU.add).then_inc(c.sem["h_bias"], 1)

        def rope_cos(c, it):
            for i in range(4):
                yield 0.299 + 0.04 * i
                wait(g, c, it, "q0", i + 1)
                g.tensor_tensor(c.rc[:, i, :].rearrange(images, i=NI), c.qk[:, i, :].rearrange(images, i=NI),
                                img_bc(k.cos), ALU.mult).then_inc(c.sem["rope_cos"], 1)

        def shift(c, it, q):
            wait(g, c, it, "row_max", q + 1)
            s3 = c.sc2[0:PR, q % 2, :].rearrange("p (h t) -> p h t", h=H)
            g.tensor_tensor(s3, s3, c.mx2[0:PR, q % 2, :].unsqueeze(2).broadcast_to([PR, H, T]), ALU.subtract)\
                .then_inc(c.sem["shifted"], 1)

        def stage(name, c, it):
            if name == "ffn":
                yield 0.018
                power(c, it, 1)
                return
            l = int(name[-1])
            if name.startswith("project"):
                yield 0.05
                power(c, it, 2 * l)
                if l == 0:
                    yield from rope_cos(c, it)
                yield 0.5
                add_bias(c, it, l)
                return
            for p in range(NPAIR):
                yield (0.5, 0.8, p - 0.25)[min(p, 2)] / PAIR_SPAN
                shift(c, it, NPAIR * l + p)
            if l == 1:
                yield (NPAIR + 1.8) / PAIR_SPAN
                power(c, it, 3)
                yield 1.0
                wait(g, c, it, "ln", 16)
                g.tensor_copy(k.xn[:, bass.ds(it * (CTX * J) + c.s * J, J), 0:D], c.xh[:, :, :])\
                    .then_inc(c.sem["xn_kept"], 1)
                wait(g, c, it, "logit", 1)
                wait(g, c, it, "xn_kept", 1)
                g.tensor_tensor(c.base[:, :, :], c.h[:, :, :], c.xh[:, :, :], ALU.add).then_inc(c.sem["base"], 1)

        run(g, stage)

    def scalar_program(a):
        def evacuate_x(c, it, n):
            wait(a, c, it, "xt_mm", max(n, 1))
            a.activation(c.xt[:, :, :], c.ps[:, 0:2, 0:NTP], ACT.Copy).then_inc(c.sem["xt"], 1)

        def queries_keys(c, it, l):
            w = k.attn[l]
            for i in range(4):
                yield 0.227 + 0.038 * i
                wait(a, c, it, "qk_mm", 4 * l + i + 1)
                dst = c.qk[:, i, :] if l == 0 else c.qt[:, i, 0:NT] if i < 2 else c.rn[:, i, :]
                bias, scale = (w.qb, DH ** -0.5) if i < 2 else (w.kb, 1.0)
                a.activation(dst, c.ps[:, i, 0:NT], ACT.Identity, bias=bias[:, i % 2:i % 2 + 1], scale=scale)\
                    .then_inc(c.sem["q0" if l == 0 else "q1"], 1)

        def value_rows(c, it, l):
            for f in range(2):
                yield 0.62 + 0.05 * f
                wait(a, c, it, "v_mm", 2 * l + f + 1)
                a.activation(c.vr[:, f, :, :, :],
                             c.ps[:, f, 0:NT].rearrange(images, i=NI).unsqueeze(2).broadcast_to([P, NI, GH, T]),
                             ACT.Identity, bias=k.attn[l].vb[:, f:f + 1]).then_inc(c.sem["v_ev"], 1)

        def exponent(c, it, q):
            wait(a, c, it, "shifted", q + 1)
            a.activation(c.sc2[0:PR, q % 2, :], c.sc2[0:PR, q % 2, :], ACT.Exp).then_inc(c.sem["prob"], 1)

        def evacuate_prob(c, it, q):
            wait(a, c, it, "probt_mm", q + 1)
            for b, (g, n) in enumerate(((0, 4), (4, 2))):
                src = c.ps[0:GK, 2 + b, 0:n * PR].rearrange("p (g t) -> p g t", g=n)
                pt = a.activation(c.pt[:, g:g + n, 0:PR], src, ACT.Copy)
            pt.then_inc(c.sem["probt"], 1)

        def evacuate_y(c, it, q):
            wait(a, c, it, "yt_mm", q + 1)
            p = q % NPAIR
            src = c.ps[:, 2, 0:2 * P].rearrange("p (f i t) -> p f i t", f=2, i=2)
            dst = c.yt[:, :, 2 * T * p:2 * T * (p + 1)].rearrange("p f (i t) -> p f i t", i=2)
            a.activation(dst, src[:, :, :, 0:T], ACT.Copy).then_inc(c.sem["yt"], 1)

        def ffn(c, it):
            yield 0.13
            wait(a, c, it, "xq_mm", 1)
            src = bft(c.ps[:, 0, :])[:, 0:2 * J * (R + 1)].rearrange("p (f j t) -> p f j t", f=2, j=J)
            a.activation(c.xq[:, :, :].rearrange("p f (j t) -> p f j t", j=J), src[:, :, :, 0:R], ACT.Copy)\
                .then_inc(c.sem["xq"], 1)
            wait(a, c, it, "unit_mm", 1)
            a.activation(c.unit, c.ps[:, 1, 0:NTP], ACT.Copy, scale=k.wunit[:, 0:1]).then_inc(c.sem["unit"], 1)
            for m in range(MH):
                yield 0.2 + 0.035 * m
                wait(a, c, it, "hid", m + 1)
                a.activation(c.a[:, m, 0:NT], c.t0[:, m, 0:NT], ACT.Identity, bias=k.conv[:, m, 3:4],
                             scale=k.conv[:, m, 1:2]).then_inc(c.sem["mid"], 1)
            for m in range(MH):
                yield 0.49 + 0.0 * m
                wait(a, c, it, "right", m + 1)
                a.activation(c.a[:, m, 0:NT], c.a[:, m, 0:NT], ACT.Silu).then_inc(c.sem["silu"], 1)

        def stage(name, c, it):
            if name == "ffn":
                yield from ffn(c, it)
                return
            l = int(name[-1])
            if name.startswith("project"):
                yield 0.15
                evacuate_x(c, it, 2 * l)
                yield from queries_keys(c, it, l)
                yield from value_rows(c, it, l)
                return
            for p in range(-2, NPAIR):
                q = NPAIR * l + p
                if p >= 0:
                    yield (p + 1.15) / PAIR_SPAN
                    evacuate_prob(c, it, q)
                    yield (p + 1.7) / PAIR_SPAN
                    evacuate_y(c, it, q)
                if p + 2 < NPAIR:
                    yield (0.407, 1.308, p + 1.9)[min(p + 2, 2)] / PAIR_SPAN
                    exponent(c, it, q + 2)
            if l == 1:
                yield (NPAIR + 2.2) / PAIR_SPAN
                evacuate_x(c, it, 3)

        run(a, stage)

    def tensor_program(t):
        def transpose_x(c, it, n):
            wait(t, c, it, "ln", 4 * n + 4)
            for j in range(J):
                for f in range(2):
                    tr = t.transpose(c.ps[:, f, R * j:R * j + R], c.xh[:, j, P * f:P * f + P], k.ident[0:R, 0:R])
            tr.then_inc(c.sem["xt_mm"], 1)

        def project(c, which, l, f, bank):
            w = k.attn[l].w
            for i in range(2):
                mm = t.matmul(c.ps[:, bank, 0:NT], w[:, which, i, P * f:P * f + P], c.xt[:, i, 0:NT],
                              start=(i == 0), stop=(i == 1))
            return mm

        def queries_keys(c, it, l):
            for i in range(4):
                yield 0.2 + 0.043 * i
                if i == 0:
                    wait(t, c, it, "xt", l + 1)
                project(c, i // 2, l, i % 2, i).then_inc(c.sem["qk_mm"], 1)

        def rotate_pairs(c, it):
            for i in range(4):
                yield 0.341 + 0.04 * i
                wait(t, c, it, "q0", i + 1)
                t.matmul(c.ps[:, i, 0:NT], k.rot[:, :], c.qk[:, i, :], start=True, stop=True)\
                    .then_inc(c.sem["rope_mm"], 1)

        def value_products(c, it, l):
            for f in range(2):
                yield 0.543 + 0.061 * f
                wait(t, c, it, *(("rope_sin", f + 1) if l == 0 else ("q1", f + 1)))
                project(c, 2, l, f, f).then_inc(c.sem["v_mm"], 1)

        def value_transposes(c, it, l):
            for q in range(4):
                yield 0.76 + 0.05 * q
                if q < 2:
                    wait(t, c, it, *(("rope_sin", 3 + q) if l == 0 else ("q1", 3 + q)))
                if q == 0:
                    wait(t, c, it, "v_ev", 2 * l + 2)
                for i in range(2):
                    for f in range(2):
                        tr = t.transpose(c.ps[0:GK, (q + 2) % 4, D * i + P * f:D * i + P * f + P],
                                         c.vr[:, f, 2 * q + i, :, :].rearrange("p r t -> p (r t)"), k.ident[:, :])
                tr.then_inc(c.sem["vt_mm"], 1)

        def scores(c, it, q):
            l, p = divmod(q, NPAIR)
            if p == 0:
                wait(t, c, it, *(("rope_sum", 2) if l == 0 else ("q1", 2)))
                wait(t, c, it, "keys", 2 * l + 2)
                wait(t, c, it, "values", 4 * l + 4)
            else:
                wait(t, c, it, "biased", q)
            t.nop(nofuse=True)
            for f in range(2):
                for r in range(2):
                    for i in range(2):
                        rows = slice(64 * r, 64 * r + 64)
                        n = 2 * p + i
                        m = (64, T)[i]
                        mm = t.matmul(c.ps[64 * i:64 * i + m, r, QH * T * f:QH * T * (f + 1)],
                                      c.qt[rows, f, T * n:T * n + m],
                                      c.kd[rows, f, n, :, :].rearrange("p o t -> p (o t)"), start=True, stop=True,
                                      skip_group_check=True)
            mm.then_inc(c.sem["score_mm"], 1)

        def transpose_prob(c, it, q):
            wait(t, c, it, "prob", q + 1)
            if q % NPAIR:
                wait(t, c, it, "yt", q)
            for g in range(G):
                tr = t.transpose(c.ps[0:GK, 2 + g // 4, PR * (g % 4):PR * (g % 4 + 1)],
                                 c.sc2[0:PR, q % 2, group_col(g):group_col(g) + GK], k.ident[0:PR, 0:PR])
            tr.then_inc(c.sem["probt_mm"], 1)

        def weigh_values(c, it, q):
            wait(t, c, it, "probt", q + 1)
            t.nop(nofuse=True)
            for i in range(2):
                for g in range(G):
                    h = GH * g
                    n = min(GH, H - h)
                    m = (64, T)[i]
                    mm = t.matmul(c.ps[64 * i:64 * i + m, 3, Y0 + DV * h:Y0 + DV * (h + n)],
                                  c.pt[:, g, 64 * i:64 * i + m],
                                  c.v[:, 2 * (q % NPAIR) + i, h:h + n, :].rearrange("p h n -> p (h n)"),
                                  start=True, stop=True, skip_group_check=True)
            mm.then_inc(c.sem["pv_mm"], 1)

        def transpose_y(c, it, q):
            wait(t, c, it, "y", q + 1)
            for f in range(2):
                tr = t.transpose(c.ps[:, 2, P * f:P * f + PR], c.y[0:PR, P * f:P * f + P], k.ident[0:PR, 0:PR])
            tr.then_inc(c.sem["yt_mm"], 1)

        def output_projection(c, it, l):
            wait(t, c, it, "yt", NPAIR * (l + 1))
            dst = c.ps[0:R, 2:4, :].rearrange("p b n -> p (b n)")
            for j in range(J):
                for f in range(2):
                    mm = t.matmul(dst[:, D * j:D * j + D], c.yt[:, f, R * j:R * j + R], k.attn[l].w[:, 3, f, :],
                                  start=(f == 0), stop=(f == 1))
            mm.then_inc(c.sem["proj_mm"], 1)

        def ffn(c, it):
            yield 0.12
            wait(t, c, it, "quant", 7)
            dst = bft(c.ps[:, 0, :])
            for j in range(J):
                for f in range(2):
                    o = (R + 1) * (J * f + j)
                    tr = t.transpose(dst[:, o:o + R], c.qb[:, j, P * f:P * f + P], k.ident_bf[0:R, 0:R])
            tr.then_inc(c.sem["xq_mm"], 1)
            for j in range(J):
                mm = t.matmul(c.ps[:, 1, R * j:R * j + R], c.unit_in[:, j:j + 1].broadcast_to([R, P]),
                              k.ident[0:R, 0:R], start=True, stop=True)
            mm.then_inc(c.sem["unit_mm"], 1)
            for m in range(MH):
                yield 0.121 + 0.023 * m
                if m == 0:
                    wait(t, c, it, "xq", 1)
                    wait(t, c, it, "h_attn", 1)
                if m == 3:
                    wait(t, c, it, "unit", 1)
                if m >= 4:
                    wait(t, c, it, "hid", m - 3)
                for f in range(2):
                    mm = t.matmul(c.ps[:, (m + 2) % 4, 0:NT], k.w1[:, f, P * m:P * m + P], c.xq[:, f, 0:NT],
                                  start=(f == 0), stop=(f == 1))
                mm.then_inc(c.sem["hid_mm"], 1)
            yield 0.58
            wait(t, c, it, "quant2", 1)
            for j in range(J):
                tr = t.transpose(c.ps[0:R, 0, P * j:P * j + P], c.t0[:, 0, R * j:R * j + R], k.ident[:, :])
            tr.then_inc(c.sem["colmax_mm"], 1)
            yield 0.648
            wait(t, c, it, "quant2", 5)
            for j in range(J):
                mm = t.matmul(c.ps[:, 1, R * j:R * j + R], c.am2[:, j:j + 1].broadcast_to([R, P]),
                              k.ident[0:R, 0:R], start=True, stop=True)
            mm.then_inc(c.sem["scale_mm"], 1)
            for j in range(J):
                yield 0.78 + 0.067 * j
                wait(t, c, it, "quant2", 9 + 2 * j)
                for m in range(MH):
                    mm = t.matmul(c.ps[0:R, OUT_BANK[j], 0:D], c.hq[:, m, R * j:R * j + R], k.w2[:, m, :],
                                  start=(m == 0), stop=(m == MH - 1))
                mm.then_inc(c.sem["out_mm"], 1)

        def stage(name, c, it):
            if name == "ffn":
                yield from ffn(c, it)
                return
            l = int(name[-1])
            if name.startswith("project"):
                yield 0.12
                transpose_x(c, it, 2 * l)
                yield from queries_keys(c, it, l)
                if l == 0:
                    yield from rotate_pairs(c, it)
                yield from value_products(c, it, l)
                yield from value_transposes(c, it, l)
                return
            for p in range(-2, NPAIR):
                q = NPAIR * l + p
                if p >= 0:
                    yield (p + 0.915) / PAIR_SPAN
                    transpose_prob(c, it, q)
                if p + 2 < NPAIR:
                    yield (0.0, 0.375, p + 1.2)[min(p + 2, 2)] / PAIR_SPAN
                    scores(c, it, q + 2)
                if p >= 0:
                    yield (p + 1.3) / PAIR_SPAN
                    weigh_values(c, it, q)
                    yield (p + 1.6) / PAIR_SPAN
                    transpose_y(c, it, q)
            yield (NPAIR + 1.082) / PAIR_SPAN
            output_projection(c, it, l)
            if l == 1:
                yield (NPAIR + 2.166) / PAIR_SPAN
                transpose_x(c, it, 3)
                yield (NPAIR + 2.3) / PAIR_SPAN
                wait(t, c, it, "xt", 3)
                for j in range(J):
                    for f in range(2):
                        mm = t.matmul(c.ps[0:R, 2, E * j:E * j + E], c.xt[:, f, R * j:R * j + R], k.wr[:, f, :],
                                      start=(f == 0), stop=(f == 1))
                mm.then_inc(c.sem["logit_mm"], 1)

        run(t, stage)

    with nc.Block() as block:
        block.sync(sync_program)
        block.vector(vector_program)
        block.gpsimd(gpsimd_program)
        block.scalar(scalar_program)
        block.tensor(tensor_program)



def experts(nc, ctx, sem, d, k, base_d, xs_d, weighted_d, b1_d, b2_d, out):
    def sb(name, shape, dt=F32):
        return ctx.enter_context(nc.sbuf_tensor(name, shape, dt))

    ew1 = sb("ew1", [P, E, 2, EH])
    ew2 = sb("ew2", [P, E, EH // P, D])
    eb1, eb2 = sb("eb1_rows", [3, E, EH], BF16), sb("eb2_rows", [3, E, D], BF16)
    ones_bf = sb("ones_bf", [P, P], BF16)
    tile_expert = sb("tile_expert", [1, TILES], I32)
    ew1_loaded, eb_loaded = sem("ew1_loaded"), sem("eb_loaded")
    ew2_loaded = [sem("ew2_loaded_even"), sem("ew2_loaded_odd")]
    ps = k.ps

    with ExitStack() as dctx:
        def sbd(name, shape, dt=F32):
            return dctx.enter_context(nc.sbuf_tensor(name, shape, dt))
        w1, w2 = sbd("weight1", [R, COLS]), sbd("weight2", [R, COLS])
        dest = [sbd("dest1", [R, COLS], U32), sbd("dest2", [R, COLS], U32)]
        row_ids = sbd("row_ids", [R, 2, COLS])
        scattered, tagged = [sem("scattered_first_half"), sem("scattered_second_half")], sem("rows_tagged")
        big = [R, COLS, E]
        pr, pr2, ta, tb = (sbd(n, big) for n in ("probs", "probs_rest", "tmp_a", "tmp_b"))
        oh = [sbd("choice1", big), sbd("choice2", big)]
        both = sbd("both", big, BF16)
        red, m1, m2, top = (sbd(n, [R, COLS]) for n in ("red", "m1", "m2", "top"))
        nt, na, nb_ = sbd("n_tiles", [R, E]), sbd("tiles_a", [R, E]), sbd("tiles_b", [R, E])
        tile_cmp, tile_sum = sbd("tile_cmp", [1, TILES, E]), sbd("tile_sum", [1, TILES])
        rank, upto, valid, spare, tile_no = (sbd("rank", [R, E]), sbd("upto", [R, R]), sbd("valid", [R, COLS]),
                                             sbd("spare", [R, 2, COLS]), sbd("tile_no", [1, TILES]))
        upto_bf = sbd("upto_bf", [R, R], BF16)
        t_loaded, step, expo, counted, dests = sem("t_loaded"), sem("step"), sem("expo"), sem("counted"), sem("dests")
        experts_known = sem("experts_known")
        tables = [(rank[:, :], d.rank), (upto[:, :], d.upto), (valid[:, :], d.valid), (spare[:, :, :], d.spare),
                  (tile_no[:, :], d.tile_no), (row_ids[:, :, :], d.row_ids)]

        with nc.Block() as block:
            @block.sync
            def _(sp):
                for dst, src in tables:
                    sp.dma_start(dst, src).then_inc(t_loaded, 16)
                for n, (dst, src) in enumerate(((eb1, b1_d), (eb2, b2_d))):
                    sp.dma_start(dst[:, :, :].rearrange("i e n -> i (e n)"), src).then_inc(eb_loaded, 16)
                for e in range(E):
                    sp.dma_start(ew1[:, e, :, :], d.W1[e].rearrange("(k p) n -> p k n", p=P)).then_inc(ew1_loaded, 16)
                for e in range(E):
                    if e >= 2:
                        sp.wait_ge(ew2_loaded[e % 2], 16 * (e // 2))
                    sp.dma_start(ew2[:, e, :, :], d.W2[e].rearrange("(k p) n -> p k n", p=P))\
                        .then_inc(ew2_loaded[e % 2], 16)

            @block.scalar
            def _(a):
                a.wait_ge(step, 2)
                a.activation(pr[:, :, :], pr[:, :, :], ACT.Exp).then_inc(expo, 1)

            @block.tensor
            def _(t):
                t.wait_ge(t_loaded, 16 * len(tables))
                t.wait_ge(counted, 1)
                flat = both[:, :, :].rearrange("p c e -> p (c e)")
                t.matmul(ps[0:R, 0, 0:COLS * E], upto_bf[:, :], flat, start=True, stop=True).then_inc(counted, 1)
                t.matmul(ps[0:R, 1, 0:COLS * E], ones_bf[0:R, 0:R], flat, start=True, stop=True).then_inc(counted, 1)

            @block.vector
            def _(v):
                count = [0]

                def beside(instruction):
                    instruction.then_inc(step, 1)
                    count[0] += 1

                def did(instruction):
                    beside(instruction)
                    v.wait_ge(step, count[0])

                def over_e(table):
                    return table[:, :].unsqueeze(2).broadcast_to(big)

                def over_c(table):
                    return table[:, :].unsqueeze(1).broadcast_to(big)

                did(v.tensor_reduce(m1[:, :], k.logits[:, :, :], AX.X, ALU.max))
                did(v.tensor_tensor(pr[:, :, :], k.logits[:, :, :], over_e(m1), ALU.subtract))
                v.wait_ge(t_loaded, 16 * len(tables))
                beside(v.memset(ones_bf[:, :], 1.0))
                beside(v.tensor_copy(upto_bf[:, :], upto[:, :]))
                v.wait_ge(expo, 1)
                did(v.tensor_reduce(red[:, :], pr[:, :, :], AX.X, ALU.add))
                did(v.reciprocal(red[:, :], red[:, :]))
                did(v.tensor_tensor(pr[:, :, :], pr[:, :, :], over_e(red), ALU.mult))
                for n, (src, m) in enumerate(((pr, m1), (pr2, m2))):
                    did(v.tensor_reduce(m[:, :], src[:, :, :], AX.X, ALU.max))
                    did(v.tensor_tensor(ta[:, :, :], src[:, :, :], over_e(m), ALU.is_ge))
                    did(v.tensor_tensor(ta[:, :, :], ta[:, :, :], over_c(rank), ALU.mult))
                    did(v.tensor_reduce(top[:, :], ta[:, :, :], AX.X, ALU.max))
                    did(v.tensor_tensor(oh[n][:, :, :], ta[:, :, :], over_e(top), ALU.is_ge))
                    if n == 0:
                        did(v.scalar_tensor_tensor(pr2[:, :, :].rearrange("p c e -> p (c e)"),
                                                   oh[0][:, :, :].rearrange("p c e -> p (c e)"), -2.0,
                                                   pr[:, :, :].rearrange("p c e -> p (c e)"), ALU.mult, ALU.add))
                beside(v.tensor_tensor(oh[0][:, :, :], oh[0][:, :, :], over_e(valid), ALU.mult))
                did(v.tensor_tensor(oh[1][:, :, :], oh[1][:, :, :], over_e(valid), ALU.mult))
                v.tensor_add(both[:, :, :], oh[0][:, :, :], oh[1][:, :, :]).then_inc(counted, 1)
                did(v.tensor_add(red[:, :], m1[:, :], m2[:, :]))
                did(v.tensor_scalar(red[:, :], red[:, :], 1e-9, None, ALU.max))
                did(v.reciprocal(red[:, :], red[:, :]))
                beside(v.tensor_mul(w1[:, :], m1[:, :], red[:, :]))
                did(v.tensor_mul(w2[:, :], m2[:, :], red[:, :]))
                v.wait_ge(counted, 3)
                did(v.tensor_copy(ta[:, :, :].rearrange("p c e -> p (c e)"), ps[0:R, 1, 0:COLS * E]))
                src, dst = ta, tb
                s = 1
                while s < COLS:
                    beside(v.tensor_copy(dst[:, 0:s, :], src[:, 0:s, :]))
                    did(v.tensor_add(dst[:, s:, :], src[:, s:, :], src[:, 0:COLS - s, :]))
                    src, dst = dst, src
                    s *= 2
                did(v.tensor_scalar(nt[:, :], src[:, COLS - 1, :], 1.0 / P, (P - 1) / P - 0.5 + 0.5 / P,
                                    ALU.mult, ALU.add))
                did(v.tensor_scalar(nt[:, :], nt[:, :], MAGIC, None, ALU.add))
                did(v.tensor_scalar(nt[:, :], nt[:, :], MAGIC, None, ALU.subtract))
                did(v.tensor_copy(na[:, :], nt[:, :]))
                a_, b_ = na, nb_
                s = 1
                while s < E:
                    beside(v.tensor_copy(b_[:, 0:s], a_[:, 0:s]))
                    did(v.tensor_add(b_[:, s:], a_[:, s:], a_[:, 0:E - s]))
                    a_, b_ = b_, a_
                    s *= 2
                did(v.tensor_tensor(b_[:, :], a_[:, :], nt[:, :], ALU.subtract))
                beside(v.tensor_scalar(b_[:, :], b_[:, :], float(P), None, ALU.mult))
                did(v.tensor_tensor(dst[:, :, :].rearrange("p c e -> p (c e)"),
                                    src[:, :, :].rearrange("p c e -> p (c e)"), ps[0:R, 1, 0:COLS * E], ALU.subtract))
                did(v.tensor_tensor(src[:, :, :].rearrange("p c e -> p (c e)"),
                                    dst[:, :, :].rearrange("p c e -> p (c e)"), ps[0:R, 0, 0:COLS * E], ALU.add))
                did(v.tensor_tensor(src[:, :, :], src[:, :, :], over_c(b_), ALU.add))
                for n in range(2):
                    did(v.tensor_tensor(dst[:, :, :], src[:, :, :], oh[n][:, :, :], ALU.mult))
                    did(v.tensor_reduce(red[:, :], dst[:, :, :], AX.X, ALU.add))
                    v.tensor_tensor(dest[n][:, :], red[:, :], spare[:, n, :], ALU.add).then_inc(dests, 1)
                    v.wait_ge(dests, n + 1)
                did(v.tensor_tensor(tile_cmp[:, :, :], tile_no[:, :].unsqueeze(2).broadcast_to([1, TILES, E]),
                                    a_[0:1, :].unsqueeze(1).broadcast_to([1, TILES, E]), ALU.is_ge))
                did(v.tensor_reduce(tile_sum[:, :], tile_cmp[:, :, :], AX.X, ALU.add))
                v.tensor_scalar(tile_expert[:, :], tile_sum[:, :], float(E - 1), None, ALU.min)\
                    .then_inc(experts_known, 1)

            @block.gpsimd
            def _(g):
                g.wait_ge(t_loaded, 16 * len(tables))
                for n, w in enumerate((w1, w2)):
                    g.wait_ge(dests, n + 1)
                    for half in range(2):
                        part = slice(half * COLS // 2, (half + 1) * COLS // 2)
                        if n == 1:
                            g.wait_ge(scattered[half], 16 * COLS // 2)
                        g.tensor_copy(k.xn[:, part, D:D + 1], row_ids[:, n, part].unsqueeze(2)).then_inc(tagged, 1)
                        g.tensor_copy(k.xn[:, part, D + 1:XW], w[:, part].unsqueeze(2)).then_inc(tagged, 1)
                        g.wait_ge(tagged, 4 * n + 2 * half + 2)
                        for i in range(part.start, part.stop):
                            g.indirect_dma_start(xs_d, bass.IndirectOffsetOnAxis(ap=dest[n][:, i:i + 1], axis=0),
                                                 k.xn[:, i, :], None).then_inc(scattered[half], 16)
                for half in range(2):
                    g.wait_ge(scattered[half], 16 * COLS)

    cs = []
    for s in range(2):
        c = Bag()
        c.s = s
        c.x, c.xt = sb(f"mx{s}", [P, XW]), sb(f"mxt{s}", [P, 2, P])
        c.h, c.ht, c.o = sb(f"mh{s}", [P, EH]), sb(f"mht{s}", [P, EH]), sb(f"mo{s}", [P, D])
        c.tag = sb(f"tag{s}", [P, 2])
        c.to, c.weight = sb(f"result_row{s}", [P, 1], U32), sb(f"pair_weight{s}", [P, 1])
        c.x_in, c.x_turned, c.xt_ready = sem(f"x_in{s}"), sem(f"x_turned{s}"), sem(f"xt_ready{s}")
        c.h_mm, c.gelu, c.h_turned, c.ht_ready = sem(f"h_mm{s}"), sem(f"gelu{s}"), sem(f"h_turned{s}"), sem(f"ht_ready{s}")
        c.o_mm, c.o_ready, c.o_out = sem(f"o_mm{s}"), sem(f"o_ready{s}"), sem(f"o_out{s}")
        c.tag_kept, c.tags = sem(f"tag_kept{s}"), sem(f"tags{s}")
        c.ps = ps[:, 4 * s:4 * s + 4, :]
        cs.append(c)
    base_in = sem("base_in")
    N = TILES // 2
    warm = sb("warm", [P, N])
    with nc.Block() as block:
        @block.sync
        def _(sp):
            def load(c, it):
                sp.dma_start(c.x[:, :], xs_d[bass.ds(it * (2 * P) + c.s * P, P), :]).then_inc(c.x_in, 16)

            for c in cs:
                load(c, 0)
            sp.dma_start(k.xn[:, :, 0:D], base_d.rearrange("c r n -> r c n")).then_inc(base_in, 16)
            with sp.Fori(1, N) as it:
                for c in cs:
                    sp.wait_ge(c.x_turned, it)
                    sp.nop(nofuse=True)
                    sp.wait_ge(c.tag_kept, it)
                    sp.nop(nofuse=True)
                    load(c, it)
            sp.wait_ge(base_in, 16)

        @block.gpsimd
        def _(g):
            def body(it, first):
                for c in cs:
                    g.wait_ge(c.tag_kept, it + 1)
                    if not first:
                        g.wait_ge(c.o_out, it * 16)
                    g.nop(nofuse=True)
                    g.tensor_copy(c.to[:, :], c.tag[:, 0:1]).then_inc(c.tags, 1)
                    g.tensor_copy(c.weight[:, :], c.tag[:, 1:2]).then_inc(c.tags, 1)
                for c in cs:
                    g.wait_ge(c.tags, it * 2 + 2)
                    g.wait_ge(c.o_ready, it + 1)
                    g.nop(nofuse=True)
                    g.indirect_dma_start(weighted_d, bass.IndirectOffsetOnAxis(ap=c.to[:, 0:1], axis=0),
                                         c.o[:, :], None).then_inc(c.o_out, 16)

            body(0, True)
            with g.Fori(1, N) as it:
                body(it, False)
            for c in cs:
                g.wait_ge(c.o_out, 16 * N)

        @block.tensor
        def _(t):
            t.wait_ge(ew1_loaded, 16 * E)
            for even_odd in ew2_loaded:
                t.wait_ge(even_odd, 16 * E // 2)
            t.wait_ge(eb_loaded, 32)

            def turn_x(c, it):
                t.wait_ge(c.x_in, it * 16 + 16)
                for f in range(2):
                    tr = t.transpose(c.ps[:, 0, P * f:P * f + P], c.x[:, P * f:P * f + P], k.ident[:, :])
                tr.then_inc(c.x_turned, 1)

            def body(it, first, last):
                experts_of = []
                for c in cs:
                    e = t.value_load(tile_expert[0:1, bass.ds(it * 2 + c.s, 1)], min_val=0, max_val=E - 1)
                    experts_of.append(e)
                    t.matmul(c.ps[:, 1, :], ones_bf[0:3, :], eb1[:, bass.ds(e, 1), :].rearrange("i o n -> i (o n)"),
                             start=True, stop=False)
                    t.wait_ge(c.xt_ready, it + 1)
                    for f in range(2):
                        mm = t.matmul(c.ps[:, 1, :], c.xt[:, f, :],
                                      ew1[:, bass.ds(e, 1), f, :].rearrange("p o n -> p (o n)"),
                                      start=False, stop=(f == 1))
                    mm.then_inc(c.h_mm, 1)
                for c in cs:
                    if not last:
                        turn_x(c, it + 1)
                    t.wait_ge(c.gelu, it + 1)
                    for f in range(4):
                        tr = t.transpose(c.ps[:, 2, P * f:P * f + P], c.h[:, P * f:P * f + P], k.ident[:, :])
                    tr.then_inc(c.h_turned, 1)
                for c, e in zip(cs, experts_of):
                    if not first:
                        t.wait_ge(c.o_ready, it)
                    t.matmul(c.ps[:, 3, 0:D], ones_bf[0:3, :], eb2[:, bass.ds(e, 1), :].rearrange("i o n -> i (o n)"),
                             start=True, stop=False)
                    t.wait_ge(c.ht_ready, it + 1)
                    for f in range(4):
                        mm = t.matmul(c.ps[:, 3, 0:D], c.ht[:, P * f:P * f + P],
                                      ew2[:, bass.ds(e, 1), f, :].rearrange("p o n -> p (o n)"),
                                      start=False, stop=(f == 3))
                    mm.then_inc(c.o_mm, 1)

            for c in cs:
                turn_x(c, 0)
            body(0, True, False)
            with t.Fori(1, N - 1) as it:
                body(it, False, False)
            body(N - 1, False, True)

        @block.scalar
        def _(a):
            with a.Fori(0, N) as it:
                a.activation(warm[:, bass.ds(it, 1)], k.ones[:, 0:1], ACT.Gelu)
                for c in cs:
                    a.wait_ge(c.h_mm, it + 1)
                    a.activation(c.h[:, :], c.ps[:, 1, :], ACT.Gelu).then_inc(c.gelu, 1)

        @block.vector
        def _(v):
            def turned_x(c, it, first):
                v.wait_ge(c.x_turned, it + 1)
                if not first:
                    v.wait_ge(c.h_mm, it)
                v.tensor_copy(c.xt[:, :, :].rearrange("p f n -> p (f n)"), c.ps[:, 0, 0:2 * P]).then_inc(c.xt_ready, 1)
                if not first:
                    v.wait_ge(c.tags, it * 2)
                v.tensor_copy(c.tag[:, :], c.x[:, D:XW]).then_inc(c.tag_kept, 1)

            def body(it, first, last):
                for c in cs:
                    v.wait_ge(c.h_turned, it + 1)
                    v.tensor_copy(c.ht[:, :], c.ps[:, 2, :]).then_inc(c.ht_ready, 1)
                    if not last:
                        turned_x(c, it + 1, False)
                for c in cs:
                    v.wait_ge(c.tags, it * 2 + 2)
                    if not first:
                        v.wait_ge(c.o_out, it * 16)
                    v.wait_ge(c.o_mm, it + 1)
                    v.tensor_scalar(c.o[:, :], c.ps[:, 3, 0:D], c.weight[:, :], None, ALU.mult).then_inc(c.o_ready, 1)

            for c in cs:
                turned_x(c, 0, True)
            body(0, True, False)
            with v.Fori(1, N - 1) as it:
                body(it, False, False)
            body(N - 1, False, True)

    taken = ew1[0:R, :, :, :].rearrange("p e f n -> p (e f n)")
    got = [[taken[:, (2 * b + n) * J * D:(2 * b + n + 1) * J * D] for n in range(2)] for b in range(NB)]
    got_in = [sem(f"got_in{b}") for b in range(NB)]
    added, stored = sem("added"), sem("out_stored")
    out_rows = out.rearrange("b t n -> (b t) n")
    last_rows = NT - (J - 1) * R
    with nc.Block() as block:
        def load(eng, b, n):
            rows = (n * COLS + J * b) * R
            eng.dma_start(got[b][n].rearrange("p (j n) -> p j n", j=J),
                          weighted_d[rows:rows + J * R, :].rearrange("(j p) n -> p j n", p=R)).then_inc(got_in[b], 16)

        @block.sync
        def _(sp):
            for b in range(NB):
                load(sp, b, 0)
            sp.wait_ge(stored, 16 * 2 * NB)

        @block.vector
        def _(v):
            for b in range(NB):
                sums = k.xn[:, J * b:J * b + J, 0:D]
                v.wait_ge(got_in[b], 32)
                for n in range(2):
                    v.tensor_tensor(sums, got[b][n].rearrange("p (j n) -> p j n", j=J), sums, ALU.add)\
                        .then_inc(added, 1)
                    if n == 0:
                        v.wait_ge(added, 2 * b + 1)

        @block.scalar
        def _(a):
            for b in range(NB):
                load(a, b, 1)
            for b in range(NB):
                a.wait_ge(added, 2 * b + 2)
                start = NT * b
                a.dma_start(out_rows[start:start + (J - 1) * R, :].rearrange("(j p) n -> p j n", p=R),
                            k.xn[:, J * b:J * b + J - 1, 0:D]).then_inc(stored, 16)
                start += (J - 1) * R
                a.dma_start(out_rows[start:start + last_rows, :], k.xn[0:last_rows, J * b + J - 1, 0:D])\
                    .then_inc(stored, 16)



def shape_constants():
    f = np.float32
    t = {}
    t["ident"] = np.eye(P, dtype=f)
    y, x = np.meshgrid(np.arange(HP), np.arange(HP), indexing="ij")
    omega = (f(1.0) / f(10000.0) ** (np.arange(D // 4, dtype=f) / f(D // 4 - 1))).astype(f)
    ya = (y.reshape(-1)[:, None].astype(f) * omega[None]).astype(f)
    xa = (x.reshape(-1)[:, None].astype(f) * omega[None]).astype(f)
    pe = np.concatenate((np.sin(xa), np.cos(xa), np.sin(ya), np.cos(ya)), axis=1).astype(f)
    t["pos"] = np.ascontiguousarray(pe[np.arange(NPB) % NP].reshape(J, RP, D).transpose(1, 0, 2))
    theta = (f(1.0) / f(10000.0) ** (f(2.0) * np.arange(DH // 2, dtype=f) / f(DH))).astype(f)
    ang = (np.arange(T, dtype=f)[None, :] * theta[(np.arange(P) % DH) // 2][:, None]).astype(f)
    t["cos"], t["sin"] = np.cos(ang).astype(f), np.sin(ang).astype(f)
    rot = np.zeros((P, P), f)
    for i in range(0, P, 2):
        rot[i + 1, i], rot[i, i + 1] = -1.0, 1.0
    t["rot"] = rot
    hm = np.zeros((P, QH), f)
    hm[np.arange(P), (np.arange(P) // DH) % QH] = 1.0
    t["head_mask"] = hm
    vm = np.zeros((GK, H), f)
    for h in range(H):
        r = h % GH if h < GH * (G - 1) else GH - 1
        vm[T * r:T * (r + 1), h] = 1.0
    t["value_mask"] = vm
    causal = np.zeros((P, H, T), f)
    for o in (0, 64):
        q, s = np.arange(T)[:, None], np.arange(T)[None]
        causal[o:o + T] = np.where(s <= q, 0.0, -1e10).astype(f)[:, None, :]
    t["causal"] = causal.reshape(P, HT)
    t["rank"] = np.ascontiguousarray(np.broadcast_to((E - np.arange(E)).astype(f)[None], (R, E)))
    t["upto"] = np.triu(np.ones((R, R), f), 1)
    valid = np.ones((R, COLS), f)
    valid[NT - (J - 1) * R:, J - 1::J] = 0.0
    t["valid"] = valid
    spare = np.zeros((R, 2, COLS), f)
    for n in range(2):
        spare[:, n, :] = (1.0 - valid) * (SLOTS + n * COLS + np.arange(COLS))
    t["spare"] = spare
    t["row_ids"] = ((np.arange(2)[None, :, None] * COLS + np.arange(COLS)[None, None]) * R
                    + np.arange(R)[:, None, None]).astype(f)
    t["filler"] = np.zeros((P, 2, XW), f)
    t["filler"][:, :, D] = 2 * COLS * R + np.arange(2)[None] * P + np.arange(P)[:, None]
    t["tile_no"] = np.arange(TILES, dtype=f)[None]
    return t


def kernel(**inputs):
    import concourse.bacc as bacc
    from concourse.bass_utils import run_bass_kernel_spmd

    a = {n: np.asarray(v) for n, v in inputs.items()}
    nc = bacc.Bacc("TRN2", target_bir_lowering=False, num_devices=1)
    arrays = {}

    def give(name, array):
        array = np.ascontiguousarray(array)
        name = "in_" + name
        arrays[name] = array
        return nc.dram_tensor(name, array.shape, mybir.dt.from_np(array.dtype), kind="ExternalInput").ap()

    def columns(v, n):
        return v.reshape(n, P).T

    d, t = Bag(), shape_constants()
    d.ident, d.pos, d.cos, d.sin, d.rot = (give(n, t[n]) for n in ("ident", "pos", "cos", "sin", "rot"))
    d.head_mask, d.value_mask, d.causal = (give(n, t[n]) for n in ("head_mask", "value_mask", "causal"))
    d.rank, d.upto, d.valid, d.spare, d.tile_no = (give(n, t[n]) for n in ("rank", "upto", "valid", "spare", "tile_no"))
    d.row_ids, d.filler = give("row_ids", t["row_ids"]), give("filler", t["filler"])
    x = a["x"].reshape(B, C, HP, PATCH, HP, PATCH)
    d.x = give("x", x.transpose(3, 5, 1, 0, 2, 4).reshape(FP, B * NP))
    d.cls, d.cls_pos = give("cls", a["L0_tok_cls_token"].reshape(D)), give("cls_pos", a["L0_tok_cls_pos_embedding"].reshape(D))
    d.ln1_g, d.ln1_b = give("ln1_g", columns(a["L0_tok_ln1_g"], KF)), give("ln1_b", columns(a["L0_tok_ln1_b"], KF))
    d.W, d.tok_bias = give("W", a["L0_tok_W"]), give("tok_bias", a["L0_tok_bias"])
    d.ln2_g, d.ln2_b = give("ln2_g", a["L0_tok_ln2_g"]), give("ln2_b", a["L0_tok_ln2_b"])
    d.attn_w = [[give(f"L0_{n}", a[f"L0_attn_{n}"].T) for n in ("wq", "wk", "wv", "wp")],
                [give(f"L1_{n}", a[f"L1_attn_{n}"]) for n in ("Wq", "Wk", "Wv", "Wo")]]
    d.attn_b = [[give(f"L{l}_b{n}", columns(a[f"L{l}_attn_b{n}"], 2)) for n in "qkv"] for l in range(2)]
    d.attn_ob = [give("L0_bp", a["L0_attn_bp"]), give("L1_bo", a["L1_attn_bo"])]
    d.w1T, d.w2T = give("w1T", a["L0_ffn_w1"].T), give("w2T", a["L0_ffn_w2"].T)
    conv = np.concatenate((a["L0_ffn_conv_w"].reshape(FH, 3), a["L0_ffn_conv_b"].reshape(FH, 1)), axis=1)
    d.conv = give("conv", conv.reshape(MH, P, 4).transpose(1, 0, 2))
    d.relT = give("relT", a["L1_attn_rel_bias"].T)
    d.Wr, d.br = give("Wr", a["L1_ffn_Wr"]), give("br", a["L1_ffn_br"])
    d.W1, d.b1, d.W2, d.b2 = (give(n, a[f"L1_ffn_{n}"]) for n in ("W1", "b1", "W2", "b2"))
    out = nc.dram_tensor("out", (B, T, D), F32, kind="ExternalOutput").ap()
    build(nc, d, out)
    r = run_bass_kernel_spmd(nc, [arrays], core_ids=[0])
    return r.results[0]["out"]
```
